# Optimizing a Trainium2 kernel written in Bass

```python
import numpy as np
import jax
import jax.numpy as jnp

def _softmax(x, axis=-1):
    return jax.nn.softmax(x, axis=axis)

def _gelu(x):
    return jax.nn.gelu(x, approximate=True)

def _silu(x):
    return jax.nn.silu(x)

def _sigmoid(x):
    return jax.nn.sigmoid(x)

def _layernorm(x, axis=-1, eps=1e-05):
    m = jnp.mean(x, axis=axis, keepdims=True)
    v = jnp.var(x, axis=axis, keepdims=True)
    return (x - m) / jnp.sqrt(v + eps)

def _scatter_add(tgt, idx, src, axis=0):
    return tgt.at[idx].add(src)

def _segment_sum(src, seg, n):
    return jax.ops.segment_sum(src, seg, n)
kernel_name = 'mk_vit_tower_d2_tok_img1024_r4_2260fc'

def setup_inputs(seed: int=0):
    np.random.seed(seed)
    _w = jnp.asarray

    def _rec_inputs():
        import jax
        import jax.numpy as jnp
        _rk = jax.random.key(seed)
        x = -0.00016672 + 0.999947 * jax.random.normal(jax.random.fold_in(_rk, 1), (64, 3, 96, 96), jnp.float32)
        return x
    x = _rec_inputs()

    def _L0_tok_setup():
        import jax, jax.numpy as jnp
        import numpy as np
        PATCH = 16
        EPS = 1e-05

        def _patchify(img, p):
            B, C, H, W = img.shape
            h, w = (H // p, W // p)
            x = img.reshape(B, C, h, p, w, p)
            x = x.transpose(0, 2, 4, 1, 3, 5)
            return x.reshape(B, h, w, C * p * p)

        def _layernorm(x, gamma):
            mu = x.mean(axis=-1, keepdims=True)
            var = ((x - mu) ** 2).mean(axis=-1, keepdims=True)
            return (x - mu) * jax.lax.rsqrt(var + EPS) * gamma

        def _posemb_sincos_2d(h, w, dim, temperature=10000.0, dtype=jnp.float32):
            y, x = jnp.meshgrid(jnp.arange(h, dtype=dtype), jnp.arange(w, dtype=dtype), indexing='ij')
            omega = jnp.arange(dim // 4, dtype=dtype) / (dim // 4 - 1)
            omega = 1.0 / temperature ** omega
            y = y.reshape(-1)[:, None] * omega[None, :]
            x = x.reshape(-1)[:, None] * omega[None, :]
            return jnp.concatenate([jnp.sin(x), jnp.cos(x), jnp.sin(y), jnp.cos(y)], axis=1)
        key = jax.random.key(seed)
        k1, k2, k3, k4 = jax.random.split(key, 4)
        patch_dim = 3 * PATCH * PATCH
        dim = 256
        img = jax.random.normal(k1, (64, 3, 96, 96), dtype=jnp.float32)
        ln1_w = jax.random.uniform(k2, (patch_dim,), dtype=jnp.float32, minval=0.9, maxval=1.1)
        W = jax.random.normal(k3, (dim, patch_dim), dtype=jnp.float32) * 0.02
        ln2_w = jax.random.uniform(k4, (dim,), dtype=jnp.float32, minval=0.9, maxval=1.1)
        return {'img': img, 'ln1_w': ln1_w, 'W': W, 'ln2_w': ln2_w}
    _L0_tok_all = _L0_tok_setup()
    _L0_tok_in = {k: v for k, v in _L0_tok_all.items() if k in ('ln1_w', 'W', 'ln2_w')}
    del _L0_tok_all

    def _L0_attn_setup():
        import jax, jax.numpy as jnp
        import numpy as np
        HEADS = 16
        DIM_HEAD = 64
        LN_EPS = 0.001
        key = jax.random.key(seed)
        ks = jax.random.split(key, 4)
        B, N, D = (8, 128, 256)
        inner = HEADS * DIM_HEAD
        return {'x': jax.random.normal(ks[0], (B, N, D), dtype=jnp.float32), 'w_qkv': jax.random.normal(ks[1], (D, 3 * inner), dtype=jnp.float32) * D ** (-0.5), 'reattn_w': jax.random.normal(ks[2], (HEADS, HEADS), dtype=jnp.float32), 'ln_gamma': jnp.ones((HEADS,), dtype=jnp.float32), 'ln_beta': jnp.zeros((HEADS,), dtype=jnp.float32), 'w_out': jax.random.normal(ks[3], (inner, D), dtype=jnp.float32) * inner ** (-0.5), 'b_out': jnp.zeros((D,), dtype=jnp.float32)}
    _L0_attn_all = _L0_attn_setup()
    _L0_attn_in = {k: v for k, v in _L0_attn_all.items() if k in ('w_qkv', 'reattn_w', 'ln_gamma', 'ln_beta', 'w_out', 'b_out')}
    del _L0_attn_all

    def _L0_ffn_setup():
        import jax, jax.numpy as jnp
        import numpy as np
        DIM = 256
        DEPTH = 7
        PAR = 8
        N_NODES = 2 ** (DEPTH + 1) - 1
        WIDTH = PAR * N_NODES
        key = jax.random.key(seed)
        k1, k2, k3, k4 = jax.random.split(key, 4)
        init_k = float(np.sqrt(1.0 / DIM))
        init_k2 = float(np.sqrt(1.0 / ((DEPTH + 1) * PAR)))
        oldx = jax.random.normal(k1, (4, 512, DIM), dtype=jnp.float32)
        W_in = jax.random.uniform(k2, (WIDTH, DIM), jnp.float32, -init_k, init_k)
        b_in = jax.random.uniform(k3, (WIDTH,), jnp.float32, -init_k, init_k)
        W_out = jax.random.uniform(k4, (DIM, WIDTH), jnp.float32, -init_k2, init_k2)
        return {'oldx': oldx, 'W_in': W_in, 'b_in': b_in, 'W_out': W_out}
    _L0_ffn_all = _L0_ffn_setup()
    _L0_ffn_in = {k: v for k, v in _L0_ffn_all.items() if k in ('W_in', 'b_in', 'W_out')}
    del _L0_ffn_all

    def _L1_attn_setup():
        import math
        import jax, jax.numpy as jnp
        import numpy as np
        N_HEADS = 16
        D_EMBED = 256
        key = jax.random.key(seed)
        ks = jax.random.split(key, 5)
        b, l, d = (2, 512, D_EMBED)
        return {'x': jax.random.normal(ks[0], (b, l, d), dtype=jnp.float32), 'w_in': jax.random.normal(ks[1], (3 * d, d), dtype=jnp.float32) * 0.02, 'b_in': jax.random.normal(ks[2], (3 * d,), dtype=jnp.float32) * 0.02, 'w_out': jax.random.normal(ks[3], (d, d), dtype=jnp.float32) * 0.02, 'b_out': jax.random.normal(ks[4], (d,), dtype=jnp.float32) * 0.02}
    _L1_attn_all = _L1_attn_setup()
    _L1_attn_in = {k: v for k, v in _L1_attn_all.items() if k in ('w_in', 'b_in', 'w_out', 'b_out')}
    del _L1_attn_all

    def _L1_ffn_setup():
        import jax, jax.numpy as jnp
        import numpy as np
        DIM = 256
        INTER = 352
        N_EXPERTS = 16
        TOPK = 2
        N_SHARED = 2
        SHARED_INTER = N_SHARED * INTER
        ROUTE_SCALE = 1.0
        key = jax.random.key(seed)
        ks = jax.random.split(key, 16)
        s = 0.02
        return {'x': jax.random.normal(ks[0], (2, 512, DIM), dtype=jnp.float32), 'gate_w': jax.random.normal(ks[1], (DIM, N_EXPERTS), dtype=jnp.float32) * s, 'gate_b': jnp.zeros((N_EXPERTS,), dtype=jnp.float32), 'w1': jax.random.normal(ks[2], (N_EXPERTS, DIM, INTER), dtype=jnp.float32) * s, 'b1': jnp.zeros((N_EXPERTS, INTER), dtype=jnp.float32), 'w3': jax.random.normal(ks[3], (N_EXPERTS, DIM, INTER), dtype=jnp.float32) * s, 'b3': jnp.zeros((N_EXPERTS, INTER), dtype=jnp.float32), 'w2': jax.random.normal(ks[4], (N_EXPERTS, INTER, DIM), dtype=jnp.float32) * s, 'b2': jnp.zeros((N_EXPERTS, DIM), dtype=jnp.float32), 'sw1': jax.random.normal(ks[5], (DIM, SHARED_INTER), dtype=jnp.float32) * s, 'sb1': jax.random.normal(ks[6], (SHARED_INTER,), dtype=jnp.float32) * s, 'sw3': jax.random.normal(ks[7], (DIM, SHARED_INTER), dtype=jnp.float32) * s, 'sb3': jax.random.normal(ks[8], (SHARED_INTER,), dtype=jnp.float32) * s, 'sw2': jax.random.normal(ks[9], (SHARED_INTER, DIM), dtype=jnp.float32) * s, 'sb2': jax.random.normal(ks[10], (DIM,), dtype=jnp.float32) * s}
    _L1_ffn_all = _L1_ffn_setup()
    _L1_ffn_in = {k: v for k, v in _L1_ffn_all.items() if k in ('gate_w', 'gate_b', 'w1', 'b1', 'w3', 'b3', 'w2', 'b2', 'sw1', 'sb1', 'sw3', 'sb3', 'sw2', 'sb2')}
    del _L1_ffn_all
    return {'x': x, 'L0_tok_ln1_w': _L0_tok_in['ln1_w'], 'L0_tok_W': _L0_tok_in['W'], 'L0_tok_ln2_w': _L0_tok_in['ln2_w'], 'L0_attn_w_qkv': _L0_attn_in['w_qkv'], 'L0_attn_reattn_w': _L0_attn_in['reattn_w'], 'L0_attn_ln_gamma': _L0_attn_in['ln_gamma'], 'L0_attn_ln_beta': _L0_attn_in['ln_beta'], 'L0_attn_w_out': _L0_attn_in['w_out'], 'L0_attn_b_out': _L0_attn_in['b_out'], 'L0_ffn_W_in': _L0_ffn_in['W_in'], 'L0_ffn_b_in': _L0_ffn_in['b_in'], 'L0_ffn_W_out': _L0_ffn_in['W_out'], 'L1_attn_w_in': _L1_attn_in['w_in'], 'L1_attn_b_in': _L1_attn_in['b_in'], 'L1_attn_w_out': _L1_attn_in['w_out'], 'L1_attn_b_out': _L1_attn_in['b_out'], 'L1_ffn_gate_w': _L1_ffn_in['gate_w'], 'L1_ffn_gate_b': _L1_ffn_in['gate_b'], 'L1_ffn_w1': _L1_ffn_in['w1'], 'L1_ffn_b1': _L1_ffn_in['b1'], 'L1_ffn_w3': _L1_ffn_in['w3'], 'L1_ffn_b3': _L1_ffn_in['b3'], 'L1_ffn_w2': _L1_ffn_in['w2'], 'L1_ffn_b2': _L1_ffn_in['b2'], 'L1_ffn_sw1': _L1_ffn_in['sw1'], 'L1_ffn_sb1': _L1_ffn_in['sb1'], 'L1_ffn_sw3': _L1_ffn_in['sw3'], 'L1_ffn_sb3': _L1_ffn_in['sb3'], 'L1_ffn_sw2': _L1_ffn_in['sw2'], 'L1_ffn_sb2': _L1_ffn_in['sb2']}

def reference(x, L0_tok_ln1_w, L0_tok_W, L0_tok_ln2_w, L0_attn_w_qkv, L0_attn_reattn_w, L0_attn_ln_gamma, L0_attn_ln_beta, L0_attn_w_out, L0_attn_b_out, L0_ffn_W_in, L0_ffn_b_in, L0_ffn_W_out, L1_attn_w_in, L1_attn_b_in, L1_attn_w_out, L1_attn_b_out, L1_ffn_gate_w, L1_ffn_gate_b, L1_ffn_w1, L1_ffn_b1, L1_ffn_w3, L1_ffn_b3, L1_ffn_w2, L1_ffn_b2, L1_ffn_sw1, L1_ffn_sb1, L1_ffn_sw3, L1_ffn_sb3, L1_ffn_sw2, L1_ffn_sb2):
    import jax
    import jax.numpy as jnp

    def _L0_tok_ref(img, ln1_w, W, ln2_w):
        import jax, jax.numpy as jnp
        import numpy as np
        PATCH = 16
        EPS = 1e-05

        def _patchify(img, p):
            B, C, H, W = img.shape
            h, w = (H // p, W // p)
            x = img.reshape(B, C, h, p, w, p)
            x = x.transpose(0, 2, 4, 1, 3, 5)
            return x.reshape(B, h, w, C * p * p)

        def _layernorm(x, gamma):
            mu = x.mean(axis=-1, keepdims=True)
            var = ((x - mu) ** 2).mean(axis=-1, keepdims=True)
            return (x - mu) * jax.lax.rsqrt(var + EPS) * gamma

        def _posemb_sincos_2d(h, w, dim, temperature=10000.0, dtype=jnp.float32):
            y, x = jnp.meshgrid(jnp.arange(h, dtype=dtype), jnp.arange(w, dtype=dtype), indexing='ij')
            omega = jnp.arange(dim // 4, dtype=dtype) / (dim // 4 - 1)
            omega = 1.0 / temperature ** omega
            y = y.reshape(-1)[:, None] * omega[None, :]
            x = x.reshape(-1)[:, None] * omega[None, :]
            return jnp.concatenate([jnp.sin(x), jnp.cos(x), jnp.sin(y), jnp.cos(y)], axis=1)
        patches = _patchify(img, PATCH)
        B, h, w, d = patches.shape
        x = patches.reshape(B, h * w, d)
        x = _layernorm(x, ln1_w)
        x = jnp.einsum('bnd,ed->bne', x, W)
        x = _layernorm(x, ln2_w)
        pe = _posemb_sincos_2d(h, w, x.shape[-1], dtype=x.dtype)
        return x + pe[None, :, :]

    def _L0_attn_ref(x, w_qkv, reattn_w, ln_gamma, ln_beta, w_out, b_out):
        import jax, jax.numpy as jnp
        import numpy as np
        HEADS = 16
        DIM_HEAD = 64
        LN_EPS = 0.001
        B, N, D = x.shape
        H, dh = (HEADS, DIM_HEAD)
        scale = dh ** (-0.5)
        qkv = x @ w_qkv
        q, k, v = jnp.split(qkv, 3, axis=-1)
        to_heads = lambda t: t.reshape(B, N, H, dh).transpose(0, 2, 1, 3)
        q, k, v = (to_heads(q), to_heads(k), to_heads(v))
        dots = jnp.einsum('bhid,bhjd->bhij', q, k) * scale
        attn = jax.nn.softmax(dots, axis=-1)
        attn = jnp.einsum('bhij,hg->bgij', attn, reattn_w)
        mean = jnp.mean(attn, axis=1, keepdims=True)
        var = jnp.var(attn, axis=1, keepdims=True)
        attn = (attn - mean) * jax.lax.rsqrt(var + LN_EPS)
        attn = attn * ln_gamma[None, :, None, None] + ln_beta[None, :, None, None]
        out = jnp.einsum('bhij,bhjd->bhid', attn, v)
        out = out.transpose(0, 2, 1, 3).reshape(B, N, H * dh)
        return out @ w_out + b_out

    def _L0_ffn_ref(oldx, W_in, b_in, W_out):
        import jax, jax.numpy as jnp
        import numpy as np
        DIM = 256
        DEPTH = 7
        PAR = 8
        N_NODES = 2 ** (DEPTH + 1) - 1
        WIDTH = PAR * N_NODES
        x = oldx.reshape(-1, DIM)
        B = x.shape[0]
        logits = x @ W_in.T + b_in
        decisions = (logits > 0).astype(jnp.int32).reshape(B, PAR, N_NODES)
        acts = jax.nn.silu(logits).reshape(B, PAR, N_NODES)
        current = jnp.zeros((B, PAR), dtype=jnp.int32)
        dmap = jax.nn.one_hot(current, N_NODES, dtype=acts.dtype)
        for d in range(DEPTH):
            cur_platform = 2 ** d - 1
            next_platform = 2 ** (d + 1) - 1
            moves = jnp.take_along_axis(decisions, current[..., None], axis=2)[..., 0]
            current = (current - cur_platform) * 2 + moves + next_platform
            dmap = dmap + jax.nn.one_hot(current, N_NODES, dtype=acts.dtype)
        masked = acts * jax.lax.stop_gradient(dmap)
        out = masked.reshape(B, WIDTH) @ W_out.T
        return out.reshape(oldx.shape)

    def _L1_attn_ref(x, w_in, b_in, w_out, b_out):
        import math
        import jax, jax.numpy as jnp
        import numpy as np
        N_HEADS = 16
        D_EMBED = 256
        b, l, d = x.shape
        h = N_HEADS
        scale = 1.0 / math.sqrt(d // h)
        x_proj = (x @ w_in.T + b_in).reshape(b, l, h, -1)
        q, k, v = jnp.split(x_proj, 3, axis=-1)
        att = jnp.einsum('blhd,bmhd->blmh', q, k) * scale
        att = jax.nn.softmax(att, axis=2)
        opt = jnp.einsum('blmh,blhd->blhd', att, v).reshape(b, l, d)
        return opt @ w_out.T + b_out

    def _L1_ffn_ref(x, gate_w, gate_b, w1, b1, w3, b3, w2, b2, sw1, sb1, sw3, sb3, sw2, sb2):
        import jax, jax.numpy as jnp
        import numpy as np
        DIM = 256
        INTER = 352
        N_EXPERTS = 16
        TOPK = 2
        N_SHARED = 2
        SHARED_INTER = N_SHARED * INTER
        ROUTE_SCALE = 1.0
        shape = x.shape
        xf = x.reshape(-1, DIM)
        logits = xf @ gate_w + gate_b
        scores = jax.nn.softmax(logits.astype(jnp.float32), axis=-1)
        top_vals, top_idx = jax.lax.top_k(scores, TOPK)
        weights = (top_vals * ROUTE_SCALE).astype(x.dtype)
        cw = (jax.nn.one_hot(top_idx, N_EXPERTS, dtype=x.dtype) * weights[..., None]).sum(axis=1)
        h = jnp.einsum('td,edh->teh', xf, w1) + b1
        g = jnp.einsum('td,edh->teh', xf, w3) + b3
        a = jax.nn.silu(h) * g
        y = jnp.einsum('teh,ehd,te->td', a, w2, cw) + cw @ b2
        z = jax.nn.silu(xf @ sw1 + sb1) * (xf @ sw3 + sb3) @ sw2 + sb2
        return (y + z).reshape(shape)
    h = _L0_tok_ref(x, L0_tok_ln1_w, L0_tok_W, L0_tok_ln2_w)
    h = h + _L0_attn_ref(_layernorm(h, axis=-1), L0_attn_w_qkv, L0_attn_reattn_w, L0_attn_ln_gamma, L0_attn_ln_beta, L0_attn_w_out, L0_attn_b_out)
    h = h + _L0_ffn_ref(_layernorm(h, axis=-1), L0_ffn_W_in, L0_ffn_b_in, L0_ffn_W_out)
    h = h + _L1_attn_ref(_layernorm(h, axis=-1), L1_attn_w_in, L1_attn_b_in, L1_attn_w_out, L1_attn_b_out)
    h = h + _L1_ffn_ref(_layernorm(h, axis=-1), L1_ffn_gate_w, L1_ffn_gate_b, L1_ffn_w1, L1_ffn_b1, L1_ffn_w3, L1_ffn_b3, L1_ffn_w2, L1_ffn_b2, L1_ffn_sw1, L1_ffn_sb1, L1_ffn_sw3, L1_ffn_sb3, L1_ffn_sw2, L1_ffn_sb2)
    return h

_drawn_inputs = setup_inputs


def setup_inputs(seed=0):
    import zlib

    import numpy as np

    out = dict(_drawn_inputs(seed))
    spreads = {'L0_attn_ln_gamma': (1.0, 0.2),
     'L0_attn_ln_beta': (0.0, 0.1),
     'L0_attn_b_out': (0.0, 0.8),
     'L1_ffn_gate_b': (0.0, 0.8),
     'L1_ffn_b1': (0.0, 0.8),
     'L1_ffn_b3': (0.0, 0.8),
     'L1_ffn_b2': (0.0, 2.0)}
    factors = {'L0_ffn_W_in': 3.979,
     'L0_ffn_b_in': 8.0,
     'L0_ffn_W_out': 4.109,
     'L1_attn_w_in': 6.97,
     'L1_attn_b_in': 8.0,
     'L1_attn_w_out': 7.188,
     'L1_attn_b_out': 24.663,
     'L1_ffn_gate_w': 8.0,
     'L1_ffn_w1': 8.0,
     'L1_ffn_w3': 8.0,
     'L1_ffn_w2': 8.0,
     'L1_ffn_sw1': 8.0,
     'L1_ffn_sb1': 8.0,
     'L1_ffn_sw3': 8.0,
     'L1_ffn_sb3': 8.0,
     'L1_ffn_sw2': 8.0,
     'L1_ffn_sb2': 64.0}
    for name, (base, spread) in spreads.items():
        noise = np.random.default_rng([zlib.crc32(name.encode()), seed]).standard_normal(out[name].shape)
        drawn = base * np.exp(spread * noise) if base else spread * noise
        out[name] = jnp.asarray(drawn.astype(out[name].dtype))
    for name, factor in factors.items():
        out[name] = (out[name] * factor).astype(out[name].dtype)
    return out
```

```python
from contextlib import ExitStack

import numpy as np

import concourse.bass as bass
from concourse import mybir

F32 = mybir.dt.float32
BF16 = mybir.dt.bfloat16
I32 = mybir.dt.int32
U32 = mybir.dt.uint32
ALU = mybir.AluOpType
ACT = mybir.ActivationFunctionType
X = mybir.AxisListType.X

B, L, D = 64, 36, 256
T = B * L
PD = 768
KP = PD // 128
IB = 8
NB = B // IB
TB = IB * L
TT = 96
NT = TB // TT
PAIRS = IB // 2
PT = 2 * L
SLOT = 64
SP2 = SLOT + L
DC = D // 128
H = 16
DH = 64
INNER = H * DH
QC = INNER // 128
IG = 8
NG = (L + IG - 1) // IG
LAST = L - (NG - 1) * IG
TREES, NODES = 8, 256
FC = TREES * 2
E_, INTER = 16, 352
SH = 704
SC = (SH + 127) // 128
IC = (INTER + 127) // 128
SLOTS = T * 2
TILES = (SLOTS + E_ * 127) // 128
GT = T // TT
SETUP = 23


def layout(parts):
    at, out = 0, {}
    for name, width in parts:
        out[name] = (at, width)
        at += width
    return out, at


COLS, CW = layout([("ident", 128), ("ones", 128), ("pair", PT), ("own", 2), ("query", IG),
                   ("head4", 4), ("right", 2), ("below", TT), ("below16", E_), ("iota", E_),
                   ("half", 4), ("pos", NT * D), ("minushalf", L), ("starts", TILES)])


def constants():
    c = np.zeros((128, CW), np.float32)

    def put(name, a):
        at, w = COLS[name]
        c[:a.shape[0], at:at + w] = a

    r = np.arange(128)
    put("ident", np.eye(128))
    put("ones", np.ones((128, 128)))
    pair = np.zeros((128, PT))
    for m in range(2):
        pair[m * SLOT + np.arange(L), m * L + np.arange(L)] = 1
    put("pair", pair)
    put("own", np.stack([r < L, (r >= L) & (r < PT)], 1))
    put("query", r[:, None] // H == np.arange(IG))
    put("head4", (r[:, None] % 64) // 16 == np.arange(4))
    put("below", r[:, None] < np.arange(TT))
    put("below16", r[:, None] < np.arange(E_))
    put("iota", np.tile(np.arange(E_), (128, 1)))
    put("minushalf", np.full((128, L), -0.5))
    put("starts", np.tile(128 * np.arange(TILES), (128, 1)))
    toward = np.zeros((128, NODES), np.float32)
    rights = np.full((128, 2), 99.0)
    for node in range(NODES - 1):
        n, k = node, 0
        while n:
            up = (n - 1) // 2
            toward[up, node] = 1 if n == 2 * up + 2 else -1
            k += n == 2 * up + 2
            n = up
        rights[node % 128, node // 128] = k
    put("right", rights)
    w = np.float32(1) / np.float32(10000.0) ** (np.arange(D // 4, dtype=np.float32) / np.float32(D // 4 - 1))
    y, x = np.meshgrid(np.arange(6, dtype=np.float32), np.arange(6, dtype=np.float32), indexing="ij")
    y, x = y.reshape(-1)[:, None] * w, x.reshape(-1)[:, None] * w
    pos = np.concatenate([np.sin(x), np.cos(x), np.sin(y), np.cos(y)], 1)
    put("pos", np.tile(pos, (IB, 1)).reshape(NT, TT, D).transpose(1, 0, 2).reshape(TT, NT * D))
    return c, toward


def program(nc, dram, out_dram):
    ctx = ExitStack()
    with ctx:
        def sb(name, shape, dt=F32):
            return ctx.enter_context(nc.sbuf_tensor(name, shape, dt))

        def semaphore(name):
            return ctx.enter_context(nc.semaphore(name))

        spill_h = nc.dram_tensor("spill_h", [T, D], F32, kind="Internal").ap()
        spill_x = nc.dram_tensor("spill_x", [T, D], F32, kind="Internal").ap()
        slot_x = nc.dram_tensor("slot_x", [TILES * 128, D], F32, kind="Internal").ap()
        slot_y = nc.dram_tensor("slot_y", [TILES * 128, D], F32, kind="Internal").ap()

        bank = [ctx.enter_context(nc.psum_tensor(f"bank{i}", [128, 512], F32)) for i in range(8)]
        oh = sb("oh", [TT, 2, GT, E_])
        gate = sb("gate", [TT, GT, 2])
        rank = sb("rank", [TT, 2, GT])
        load = sb("load", [TT, E_])
        const = sb("const", [128, CW])

        def C(name, parts=128):
            at, w = COLS[name]
            return const[0:parts, at:at + w]

        phase1(nc, dram, bank, oh, gate, rank, load, const, C, spill_h, spill_x, slot_x, semaphore)
        phase2(nc, dram, out_dram, bank, oh, gate, rank, load, const, C, spill_h, spill_x, slot_x, slot_y, semaphore)


def wait_apart(eng, sem, value, passed):
    eng.wait_ge(sem, value)
    eng.sem_inc(passed, 1)


class Signal:

    def __init__(self, sem, per):
        self.sem, self.per = sem, per

    def at(self, rnd, k):
        return rnd * self.per + k


def phase1(nc, dram, bank, oh, gate, rank, load, const, C, spill_h, spill_x, slot_x, semaphore):
    ctx = ExitStack()
    with ctx:
        def sb(name, shape, dt=F32):
            return ctx.enter_context(nc.sbuf_tensor(name, shape, dt))

        def sig(name, per=1):
            return Signal(semaphore(name), per)

        w_tok = sb("w_tok", [128, KP, D])
        w_qkv = sb("w_qkv", [128, DC, 3 * INNER])
        w_out0 = sb("w_out0", [128, QC, D])
        w_tree = sb("w_tree", [128, DC, TREES * NODES])
        w_leaf = sb("w_leaf", [128, FC, D])
        w_in1 = sb("w_in1", [128, DC, 3 * D])
        w_out1 = sb("w_out1", [128, DC, D])
        w_sh1 = sb("w_sh1", [128, DC, SH])
        w_sh3 = sb("w_sh3", [128, DC, SH])
        w_sh2 = sb("w_sh2", [128, SC, D])
        w_gate = sb("w_gate", [128, DC, E_])
        b_gate = sb("b_gate", [TT, E_])
        g_ln1 = sb("g_ln1", [128, KP])
        g_ln2 = sb("g_ln2", [TT, D])
        g_head = sb("g_head", [PT, H])
        b_head = sb("b_head", [128, QC])
        b_out0 = sb("b_out0", [128, DC])
        b_tree = sb("b_tree", [128, FC])
        b_in1 = sb("b_in1", [128, 6])
        b_q1 = sb("b_q1", [128, DC])
        b_out1 = sb("b_out1", [128, DC])
        b_sh1 = sb("b_sh1", [128, SC])
        b_sh3 = sb("b_sh3", [128, SC])
        b_sh2 = sb("b_sh2", [128, DC])
        toward = sb("toward", [128, NODES], BF16)
        wx = sb("wx", [128, H])
        wm = sb("wm", [128, 2])
        mix8 = sb("mix8", [128, IG, H])
        patch = sb("patch", [TT, NT, PD])
        stA = sb("stA", [TT, NT, 12])
        mvA = sb("mvA", [TT, NT, 2])
        rsA = sb("rsA", [TT, 2, NT])
        wide = sb("wide", [128, 8, TB])
        hA = sb("hA", [TT, NT, D])
        xA = sb("xA", [TT, NT, D])
        xTA = sb("xTA", [128, DC, TB])
        qk = sb("qk", [128, 2 * QC, TB])
        xsum = sb("xsum", [128, DC, IB])
        vbias = sb("vbias", [128, QC, IB])
        val = sb("val", [PT, INNER])
        sc = sb("sc", [SP2, L, H])
        prob = sb("prob", [128, NG, PT])
        pmax = sb("pmax", [128, 3, NG, 2])
        sq = sb("sq", [PT, L, H])
        var = sb("var", [PT, 3, L])
        own = sb("own", [PT, 2, L])
        mixed_in = sb("mixed_in", [128, H * PT])
        att = mixed_in[0:PT, :].rearrange("q (g m i) -> q g m i", g=H, m=2)
        yTA = mixed_in[:, 0:DC * TB].rearrange("p (c t) -> p c t", c=DC)
        stB = sb("stB", [TT, NT, 6])
        mvB = sb("mvB", [TT, NT, 2])
        rsB = sb("rsB", [TT, 2, NT])
        hB = sb("hB", [TT, NT, D])
        xB = sb("xB", [TT, NT, D])
        xTB = sb("xTB", [128, DC, TB])
        th = sb("th", [128, 2, TB])
        zb = sb("zb", [128, 2, TB])
        toward32 = th[:, :, :].rearrange("p a t -> p (a t)")[:, 0:NODES]
        dec = sb("dec", [128, TB], BF16)
        big = sb("big", [128, 20, TB])
        k4 = big[:, 0:8, :].rearrange("p (c a) t -> p c a t", c=DC)
        q1 = big[:, 8:10, :]
        v1 = big[:, 10:12, :]
        o1 = big[:, 12:14, :]
        up = big[:, 14:20, :]
        soft = sb("soft", [128, H * L])
        e1 = soft[0:SP2, :].rearrange("q (h l) -> q h l", h=H)
        yTB = soft[:, :].rearrange("p (c t) -> p c t", c=DC)
        m1 = sb("m1", [SP2, 3, H])
        r1 = sb("r1", [SP2, H, 16])
        lg = sb("lg", [TT, 2, E_])
        top = sb("top", [TT, 8])
        topi = sb("topi", [TT, 8], U32)
        topf = sb("topf", [TT, 2])
        gsum = sb("gsum", [TT, 4])
        both = sb("both", [TT, E_])
        rk = sb("rk", [TT, 2, E_])
        zero = sb("zero", [128, D])

        weights_in = semaphore("weights_in")
        pe_passed = semaphore("pe_passed")
        dve_passed = semaphore("dve_passed")
        pool_passed = semaphore("pool_passed")
        made = semaphore("made")
        patch_in = sig("patch_in", 16)
        patch_stats = sig("patch_stats", 3 * NT)
        patch_rstd = sig("patch_rstd", 2)
        patch_norm = sig("patch_norm", NT)
        patch_turned = sig("patch_turned", KP)
        patch_T = sig("patch_T", KP)
        emb = sig("emb", 2)
        emb_T = sig("emb_T", 2)
        emb_turned = sig("emb_turned", 1)
        emb_stats = sig("emb_stats", 2 * NT)
        emb_rstd = sig("emb_rstd", 2)
        emb_steps = sig("emb_steps", 3 * NT)
        statsA = sig("statsA", 2 * NT)
        rstdA = sig("rstdA", 2)
        xA_ready = sig("xA_ready", NT)
        xA_turned = sig("xA_turned", 1)
        xTA_ready = sig("xTA_ready", 2)
        qk_done = sig("qk_done", 2 * QC)
        qk_ready = sig("qk_ready", 2 * QC)
        xsum_ready = sig("xsum_ready", 1)
        vsum_done = sig("vsum_done", 1)
        vbias_ready = sig("vbias_ready", 1)
        v_done = sig("v_done", PAIRS)
        v_ready = sig("v_ready", 2 * PAIRS)
        sc_done = sig("sc_done", PAIRS)
        sc_ready = sig("sc_ready", 2 * PAIRS)
        sc_turned = sig("sc_turned", PAIRS)
        sm_steps = sig("sm_steps", 5 * PAIRS)
        exp_done = sig("exp_done", PAIRS)
        mixed = sig("mixed", PAIRS)
        squared = sig("squared", 2 * PAIRS)
        mixvar = sig("mixvar", PAIRS)
        mix_rstd = sig("mix_rstd", 3 * PAIRS)
        att_ready = sig("att_ready", 2 * PAIRS)
        av_done = sig("av_done", 2 * PAIRS)
        av_ready = sig("av_ready", 2 * PAIRS)
        out0_done = sig("out0_done", 2)
        out0_T = sig("out0_T", 2)
        out0_turned = sig("out0_turned", 1)
        hB_ready = sig("hB_ready", 4 * NT)
        statsB = sig("statsB", 2 * 3 * NT)
        rstdB = sig("rstdB", 2 * 3)
        xB_ready = sig("xB_ready", 3 * NT)
        xB_turned = sig("xB_turned", 3)
        xTB_ready = sig("xTB_ready", 2 * 3)
        projB = sig("projB", 2 * 3)
        projB_T = sig("projB_T", 2 * 3)
        projB_turned = sig("projB_turned", 3)
        z_done = sig("z_done", FC)
        z_tanh = sig("z_tanh", FC)
        z_half = sig("z_half", FC)
        z_silu = sig("z_silu", FC)
        decided = sig("decided", TREES)
        path_done = sig("path_done", FC)
        leaf_ready = sig("leaf_ready", FC)
        qkv1_done = sig("qkv1_done", 6)
        q1_ready = sig("q1_ready", 2)
        k1_ready = sig("k1_ready", 8)
        v1_ready = sig("v1_ready", 2)
        sc1_done = sig("sc1_done", PAIRS)
        sm1_steps = sig("sm1_steps", 8 * PAIRS)
        exp1_done = sig("exp1_done", PAIRS)
        r1_turned = sig("r1_turned", PAIRS)
        o1_ready = sig("o1_ready", PAIRS)
        sh_done = sig("sh_done", 2 * SC)
        sh_tanh = sig("sh_tanh", SC)
        sh_steps = sig("sh_steps", 3 * SC)
        lg_done = sig("lg_done", NT)
        rt_steps = sig("rt_steps", 14 * NT)
        rt_exp = sig("rt_exp", NT)
        rank_done = sig("rank_done", NT)
        spilled = sig("spilled", 32)
        zeroed = semaphore("zeroed")
        ranked = sig("ranked", 2 * NT)

        loads = [
            (const[:, :], dram["const"]), (w_tok[:, :, :], dram["w_tok"]), (w_qkv[:, :, :], dram["w_qkv"]),
            (w_out0[:, :, :], dram["w_out0"]), (w_tree[:, :, :], dram["w_tree"]), (w_leaf[:, :, :], dram["w_leaf"]),
            (w_in1[:, :, :], dram["w_in1"]), (w_out1[:, :, :], dram["w_out1"]), (w_sh1[:, :, :], dram["w_sh1"]),
            (w_sh3[:, :, :], dram["w_sh3"]), (w_sh2[:, :, :], dram["w_sh2"]), (w_gate[:, :, :], dram["w_gate"]),
            (b_gate[:, :], dram["b_gate"].partition_broadcast(TT)), (g_ln1[:, :], dram["g_ln1"]),
            (g_ln2[:, :], dram["g_ln2"].partition_broadcast(TT)),
            (g_head[:, :], dram["g_head"].partition_broadcast(PT)), (b_out0[:, :], dram["b_out0"]),
            (b_tree[:, :], dram["b_tree"]), (b_in1[:, :], dram["b_in1"]), (b_out1[:, :], dram["b_out1"]),
            (b_sh1[:, :], dram["b_sh1"]), (b_sh3[:, :], dram["b_sh3"]), (b_sh2[:, :], dram["b_sh2"]),
            (toward32, dram["toward"]), (b_head[:, :], dram["b_head"]),
            (wx[:, :], dram["wx"]),
        ]
        WEIGHTS = 16 * len(loads)
        ident = C("ident")
        A_STEPS = ["patch", "embed", "normA", "qk", "pair0", "pair1", "pair2", "pair3", "out0"]
        B_STEPS = ["tree0", "tree1", "tree2", "tree3", "leaf", "qkv1", "pairs1", "out1", "shared"]
        MIXED = [("A", "patch"), ("B", "tree0"), ("A", "embed"), ("B", "tree1"), ("A", "normA"), ("B", "tree2"),
                 ("A", "qk"), ("B", "tree3"), ("A", "pair0"), ("B", "leaf"), ("A", "pair1"), ("B", "qkv1"),
                 ("A", "pair2"), ("B", "pairs1"), ("B", "out1"), ("A", "pair3"), ("B", "shared"), ("A", "out0")]

        def rounds(eng, steps):
            for s in A_STEPS:
                steps(s, 0)
            with eng.Fori(1, NB) as i:
                for thread, s in MIXED:
                    steps(s, i if thread == "A" else i - 1)
            for s in B_STEPS:
                steps(s, NB - 1)

        block = ctx.enter_context(nc.Block())

        @block.sync
        def _(sp):
            for dst, src in loads:
                sp.dma_start(dst, src).then_inc(weights_in, 16)
            sp.wait_ge(made, 1)
            for t in range(TILES):
                sp.dma_start(slot_x[t * 128:(t + 1) * 128, :], zero[:, :]).then_inc(zeroed, 16)

            def steps(s, r):
                if s == "patch":
                    sp.wait_ge(patch_turned.sem, patch_turned.at(r, 0))
                    sp.dma_start(patch[:, :, :], dram["patches"][bass.ds(r * TT, TT), :, :]).then_inc(patch_in.sem, 16)
                if s == "shared":
                    sp.wait_ge(hB_ready.sem, hB_ready.at(r, 4 * NT))
                    sp.dma_start(spill_h[bass.ds(r * TB, TB), :].rearrange("(j p) d -> p j d", p=TT),
                                 hB[:, :, :]).then_inc(spilled.sem, 16)
                    sp.dma_start(spill_x[bass.ds(r * TB, TB), :].rearrange("(j p) d -> p j d", p=TT),
                                 xB[:, :, :]).then_inc(spilled.sem, 16)

            rounds(sp, steps)
            sp.wait_ge(spilled.sem, 32 * NB)
            sp.wait_ge(zeroed, 16 * TILES)

        @block.gpsimd
        def _(pool):
            minus = C("minushalf")

            def inverse_root(out, mid, var_ap, done, r, k, eps):
                nc.gpsimd.tensor_scalar(mid, var_ap, 1.0, eps, ALU.mult, ALU.add).then_inc(done.sem, 1)
                pool.wait_ge(done.sem, done.at(r, k + 1))
                n = mid.shape[-1]
                nc.gpsimd.tensor_tensor(out, mid, minus[0:mid.shape[0], 0:n], ALU.pow).then_inc(done.sem, 1)

            pool.wait_ge(weights_in, WEIGHTS)

            def steps(s, r):
                if s == "patch":
                    wait_apart(pool, patch_stats.sem, patch_stats.at(r, 3 * NT), pool_passed)
                    inverse_root(rsA[:, 1, :], rsA[:, 0, :], mvA[:, :, 1], patch_rstd, r, 0, 1e-5)
                if s == "embed":
                    wait_apart(pool, emb_stats.sem, emb_stats.at(r, 2 * NT), pool_passed)
                    inverse_root(rsA[:, 1, :], rsA[:, 0, :], mvA[:, :, 1], emb_rstd, r, 0, 1e-5)
                if s == "normA":
                    wait_apart(pool, statsA.sem, statsA.at(r, 2 * NT), pool_passed)
                    inverse_root(rsA[:, 1, :], rsA[:, 0, :], mvA[:, :, 1], rstdA, r, 0, 1e-5)
                if s.startswith("pair") and s != "pairs1":
                    p = int(s[4:])
                    wait_apart(pool, mixvar.sem, mixvar.at(r, p + 1), pool_passed)
                    nc.gpsimd.tensor_scalar(var[:, 1, :], var[:, 0, :], 1.0 / H, 1e-3,
                                            ALU.mult, ALU.add).then_inc(mix_rstd.sem, 1)
                    pool.wait_ge(mix_rstd.sem, mix_rstd.at(r, 3 * p + 1))
                    nc.gpsimd.tensor_tensor(var[:, 2, :], var[:, 1, :], minus[0:PT, 0:L], ALU.pow).then_inc(mix_rstd.sem, 1)
                    pool.wait_ge(mix_rstd.sem, mix_rstd.at(r, 3 * p + 2))
                    nc.gpsimd.tensor_tensor(own[:, :, :], var[:, 2, :].unsqueeze(1).to_broadcast([PT, 2, L]),
                                            C("own", PT).unsqueeze(2).to_broadcast([PT, 2, L]),
                                            ALU.mult).then_inc(mix_rstd.sem, 1)
                for g, name in enumerate(["out0", "leaf", "out1"]):
                    if s == name:
                        wait_apart(pool, statsB.sem, statsB.at(r, 2 * NT * (g + 1)), pool_passed)
                        inverse_root(rsB[:, 1, :], rsB[:, 0, :], mvB[:, :, 1], rstdB, r, 2 * g, 1e-5)

            rounds(pool, steps)

        @block.scalar
        def _(act):
            def copy(dst, src, sem, **kw):
                nc.scalar.activation(dst, src, ACT.Identity, **kw).then_inc(sem.sem, 1)

            act.wait_ge(weights_in, WEIGHTS)
            act.wait_ge(made, SETUP)

            def turn_in(xT, turned, ready, r, k):
                act.wait_ge(turned.sem, turned.at(r, k + 1))
                for m in range(DC):
                    copy(xT[:, m, :], bank[(0 if xT is xTA else 5) + m][:, 0:TB], ready)

            def glueB(r, g, bias):
                for m in range(DC):
                    act.wait_ge(projB.sem, projB.at(r, 2 * g + m + 1))
                    if bias is None:
                        copy(yTB[:, m, :], bank[5 + m][:, 0:TB], projB_T)
                    else:
                        copy(yTB[:, m, :], bank[5 + m][:, 0:TB], projB_T, bias=bias[:, m:m + 1])

            def steps(s, r):
                if s == "patch":
                    for k in range(KP):
                        act.wait_ge(patch_turned.sem, patch_turned.at(r, k + 1))
                        copy(wide[:, k, :], bank[k % 2][:, 0:TB], patch_T)
                if s == "embed":
                    for m in range(DC):
                        act.wait_ge(emb.sem, emb.at(r, m + 1))
                        copy(yTA[:, m, :], bank[m][:, 0:TB], emb_T)
                if s == "normA":
                    turn_in(xTA, xA_turned, xTA_ready, r, 0)
                if s == "qk":
                    for c in range(2 * QC):
                        act.wait_ge(qk_done.sem, qk_done.at(r, c + 1))
                        copy(qk[:, c, :], bank[c % 2][:, 0:TB], qk_ready, scale=DH ** -0.5 if c < QC else 1.0)
                if s.startswith("pair") and s != "pairs1":
                    p = int(s[4:])
                    act.wait_ge(sc_done.sem, sc_done.at(r, p + 1))
                    sv = sc[:, :, :].rearrange("q l (a e) -> q e a l", e=2)
                    for e in range(2):
                        copy(sv[:, e], bank[e][0:SP2, 0:8 * L].rearrange("q (a l) -> q a l", l=L), sc_ready)
                    act.wait_ge(sm_steps.sem, sm_steps.at(r, 5 * p + 2))
                    nc.scalar.activation(prob[:, :, :], prob[:, :, :], ACT.Exp).then_inc(exp_done.sem, 1)
                    act.wait_ge(mixed.sem, mixed.at(r, p + 1))
                    for part, (i0, i1) in enumerate(((0, 32), (32, L))):
                        nc.scalar.activation(sq[:, i0:i1, :].rearrange("q i g -> q (i g)"),
                                             bank[3 + part][0:PT, 0:(i1 - i0) * H], ACT.Square).then_inc(squared.sem, 1)
                if s == "out0":
                    for m in range(DC):
                        act.wait_ge(out0_done.sem, out0_done.at(r, m + 1))
                        copy(yTA[:, m, :], bank[m][:, 0:TB], out0_T, bias=b_out0[:, m:m + 1])
                    turn_in(xTB, xB_turned, xTB_ready, r, 0)
                if s.startswith("tree"):
                    for c in range(4 * int(s[4:]), 4 * int(s[4:]) + 4):
                        act.wait_ge(z_half.sem, z_half.at(r, c + 1))
                        nc.scalar.activation(th[:, c % 2, :], zb[:, c % 2, :], ACT.Tanh).then_inc(z_tanh.sem, 1)
                if s == "leaf":
                    glueB(r, 0, None)
                    turn_in(xTB, xB_turned, xTB_ready, r, 1)
                if s == "qkv1":
                    for c in (0, 1):
                        act.wait_ge(qkv1_done.sem, qkv1_done.at(r, c + 1))
                        copy(q1[:, c, :], bank[5 + c % 2][:, 0:TB], q1_ready, scale=0.25, bias=b_q1[:, c:c + 1])
                    for c in (4, 5):
                        act.wait_ge(qkv1_done.sem, qkv1_done.at(r, c + 1))
                        copy(v1[:, c - 4, :], bank[5 + c % 2][:, 0:TB], v1_ready, bias=b_in1[:, c:c + 1])
                if s == "pairs1":
                    for p in range(PAIRS):
                        act.wait_ge(sm1_steps.sem, sm1_steps.at(r, 8 * p + 4))
                        nc.scalar.activation(e1[:, :, :], e1[:, :, :], ACT.Exp).then_inc(exp1_done.sem, 1)
                if s == "out1":
                    glueB(r, 1, b_out1)
                    turn_in(xTB, xB_turned, xTB_ready, r, 2)
                if s == "shared":
                    for c in range(SC):
                        n = min(128, SH - 128 * c)
                        act.wait_ge(sh_steps.sem, sh_steps.at(r, 3 * c + 1))
                        nc.scalar.activation(th[0:n, c % 2, :], zb[0:n, c % 2, :], ACT.Tanh).then_inc(sh_tanh.sem, 1)
                    for j in range(NT):
                        act.wait_ge(rt_steps.sem, rt_steps.at(r, 14 * j + 3))
                        nc.scalar.activation(lg[:, 1, :], lg[:, 1, :], ACT.Exp).then_inc(rt_exp.sem, 1)
                    glueB(r, 2, b_sh2)

            rounds(act, steps)

        @block.tensor
        def _(pe):
            def project(dst, weight, x, cols, chunks, sig_, rows=None):
                for k in range(chunks):
                    n = 128 if rows is None else min(128, rows - 128 * k)
                    last = nc.tensor.matmul(dst, weight[0:n, k, cols], x[0:n, k, :], start=k == 0, stop=k == chunks - 1)
                last.then_inc(sig_.sem, 1)

            def turn_out(yT, b0, turned):
                for j in range(NT):
                    for m in range(DC):
                        last = nc.tensor.transpose(bank[b0 + j // 2][0:TT, (j % 2) * D + m * 128:(j % 2) * D + (m + 1) * 128],
                                                   yT[:, m, j * TT:(j + 1) * TT], ident)
                last.then_inc(turned.sem, 1)

            def turn_back(x, b0, turned):
                for j in range(NT):
                    for m in range(DC):
                        last = nc.tensor.transpose(bank[b0 + m][:, j * TT:(j + 1) * TT],
                                                   x[:, j, m * 128:(m + 1) * 128], ident[0:TT, 0:TT])
                last.then_inc(turned.sem, 1)

            pe.wait_ge(weights_in, WEIGHTS)
            pe.wait_ge(made, SETUP)

            def glueB(r, g):
                pe.wait_ge(projB_T.sem, projB_T.at(r, 2 * g + 2))
                turn_out(yTB, 5, projB_turned)
                if g < 2:
                    pe.wait_ge(xB_ready.sem, xB_ready.at(r, NT * (g + 2)))
                    turn_back(xB, 5, xB_turned)

            def path(r, c):
                pe.wait_ge(decided.sem, decided.at(r, c // 2 + 1))
                if c:
                    pe.wait_ge(leaf_ready.sem, leaf_ready.at(r, c))
                nc.tensor.matmul(bank[7][:, 0:TB], toward[:, (c % 2) * 128:(c % 2 + 1) * 128], dec[:, :],
                                 start=True, stop=True).then_inc(path_done.sem, 1)

            def steps(s, r):
                if s == "patch":
                    for j in range(NT):
                        pe.wait_ge(patch_norm.sem, patch_norm.at(r, j + 1))
                    for k in range(KP):
                        if k >= 2:
                            pe.wait_ge(patch_T.sem, patch_T.at(r, k - 1))
                        for j in range(NT):
                            last = nc.tensor.transpose(bank[k % 2][:, j * TT:(j + 1) * TT],
                                                       patch[:, j, k * 128:(k + 1) * 128], ident[0:TT, 0:TT])
                        last.then_inc(patch_turned.sem, 1)
                if s == "embed":
                    pe.wait_ge(patch_T.sem, patch_T.at(r, KP))
                    for m in range(DC):
                        project(bank[m][:, 0:TB], w_tok, wide, slice(m * 128, (m + 1) * 128), KP, emb)
                    pe.wait_ge(emb_T.sem, emb_T.at(r, 2))
                    turn_out(yTA, 0, emb_turned)
                if s == "normA":
                    pe.wait_ge(xA_ready.sem, xA_ready.at(r, NT))
                    turn_back(xA, 0, xA_turned)
                if s == "qk":
                    pe.wait_ge(xTA_ready.sem, xTA_ready.at(r, 2))
                    for c in range(2 * QC):
                        if c >= 2:
                            pe.wait_ge(qk_ready.sem, qk_ready.at(r, c - 1))
                        project(bank[c % 2][:, 0:TB], w_qkv, xTA, slice(c * 128, (c + 1) * 128), DC, qk_done)
                    pe.wait_ge(xsum_ready.sem, xsum_ready.at(r, 1))
                    for c in range(QC):
                        for k in range(DC):
                            last = nc.tensor.matmul(bank[2][:, c * IB:(c + 1) * IB],
                                                    w_qkv[:, k, 2 * INNER + c * 128:2 * INNER + (c + 1) * 128],
                                                    xsum[:, k, :], start=k == 0, stop=k == DC - 1)
                    last.then_inc(vsum_done.sem, 1)
                if s.startswith("pair") and s != "pairs1":
                    p = int(s[4:])
                    if p == 0:
                        pe.wait_ge(qk_ready.sem, qk_ready.at(r, 2 * QC))
                        pe.wait_ge(vbias_ready.sem, vbias_ready.at(r, 1))
                    tok = slice(p * PT, (p + 1) * PT)
                    for n in range(2):
                        for k in range(DC):
                            last = nc.tensor.matmul(bank[n][0:PT, :], xTA[:, k, tok],
                                                    w_qkv[:, k, 2 * INNER + 512 * n:2 * INNER + 512 * (n + 1)],
                                                    start=k == 0, stop=k == DC - 1)
                    last.then_inc(v_done.sem, 1)
                    wait_apart(pe, v_ready.sem, v_ready.at(r, 2 * p + 2), pe_passed)
                    for h in range(H):
                        row = slice(64 * (h % 2), 64 * (h % 2) + 64)
                        for m in range(2):
                            t = slice(p * PT + m * L, p * PT + (m + 1) * L)
                            last = nc.tensor.matmul(bank[h % 2][SLOT * m:SLOT * m + L, (h // 2) * L:(h // 2 + 1) * L],
                                                    qk[row, QC + h // 2, t], qk[row, h // 2, t], start=True, stop=True)
                    last.then_inc(sc_done.sem, 1)
                    pe.wait_ge(sc_ready.sem, sc_ready.at(r, 2 * p + 2))
                    for c in range(NG):
                        w = IG if c < NG - 1 else LAST
                        last = nc.tensor.transpose(bank[2][0:H * w, c * SP2:(c + 1) * SP2],
                                                   sc[:, c * IG:c * IG + w, :].rearrange("q i h -> q (i h)"),
                                                   ident[0:SP2, 0:SP2])
                    last.then_inc(sc_turned.sem, 1)
                    pe.wait_ge(sm_steps.sem, sm_steps.at(r, 5 * p + 5))
                    if p:
                        pe.wait_ge(av_ready.sem, av_ready.at(r, 2 * p))
                    for c in range(NG):
                        w = IG if c < NG - 1 else LAST
                        dst = bank[3][0:PT, c * 128:(c + 1) * 128] if c < NG - 1 else bank[4][0:PT, 0:H * w]
                        mat = mix8[0:H * w, 0:w, :].rearrange("p i g -> p (i g)")
                        last = nc.tensor.matmul(dst, prob[0:H * w, c, :], mat, start=True, stop=True)
                    last.then_inc(mixed.sem, 1)
                    pe.wait_ge(att_ready.sem, att_ready.at(r, 2 * p + 2))
                    for half in range(2):
                        if half:
                            pe.wait_ge(av_ready.sem, av_ready.at(r, 2 * p + 1))
                        for g in range(8 * half, 8 * half + 8):
                            at = 128 + (g // 2 - 4 * half) * PT
                            last = nc.tensor.matmul(bank[4][64 * (g % 2):64 * (g % 2) + 64, at:at + PT],
                                                    val[:, g * DH:(g + 1) * DH],
                                                    att[:, g, :, :].rearrange("q m i -> q (m i)"), start=True, stop=True)
                        last.then_inc(av_done.sem, 1)
                if s == "out0":
                    pe.wait_ge(av_ready.sem, av_ready.at(r, 2 * PAIRS))
                    for m in range(DC):
                        project(bank[m][:, 0:TB], w_out0, wide, slice(m * 128, (m + 1) * 128), QC, out0_done)
                    pe.wait_ge(out0_T.sem, out0_T.at(r, 2))
                    turn_out(yTA, 0, out0_turned)
                    pe.wait_ge(xB_ready.sem, xB_ready.at(r, NT))
                    turn_back(xB, 5, xB_turned)
                if s.startswith("tree"):
                    if s == "tree0":
                        pe.wait_ge(xTB_ready.sem, xTB_ready.at(r, 2))
                    for c in range(4 * int(s[4:]), 4 * int(s[4:]) + 4):
                        if c >= 2:
                            pe.wait_ge(z_half.sem, z_half.at(r, c - 1))
                        project(bank[5 + c % 2][:, 0:TB], w_tree, xTB, slice(c * 128, (c + 1) * 128), DC, z_done)
                        if c % 4:
                            path(r, c - 1)
                    path(r, c)
                if s == "leaf":
                    pe.wait_ge(leaf_ready.sem, leaf_ready.at(r, FC))
                    for m in range(DC):
                        project(bank[5 + m][:, 0:TB], w_leaf, big, slice(m * 128, (m + 1) * 128), FC, projB)
                    glueB(r, 0)
                if s == "qkv1":
                    pe.wait_ge(xTB_ready.sem, xTB_ready.at(r, 4))
                    for c in range(6):
                        if c == 2:
                            pe.wait_ge(q1_ready.sem, q1_ready.at(r, 1))
                        if c == 3:
                            pe.wait_ge(q1_ready.sem, q1_ready.at(r, 2))
                        if c >= 4:
                            pe.wait_ge(k1_ready.sem, k1_ready.at(r, 4 * (c - 3)))
                        project(bank[5 + c % 2][:, 0:TB], w_in1, xTB, slice(c * 128, (c + 1) * 128), DC, qkv1_done)
                if s == "pairs1":
                    wait_apart(pe, v1_ready.sem, v1_ready.at(r, 2), pe_passed)
                    for p in range(PAIRS):
                        if p:
                            wait_apart(pe, sm1_steps.sem, sm1_steps.at(r, 8 * (p - 1) + 4), pe_passed)
                        for h in range(H):
                            c, b, a = h // 8, (h // 4) % 2, h % 4
                            for m in range(2):
                                t = slice(p * PT + m * L, p * PT + (m + 1) * L)
                                last = nc.tensor.matmul(bank[5 + b][SLOT * m:SLOT * m + L, (4 * c + a) * L:(4 * c + a + 1) * L],
                                                        q1[64 * b:64 * b + 64, c, t], k4[64 * b:64 * b + 64, c, a, t],
                                                        start=True, stop=True)
                        last.then_inc(sc1_done.sem, 1)
                        pe.wait_ge(sm1_steps.sem, sm1_steps.at(r, 8 * p + 8))
                        if p:
                            pe.wait_ge(o1_ready.sem, o1_ready.at(r, p))
                        for c in range(DC):
                            last = nc.tensor.matmul(bank[7][:, c * PT:(c + 1) * PT],
                                                    r1[:, c * 8:(c + 1) * 8, :].rearrange("q h d -> q (h d)"),
                                                    C("pair", SP2), start=True, stop=True)
                        last.then_inc(r1_turned.sem, 1)
                if s == "out1":
                    pe.wait_ge(o1_ready.sem, o1_ready.at(r, PAIRS))
                    for m in range(DC):
                        project(bank[5 + m][:, 0:TB], w_out1, o1, slice(m * 128, (m + 1) * 128), DC, projB)
                    glueB(r, 1)
                if s == "shared":
                    pe.wait_ge(xTB_ready.sem, xTB_ready.at(r, 6))
                    for c in range(SC):
                        n = min(128, SH - 128 * c)
                        if c:
                            pe.wait_ge(sh_steps.sem, sh_steps.at(r, 3 * c))
                        project(bank[5][0:n, 0:TB], w_sh1, xTB, slice(c * 128, c * 128 + n), DC, sh_done)
                        project(bank[6][0:n, 0:TB], w_sh3, xTB, slice(c * 128, c * 128 + n), DC, sh_done)
                    for j in range(NT):
                        if j:
                            pe.wait_ge(rt_steps.sem, rt_steps.at(r, 14 * j))
                        for k in range(DC):
                            last = nc.tensor.matmul(bank[7][0:TT, 0:E_], xTB[:, k, j * TT:(j + 1) * TT], w_gate[:, k, :],
                                                    start=k == 0, stop=k == DC - 1)
                        last.then_inc(lg_done.sem, 1)
                        pe.wait_ge(rt_steps.sem, rt_steps.at(r, 14 * j + 9))
                        nc.tensor.matmul(bank[7][0:TT, 64:64 + E_], C("below", TT), both[:, :], start=True, stop=False)
                        nc.tensor.matmul(bank[7][0:TT, 64:64 + E_], C("ones", TT)[:, 0:TT], load[:, :],
                                         start=False, stop=True).then_inc(rank_done.sem, 1)
                    pe.wait_ge(sh_steps.sem, sh_steps.at(r, 3 * SC))
                    for m in range(DC):
                        project(bank[5 + m][:, 0:TB], w_sh2, up, slice(m * 128, (m + 1) * 128), SC, projB, rows=SH)
                    glueB(r, 2)

            rounds(pe, steps)

        @block.vector
        def _(dve):
            v = nc.vector

            n = [0]

            def step(ins):
                n[0] += 1
                ins.then_inc(made, 1)
                dve.wait_ge(made, n[0])

            step(v.memset(zero[:, :], 0.0))
            step(v.memset(load[:, :], 0.0))
            step(v.memset(sc[:, :, :], 0.0))
            for i in range(8):
                step(v.memset(bank[i][:, :], 0.0))
            dve.wait_ge(weights_in, WEIGHTS)
            for k in range(KP):
                step(v.tensor_scalar(w_tok[:, k, :], w_tok[:, k, :], g_ln1[:, k:k + 1], None, ALU.mult))
            step(v.tensor_reduce(wm[:, 0:1], wx[:, :], X, ALU.add, negate=True))
            step(v.tensor_scalar(wm[:, 1:2], wm[:, 0:1], 1.0 / H, None, ALU.mult))
            step(v.tensor_scalar(wx[:, :], wx[:, :], wm[:, 1:2], None, ALU.add))
            step(v.tensor_tensor(mix8[:, :, :], wx[:, :].unsqueeze(1).to_broadcast([128, IG, H]),
                                 C("query").unsqueeze(2).to_broadcast([128, IG, H]), ALU.mult))
            step(v.tensor_scalar(b_q1[:, :], b_in1[:, 0:2], 0.25, None, ALU.mult))
            step(v.tensor_copy(toward[:, :], toward32))
            assert n[0] == SETUP, n[0]

            def stats(src, st, mv, j, sig_, r, k):
                v.bn_stats(st, src).then_inc(sig_.sem, 1)
                wait_apart(dve, sig_.sem, sig_.at(r, k + 1), dve_passed)
                v.bn_aggr(mv[:, j, :], st).then_inc(sig_.sem, 1)

            def norm(dst, src, mv, rs, j, sig_):
                v.tensor_scalar(dst, src, mv[:, j, 0:1], rs[:, 1, j:j + 1], ALU.subtract, ALU.mult).then_inc(sig_.sem, 1)

            def glueB(r, g, source):
                base, turned, tk = source
                dve.wait_ge(turned.sem, turned.at(r, tk))
                for j in range(NT):
                    v.tensor_tensor(hB[:, j, :], bank[base + j // 2][0:TT, (j % 2) * D:(j % 2 + 1) * D],
                                    (hA if g == 0 else hB)[:, j, :], ALU.add).then_inc(hB_ready.sem, 1)
                if g == 3:
                    return
                for j in range(NT):
                    dve.wait_ge(hB_ready.sem, hB_ready.at(r, NT * g + j + 1))
                    stats(hB[:, j, :], stB[:, j, :], mvB, j, statsB, r, 2 * (NT * g + j))
                dve.wait_ge(statsB.sem, statsB.at(r, 2 * NT * (g + 1)))
                dve.wait_ge(rstdB.sem, rstdB.at(r, 2 * (g + 1)))
                for j in range(NT):
                    norm(xB[:, j, :], hB[:, j, :], mvB, rsB, j, xB_ready)

            def steps(s, r):
                if s == "patch":
                    dve.wait_ge(patch_in.sem, patch_in.at(r, 16))
                    for j in range(NT):
                        for e in range(2):
                            v.bn_stats(stA[:, j, 6 * e:6 * e + 6], patch[:, j, 384 * e:384 * e + 384]).then_inc(patch_stats.sem, 1)
                        wait_apart(dve, patch_stats.sem, patch_stats.at(r, 3 * j + 2), dve_passed)
                        v.bn_aggr(mvA[:, j, :], stA[:, j, :]).then_inc(patch_stats.sem, 1)
                    dve.wait_ge(patch_stats.sem, patch_stats.at(r, 3 * NT))
                    dve.wait_ge(patch_rstd.sem, patch_rstd.at(r, 2))
                    for j in range(NT):
                        norm(patch[:, j, :], patch[:, j, :], mvA, rsA, j, patch_norm)
                if s == "embed":
                    dve.wait_ge(emb_turned.sem, emb_turned.at(r, 1))
                    dve.wait_ge(patch_norm.sem, patch_norm.at(r, NT))
                    for j in range(NT):
                        src = bank[j // 2][0:TT, (j % 2) * D:(j % 2 + 1) * D]
                        stats(src, stA[:, j, 0:6], mvA, j, emb_stats, r, 2 * j)
                    dve.wait_ge(emb_stats.sem, emb_stats.at(r, 2 * NT))
                    dve.wait_ge(emb_rstd.sem, emb_rstd.at(r, 2))
                    pos = C("pos", TT).rearrange("p (j d) -> p j d", j=NT)
                    for j in range(NT):
                        norm(hA[:, j, :], bank[j // 2][0:TT, (j % 2) * D:(j % 2 + 1) * D], mvA, rsA, j, emb_steps)
                    for j in range(NT):
                        dve.wait_ge(emb_steps.sem, emb_steps.at(r, j + 1))
                        v.tensor_tensor(hA[:, j, :], hA[:, j, :], g_ln2[:, :], ALU.mult).then_inc(emb_steps.sem, 1)
                    for j in range(NT):
                        dve.wait_ge(emb_steps.sem, emb_steps.at(r, NT + j + 1))
                        v.tensor_tensor(hA[:, j, :], hA[:, j, :], pos[:, j, :], ALU.add).then_inc(emb_steps.sem, 1)
                if s == "normA":
                    for j in range(NT):
                        dve.wait_ge(emb_steps.sem, emb_steps.at(r, 2 * NT + j + 1))
                        stats(hA[:, j, :], stA[:, j, 0:6], mvA, j, statsA, r, 2 * j)
                    dve.wait_ge(statsA.sem, statsA.at(r, 2 * NT))
                    dve.wait_ge(rstdA.sem, rstdA.at(r, 2))
                    for j in range(NT):
                        norm(xA[:, j, :], hA[:, j, :], mvA, rsA, j, xA_ready)
                if s == "qk":
                    dve.wait_ge(xTA_ready.sem, xTA_ready.at(r, 2))
                    v.tensor_reduce(xsum[:, :, :], xTA[:, :, :].rearrange("p c (m l) -> p c m l", m=IB), X,
                                    ALU.add).then_inc(xsum_ready.sem, 1)
                    dve.wait_ge(vsum_done.sem, vsum_done.at(r, 1))
                    v.tensor_tensor(vbias[:, :, :], bank[2][:, 0:QC * IB].rearrange("p (c m) -> p c m", c=QC),
                                    b_head[:, :].unsqueeze(2).to_broadcast([128, QC, IB]), ALU.mult).then_inc(vbias_ready.sem, 1)
                if s.startswith("pair") and s != "pairs1":
                    p = int(s[4:])
                    dve.wait_ge(v_done.sem, v_done.at(r, p + 1))
                    for e in range(2):
                        v.tensor_tensor(val[:, 512 * e:512 * (e + 1)].rearrange("q (h d) -> q h d", h=8),
                                        bank[e][0:PT, :].rearrange("q (h d) -> q h d", h=8),
                                        g_head[:, 8 * e:8 * e + 8].unsqueeze(2).to_broadcast([PT, 8, DH]),
                                        ALU.mult).then_inc(v_ready.sem, 1)
                    dve.wait_ge(sc_turned.sem, sc_turned.at(r, p + 1))
                    full = bank[2][:, 0:NG * SP2].rearrange("q (c s) -> q c s", s=SP2)
                    pv = prob[:, :, :].rearrange("q c (m l) -> q c m l", m=2)
                    k = 5 * p
                    view = two_images(full)
                    v.tensor_reduce(pmax[:, 0], view, X, ALU.max).then_inc(sm_steps.sem, 1)
                    dve.wait_ge(sm_steps.sem, sm_steps.at(r, k + 1))
                    v.tensor_tensor(pv, view, pmax[:, 0].unsqueeze(3).to_broadcast([128, NG, 2, L]),
                                    ALU.subtract).then_inc(sm_steps.sem, 1)
                    dve.wait_ge(exp_done.sem, exp_done.at(r, p + 1))
                    v.tensor_reduce(pmax[:, 1], pv, X, ALU.add).then_inc(sm_steps.sem, 1)
                    dve.wait_ge(sm_steps.sem, sm_steps.at(r, k + 3))
                    v.reciprocal(pmax[:, 2], pmax[:, 1]).then_inc(sm_steps.sem, 1)
                    dve.wait_ge(sm_steps.sem, sm_steps.at(r, k + 4))
                    v.tensor_tensor(pv, pv, pmax[:, 2].unsqueeze(3).to_broadcast([128, NG, 2, L]),
                                    ALU.mult).then_inc(sm_steps.sem, 1)
                    dve.wait_ge(squared.sem, squared.at(r, 2 * p + 2))
                    v.tensor_reduce(var[:, 0, :], sq[:, :, :], X, ALU.add).then_inc(mixvar.sem, 1)
                    dve.wait_ge(mix_rstd.sem, mix_rstd.at(r, 3 * p + 3))
                    for part, (i0, i1) in enumerate(((0, 32), (32, L))):
                        n = i1 - i0
                        src = bank[3 + part][0:PT, 0:n * H].rearrange("q (i g) -> q g i", g=H)
                        v.tensor_tensor(att[:, :, :, i0:i1], src.unsqueeze(2).to_broadcast([PT, H, 2, n]),
                                        own[:, :, i0:i1].unsqueeze(1).to_broadcast([PT, H, 2, n]),
                                        ALU.mult).then_inc(att_ready.sem, 1)
                    for half in range(2):
                        dve.wait_ge(av_done.sem, av_done.at(r, 2 * p + half + 1))
                        bias = vbias[:, 4 * half:4 * half + 4, 2 * p:2 * p + 2].unsqueeze(3).to_broadcast([128, 4, 2, L])
                        v.tensor_tensor(wide[:, 4 * half:4 * half + 4, p * PT:(p + 1) * PT].rearrange("q c (m l) -> q c m l", m=2),
                                        bank[4][:, 128:128 + 4 * PT].rearrange("q (c m l) -> q c m l", c=4, m=2),
                                        bias, ALU.add).then_inc(av_ready.sem, 1)
                if s == "out0":
                    dve.wait_ge(spilled.sem, spilled.at(r, 0))
                    glueB(r, 0, (0, out0_turned, 1))
                if s.startswith("tree"):
                    for c in range(4 * int(s[4:]), 4 * int(s[4:]) + 4):
                        dve.wait_ge(z_done.sem, z_done.at(r, c + 1))
                        v.tensor_scalar(zb[:, c % 2, :], bank[5 + c % 2][:, 0:TB], b_tree[:, c:c + 1], 0.5,
                                        ALU.add, ALU.mult).then_inc(z_half.sem, 1)
                        if c % 2 == 0:
                            dve.wait_ge(z_half.sem, z_half.at(r, c + 1))
                            v.tensor_scalar(dec[:, :], zb[:, c % 2, :], 0.0, None, ALU.is_gt).then_inc(decided.sem, 1)
                        dve.wait_ge(z_half.sem, z_half.at(r, c + 1))
                        dve.wait_ge(z_tanh.sem, z_tanh.at(r, c + 1))
                        v.scalar_tensor_tensor(zb[:, c % 2, :], th[:, c % 2, :], 1.0, zb[:, c % 2, :],
                                               ALU.add, ALU.mult).then_inc(z_silu.sem, 1)
                        dve.wait_ge(z_silu.sem, z_silu.at(r, c + 1))
                        dve.wait_ge(path_done.sem, path_done.at(r, c + 1))
                        rights = C("right")[:, c % 2:c % 2 + 1]
                        v.scalar_tensor_tensor(big[:, c, :], bank[7][:, 0:TB], rights, zb[:, c % 2, :],
                                               ALU.is_equal, ALU.mult).then_inc(leaf_ready.sem, 1)
                if s == "leaf":
                    glueB(r, 1, (5, projB_turned, 1))
                if s == "qkv1":
                    for c in (2, 3):
                        dve.wait_ge(qkv1_done.sem, qkv1_done.at(r, c + 1))
                        for a in range(4):
                            v.tensor_scalar(k4[:, c - 2, a, :], bank[5 + c % 2][:, 0:TB], b_in1[:, c:c + 1],
                                            C("head4")[:, a:a + 1], ALU.add, ALU.mult).then_inc(k1_ready.sem, 1)
                if s == "pairs1":
                    for p in range(PAIRS):
                        dve.wait_ge(sc1_done.sem, sc1_done.at(r, p + 1))
                        k = 8 * p
                        for b in range(2):
                            src = bank[5 + b][0:SP2, 0:8 * L].rearrange("q (h l) -> q h l", l=L)
                            v.tensor_reduce(m1[:, 0, 8 * b:8 * b + 8], src, X, ALU.max).then_inc(sm1_steps.sem, 1)
                        dve.wait_ge(sm1_steps.sem, sm1_steps.at(r, k + 2))
                        for b in range(2):
                            src = bank[5 + b][0:SP2, 0:8 * L].rearrange("q (h l) -> q h l", l=L)
                            v.tensor_tensor(e1[:, 8 * b:8 * b + 8, :], src,
                                            m1[:, 0, 8 * b:8 * b + 8].unsqueeze(2).to_broadcast([SP2, 8, L]),
                                            ALU.subtract).then_inc(sm1_steps.sem, 1)
                        dve.wait_ge(exp1_done.sem, exp1_done.at(r, p + 1))
                        v.tensor_reduce(m1[:, 1, :], e1[:, :, :], X, ALU.add).then_inc(sm1_steps.sem, 1)
                        dve.wait_ge(sm1_steps.sem, sm1_steps.at(r, k + 5))
                        v.reciprocal(m1[:, 2, :], m1[:, 1, :]).then_inc(sm1_steps.sem, 1)
                        dve.wait_ge(sm1_steps.sem, sm1_steps.at(r, k + 6))
                        for b in range(2):
                            bb = slice(8 * b, 8 * b + 8)
                            dst = r1[:, :, :].rearrange("q (c b a) d -> q b c a d", c=2, b=2)[:, b]
                            v.tensor_tensor(dst, m1[:, 1, bb].rearrange("q (c a) -> q c a", c=2).unsqueeze(3).to_broadcast([SP2, 2, 4, 16]),
                                            m1[:, 2, bb].rearrange("q (c a) -> q c a", c=2).unsqueeze(3).to_broadcast([SP2, 2, 4, 16]),
                                            ALU.mult).then_inc(sm1_steps.sem, 1)
                        dve.wait_ge(r1_turned.sem, r1_turned.at(r, p + 1))
                        dve.wait_ge(v1_ready.sem, v1_ready.at(r, 2))
                        tok = slice(p * PT, (p + 1) * PT)
                        v.tensor_tensor(o1[:, :, tok], v1[:, :, tok], bank[7][:, 0:2 * PT].rearrange("q (c t) -> q c t", c=DC),
                                        ALU.mult).then_inc(o1_ready.sem, 1)
                if s == "out1":
                    glueB(r, 2, (5, projB_turned, 2))
                if s == "shared":
                    for c in range(SC):
                        nn = min(128, SH - 128 * c)
                        k = 3 * c
                        dve.wait_ge(sh_done.sem, sh_done.at(r, 2 * c + 1))
                        v.tensor_scalar(zb[0:nn, c % 2, :], bank[5][0:nn, 0:TB], b_sh1[0:nn, c:c + 1], 0.5,
                                        ALU.add, ALU.mult).then_inc(sh_steps.sem, 1)
                        dve.wait_ge(sh_steps.sem, sh_steps.at(r, k + 1))
                        dve.wait_ge(sh_tanh.sem, sh_tanh.at(r, c + 1))
                        v.scalar_tensor_tensor(zb[0:nn, c % 2, :], th[0:nn, c % 2, :], 1.0, zb[0:nn, c % 2, :],
                                               ALU.add, ALU.mult).then_inc(sh_steps.sem, 1)
                        dve.wait_ge(sh_steps.sem, sh_steps.at(r, k + 2))
                        dve.wait_ge(sh_done.sem, sh_done.at(r, 2 * c + 2))
                        v.scalar_tensor_tensor(up[0:nn, c, :], bank[6][0:nn, 0:TB], b_sh3[0:nn, c:c + 1], zb[0:nn, c % 2, :],
                                               ALU.add, ALU.mult).then_inc(sh_steps.sem, 1)
                    for j in range(NT):
                        route(r, j)
                    glueB(r, 3, (5, projB_turned, 3))

            def two_images(full):
                return bass.AP(full.tensor, full.offset, [list(full.ap[0]), list(full.ap[1]), [SLOT, 2], [1, L]])

            def route(r, j):
                k = 14 * j
                at = [0]

                def do(ins):
                    at[0] += 1
                    ins.then_inc(rt_steps.sem, 1)

                def own_wait():
                    dve.wait_ge(rt_steps.sem, rt_steps.at(r, k + at[0]))

                g = r * NT + j
                dve.wait_ge(lg_done.sem, lg_done.at(r, j + 1))
                do(v.tensor_tensor(lg[:, 0, :], bank[7][0:TT, 0:E_], b_gate[:, :], ALU.add))
                wait_apart(dve, rt_steps.sem, rt_steps.at(r, k + at[0]), dve_passed)
                do(v.max(top[:, :], lg[:, 0, :]))
                own_wait()
                do(v.tensor_scalar(lg[:, 1, :], lg[:, 0, :], top[:, 0:1], None, ALU.subtract))
                do(v.max_index(topi[:, :], top[:, :], lg[:, 0, :]))
                own_wait()
                do(v.tensor_copy(topf[:, :], topi[:, 0:2]))
                own_wait()
                for e in range(2):
                    do(v.tensor_scalar(oh[:, e, bass.ds(g, 1), :].rearrange("q a e -> q (a e)"), C("iota", TT), topf[:, e:e + 1], None, ALU.is_equal))
                dve.wait_ge(rt_exp.sem, rt_exp.at(r, j + 1))
                do(v.tensor_reduce(gsum[:, 0:1], lg[:, 1, :], X, ALU.add))
                own_wait()
                do(v.tensor_tensor(both[:, :], oh[:, 0, bass.ds(g, 1), :].rearrange("q a e -> q (a e)"),
                                   oh[:, 1, bass.ds(g, 1), :].rearrange("q a e -> q (a e)"), ALU.add))
                assert at[0] == 9
                do(v.reciprocal(gsum[:, 1:2], gsum[:, 0:1]))
                own_wait()
                do(v.tensor_tensor(rk[:, :, :], oh[:, :, bass.ds(g, 1), :].rearrange("q b a e -> q b (a e)"),
                                   lg[:, 1, :].unsqueeze(1).to_broadcast([TT, 2, E_]), ALU.mult))
                own_wait()
                do(v.tensor_reduce(gsum[:, 2:4], rk[:, :, :], X, ALU.add))
                own_wait()
                do(v.tensor_scalar(gate[:, bass.ds(g, 1), :].rearrange("q a b -> q (a b)"), gsum[:, 2:4], gsum[:, 1:2], None, ALU.mult))
                dve.wait_ge(rank_done.sem, rank_done.at(r, j + 1))
                do(v.tensor_tensor(rk[:, :, :], oh[:, :, bass.ds(g, 1), :].rearrange("q b a e -> q b (a e)"),
                                   bank[7][0:TT, 64:64 + E_].unsqueeze(1).to_broadcast([TT, 2, E_]), ALU.mult))
                own_wait()
                assert at[0] == 14
                v.tensor_reduce(rank[:, :, bass.ds(g, 1)].rearrange("q b a -> q (b a)"), rk[:, :, :], X,
                                ALU.add).then_inc(ranked.sem, 1)
                v.tensor_tensor(load[:, :], load[:, :], both[:, :], ALU.add).then_inc(ranked.sem, 1)
                dve.wait_ge(ranked.sem, ranked.at(r, 2 * j + 2))

            rounds(dve, steps)


def phase2(nc, dram, out_dram, bank, oh, gate, rank, load, const, C, spill_h, spill_x, slot_x, slot_y, semaphore):
    ctx = ExitStack()
    with ctx:
        def sb(name, shape, dt=F32):
            return ctx.enter_context(nc.sbuf_tensor(name, shape, dt))

        RING = 3
        WE = 4 * INTER + 2 * D + 2 * IC
        h = sb("h", [TT, GT, D])
        x = sb("x", [TT, GT, D])
        back = sb("back", [TT, 2 * GT, D])
        count = sb("count", [E_, 128], I32)
        padded = sb("padded", [E_, 128])
        off = sb("off", [TT, E_])
        prod = sb("prod", [TT, 2 * GT, E_])
        posf = sb("posf", [TT, 2, 2 * GT])
        pos = sb("pos", [TT, 2 * GT], I32)
        reach = sb("reach", [1, TILES, E_ - 1])
        owner = sb("owner", [1, TILES])
        owneri = sb("owneri", [1, TILES], I32)
        we = sb("we", [128, RING, WE])
        w2b = sb("w2b", [INTER - 2 * 128, RING, D])
        b2 = sb("b2", [128, RING, D])
        xg = sb("xg", [128, RING, D])
        xgT = sb("xgT", [128, RING, DC, 128])
        thx = sb("thx", [128, RING, IC, 128])
        zx = sb("zx", [128, RING, IC, 128])
        ax = sb("ax", [128, RING, IC, 128])
        yx = sb("yx", [128, RING, D])
        ident = C("ident")

        h_in = semaphore("h_in")
        x_in = semaphore("x_in")
        counted = semaphore("counted")
        placed = semaphore("placed")
        offsets = semaphore("offsets")
        scattered = semaphore("scattered")
        w_in = [semaphore(f"w_in{i}") for i in range(RING)]
        xg_in = [semaphore(f"xg_in{i}") for i in range(RING)]
        xg_turned = semaphore("xg_turned")
        xgT_ready = semaphore("xgT_ready")
        up_done = semaphore("up_done")
        half_done = semaphore("half_done")
        tanh_done = semaphore("tanh_done")
        silu_done = semaphore("silu_done")
        a_ready = semaphore("a_ready")
        y_done = semaphore("y_done")
        y_ready = semaphore("y_ready")
        y_out = [semaphore(f"y_out{i}") for i in range(RING)]
        gathered = [semaphore(f"gathered{i}") for i in range(GT // 4)]
        added = semaphore("added")
        stored = semaphore("stored")
        PLACED = 13

        def tiles(tile):
            def run(eng):
                for k in range(RING):
                    tile(0, k)
                with eng.Fori(1, TILES // RING - 1) as i:
                    for k in range(RING):
                        tile(i, k)
                for k in range(RING):
                    tile(TILES // RING - 1, k)
            return run

        def before(rnd, k):
            if k:
                return rnd, k - 1
            return None if isinstance(rnd, int) and rnd == 0 else (rnd - 1, RING - 1)

        def after(rnd, k):
            if k < RING - 1:
                return rnd, k + 1
            return None if isinstance(rnd, int) and rnd == TILES // RING - 1 else (rnd + 1, 0)

        turned = bank[0][:, 0:D]
        y_bank = bank[1][:, 0:D]
        w1 = [we[:, k, 0:2 * INTER].rearrange("p (c n) -> p c n", c=DC) for k in range(RING)]
        w3 = [we[:, k, 2 * INTER:4 * INTER].rearrange("p (c n) -> p c n", c=DC) for k in range(RING)]
        w2 = [we[:, k, 4 * INTER:4 * INTER + 2 * D].rearrange("p (c n) -> p c n", c=2) for k in range(RING)]
        bias = [we[:, k, 4 * INTER + 2 * D:WE] for k in range(RING)]

        block = ctx.enter_context(nc.Block())

        @block.sync
        def _(sp):
            sp.dma_start(x[:, :, :], spill_x.rearrange("(g p) d -> p g d", p=TT)).then_inc(x_in, 16)
            sp.dma_start(h[:, :, :], spill_h.rearrange("(g p) d -> p g d", p=TT)).then_inc(h_in, 16)
            sp.wait_ge(placed, PLACED)
            sp.wait_ge(scattered, 16 * 2 * GT)

            def tile(rnd, k):
                t = rnd * RING + k
                if not isinstance(rnd, int) or rnd:
                    sp.wait_ge(y_ready, t - RING + 1)
                e = sp.value_load(owneri[0:1, bass.ds(t, 1)], min_val=0, max_val=E_ - 1)
                sp.dma_start(xg[:, k, :], slot_x[bass.ds(t * 128, 128), :]).then_inc(xg_in[k], 16)
                sp.dma_start(we[:, k, :], dram["we"][bass.ds(e, 1), :, :].rearrange("a p n -> (a p) n")).then_inc(w_in[k], 16)
                sp.dma_start(w2b[:, k, :], dram["w2b"][bass.ds(e, 1), :, :].rearrange("a p n -> (a p) n")).then_inc(w_in[k], 16)
                sp.dma_start(b2[:, k, :], dram["b2"][bass.ds(e, 1), :].to_broadcast([128, D])).then_inc(w_in[k], 16)

            tiles(tile)(sp)
            for g in range(GT):
                sp.wait_ge(added, 2 * g + 2)
                sp.dma_start(out_dram[g * TT:(g + 1) * TT, :], h[:, g, :]).then_inc(stored, 16)
            sp.wait_ge(stored, 16 * GT)

        @block.gpsimd
        def _(pool):
            pool.wait_ge(x_in, 16)
            pool.wait_ge(placed, PLACED)
            for e in range(2):
                for g in range(GT):
                    nc.gpsimd.indirect_dma_start(
                        out=slot_x, out_offset=bass.IndirectOffsetOnAxis(ap=pos[:, e * GT + g:e * GT + g + 1], axis=0),
                        in_=x[:, g, :], in_offset=None).then_inc(scattered, 16)
            for k in range(RING):
                pool.wait_ge(y_out[k], 16 * (TILES // RING))
            for g in range(GT):
                for e in range(2):
                    nc.gpsimd.indirect_dma_start(
                        out=back[:, e * GT + g, :], out_offset=None, in_=slot_y,
                        in_offset=bass.IndirectOffsetOnAxis(ap=pos[:, e * GT + g:e * GT + g + 1], axis=0),
                    ).then_inc(gathered[g // 4], 16)

        @block.tensor
        def _(pe):
            nc.tensor.matmul(bank[0][0:E_, 0:128], load[:, :], C("ones", TT), start=True, stop=True).then_inc(counted, 1)
            pe.wait_ge(placed, 3)
            nc.tensor.matmul(bank[1][0:TT, 0:E_], padded[:, 0:TT], C("below16", E_), start=True, stop=True).then_inc(offsets, 1)
            pe.wait_ge(placed, PLACED)

            def turn(rnd, k):
                pe.wait_ge(xg_in[k], (rnd + 1) * 16)
                for m in range(DC):
                    last = nc.tensor.transpose(turned[:, m * 128:(m + 1) * 128], xg[:, k, m * 128:(m + 1) * 128], ident)
                last.then_inc(xg_turned, 1)

            def down(rnd, k):
                t = rnd * RING + k
                pe.wait_ge(a_ready, t * IC + IC)
                if not isinstance(rnd, int) or t:
                    pe.wait_ge(y_ready, t)
                for c in range(IC):
                    n = min(128, INTER - 128 * c)
                    last = nc.tensor.matmul(y_bank, ax[0:n, k, c, :], w2[k][:, c, :] if c < 2 else w2b[:, k, :],
                                            start=c == 0, stop=c == IC - 1)
                last.then_inc(y_done, 1)

            def tile(rnd, k):
                t = rnd * RING + k
                pe.wait_ge(xgT_ready, t + 1)
                pe.wait_ge(w_in[k], (rnd + 1) * 48)
                for e, w in enumerate((w1[k], w3[k])):
                    for c in range(IC):
                        n = min(128, INTER - 128 * c)
                        for m in range(DC):
                            last = nc.tensor.matmul(bank[2 + 2 * k + e][0:n, c * 128:(c + 1) * 128],
                                                    w[:, m, c * 128:c * 128 + n], xgT[:, k, m, :],
                                                    start=m == 0, stop=m == DC - 1)
                    last.then_inc(up_done, 1)
                if before(rnd, k):
                    down(*before(rnd, k))
                if after(rnd, k):
                    turn(*after(rnd, k))

            turn(0, 0)
            tiles(tile)(pe)
            down(TILES // RING - 1, RING - 1)

        @block.scalar
        def _(act):
            def rows(rnd, k):
                t = rnd * RING + k
                act.wait_ge(xg_turned, t + 1)
                nc.scalar.activation(xgT[:, k, :, :].rearrange("p c t -> p (c t)"), turned, ACT.Identity).then_inc(xgT_ready, 1)

            def store(rnd, k):
                t = rnd * RING + k
                act.wait_ge(y_ready, t + 1)
                act.dma_start(slot_y[bass.ds(t * 128, 128), :], yx[:, k, :]).then_inc(y_out[k], 16)

            def tile(rnd, k):
                t = rnd * RING + k
                act.wait_ge(half_done, t * IC + IC)
                nc.scalar.activation(thx[:, k, :, :], zx[:, k, :, :], ACT.Tanh).then_inc(tanh_done, 1)
                if after(rnd, k):
                    rows(*after(rnd, k))
                if before(rnd, k):
                    store(*before(rnd, k))

            rows(0, 0)
            tiles(tile)(act)
            store(TILES // RING - 1, RING - 1)

        @block.vector
        def _(dve):
            v = nc.vector
            n = [0]

            def step(ins):
                n[0] += 1
                ins.then_inc(placed, 1)
                dve.wait_ge(placed, n[0])

            dve.wait_ge(counted, 1)
            step(v.tensor_scalar(count[:, :], bank[0][0:E_, 0:128], 127.0, None, ALU.add))
            step(v.tensor_scalar(count[:, :], count[:, :], 7, 7, ALU.arith_shift_right, ALU.logical_shift_left))
            step(v.tensor_copy(padded[:, :], count[:, :]))
            dve.wait_ge(offsets, 1)
            step(v.tensor_copy(off[:, :], bank[1][0:TT, 0:E_]))
            step(v.tensor_tensor(prod[:, :, :], oh[:, :, :, :].rearrange("p b g e -> p (b g) e"),
                                 off[:, :].unsqueeze(1).to_broadcast([TT, 2 * GT, E_]), ALU.mult))
            step(v.tensor_reduce(posf[:, 0, :], prod[:, :, :], X, ALU.add))
            step(v.tensor_tensor(posf[:, 1, :], posf[:, 0, :], rank[:, :, :].rearrange("p b g -> p (b g)"), ALU.add))
            step(v.tensor_copy(pos[:, :], posf[:, 1, :]))
            step(v.tensor_tensor(reach[:, :, :], C("starts", 1).unsqueeze(2).to_broadcast([1, TILES, E_ - 1]),
                                 off[0:1, 1:E_].unsqueeze(1).to_broadcast([1, TILES, E_ - 1]), ALU.is_ge))
            step(v.tensor_reduce(owner[:, :], reach[:, :, :], X, ALU.add))
            step(v.tensor_copy(owneri[:, :], owner[:, :]))
            step(v.memset(zx[:, :, :, :], 0.0))
            step(v.memset(thx[:, :, :, :], 0.0))
            assert n[0] == PLACED

            def result(rnd, k):
                t = rnd * RING + k
                dve.wait_ge(y_done, t + 1)
                if not isinstance(rnd, int) or rnd:
                    dve.wait_ge(y_out[k], rnd * 16)
                v.tensor_tensor(yx[:, k, :], y_bank, b2[:, k, :], ALU.add).then_inc(y_ready, 1)

            def tile(rnd, k):
                t = rnd * RING + k
                dve.wait_ge(up_done, t * 2 + 1)
                for c in range(IC):
                    m = min(128, INTER - 128 * c)
                    v.tensor_scalar(zx[0:m, k, c, :], bank[2 + 2 * k][0:m, c * 128:(c + 1) * 128], bias[k][0:m, c:c + 1], 0.5,
                                    ALU.add, ALU.mult).then_inc(half_done, 1)
                if before(rnd, k):
                    result(*before(rnd, k))
                dve.wait_ge(tanh_done, t + 1)
                v.scalar_tensor_tensor(zx[:, k, :, :], thx[:, k, :, :], 1.0, zx[:, k, :, :], ALU.add, ALU.mult).then_inc(silu_done, 1)
                dve.wait_ge(silu_done, t + 1)
                dve.wait_ge(up_done, t * 2 + 2)
                for c in range(IC):
                    m = min(128, INTER - 128 * c)
                    v.scalar_tensor_tensor(ax[0:m, k, c, :], bank[3 + 2 * k][0:m, c * 128:(c + 1) * 128],
                                           bias[k][0:m, IC + c:IC + c + 1], zx[0:m, k, c, :], ALU.add, ALU.mult).then_inc(a_ready, 1)

            tiles(tile)(dve)
            result(TILES // RING - 1, RING - 1)
            dve.wait_ge(h_in, 16)
            for g in range(GT):
                if g % 4 == 0:
                    dve.wait_ge(gathered[g // 4], 16 * 8)
                for e in range(2):
                    if e:
                        dve.wait_ge(added, 2 * g + 1)
                    v.scalar_tensor_tensor(h[:, g, :], back[:, e * GT + g, :], gate[:, g, e:e + 1], h[:, g, :],
                                           ALU.mult, ALU.add).then_inc(added, 1)


def kernel(**inputs):
    import concourse.bacc as bacc
    from concourse.bass_utils import run_bass_kernel_spmd

    a = {k: np.asarray(v) for k, v in inputs.items()}

    def rows(w):
        return w.reshape(-1, 128, w.shape[1]).transpose(1, 0, 2)

    def column(b, chunks):
        out = np.zeros(chunks * 128, b.dtype)
        out[:b.size] = b
        return out.reshape(chunks, 128).T

    const, toward = constants()
    f = np.float32
    tree = np.zeros((TREES, NODES, D), f)
    tree[:, :NODES - 1] = a["L0_ffn_W_in"].reshape(TREES, NODES - 1, D)
    tree_b = np.zeros((TREES, NODES), f)
    tree_b[:, :NODES - 1] = a["L0_ffn_b_in"].reshape(TREES, NODES - 1)
    leaf = np.zeros((D, TREES, NODES), f)
    leaf[:, :, :NODES - 1] = a["L0_ffn_W_out"].reshape(D, TREES, NODES - 1)
    in1 = a["L1_attn_w_in"].reshape(H, 3, 16, D).transpose(1, 0, 2, 3).reshape(3 * D, D)
    in1_b = a["L1_attn_b_in"].reshape(H, 3, 16).transpose(1, 0, 2).reshape(3 * D)
    sh2 = np.zeros((SC * 128, D), f)
    sh2[:SH] = a["L1_ffn_sw2"]
    we = np.zeros((E_, 128, 4 * INTER + 2 * D + 2 * IC), f)
    for e in range(E_):
        we[e, :, 0:2 * INTER] = rows(a["L1_ffn_w1"][e]).reshape(128, -1)
        we[e, :, 2 * INTER:4 * INTER] = rows(a["L1_ffn_w3"][e]).reshape(128, -1)
        we[e, :, 4 * INTER:4 * INTER + 2 * D] = rows(a["L1_ffn_w2"][e, :256]).reshape(128, -1)
        we[e, :, -2 * IC:-IC] = column(a["L1_ffn_b1"][e], IC)
        we[e, :, -IC:] = column(a["L1_ffn_b3"][e], IC)
    arrays = {
        "const": const, "toward": toward,
        "patches": a["x"].reshape(B, 3, 6, 16, 6, 16).transpose(0, 2, 4, 1, 3, 5).reshape(NB, NT, TT, PD).transpose(0, 2, 1, 3).reshape(NB * TT, NT, PD),
        "w_tok": rows(a["L0_tok_W"].T), "g_ln1": column(a["L0_tok_ln1_w"], KP), "g_ln2": a["L0_tok_ln2_w"],
        "w_qkv": rows(a["L0_attn_w_qkv"]), "w_out0": rows(a["L0_attn_w_out"]), "b_out0": column(a["L0_attn_b_out"], DC),
        "g_head": a["L0_attn_ln_gamma"], "b_head": column(np.repeat(a["L0_attn_ln_beta"], DH), QC),
        "wx": np.tile(a["L0_attn_reattn_w"], (IG, 1)),
        "w_tree": rows(tree.reshape(-1, D).T), "b_tree": column(tree_b.reshape(-1), FC),
        "w_leaf": rows(leaf.reshape(D, -1).T),
        "w_in1": rows(in1.T), "b_in1": column(in1_b, 6), "w_out1": rows(a["L1_attn_w_out"].T), "b_out1": column(a["L1_attn_b_out"], DC),
        "w_sh1": rows(a["L1_ffn_sw1"]), "w_sh3": rows(a["L1_ffn_sw3"]), "w_sh2": rows(sh2),
        "b_sh1": column(a["L1_ffn_sb1"], SC), "b_sh3": column(a["L1_ffn_sb3"], SC), "b_sh2": column(a["L1_ffn_sb2"], DC),
        "w_gate": rows(a["L1_ffn_gate_w"]), "b_gate": a["L1_ffn_gate_b"],
        "we": we, "w2b": a["L1_ffn_w2"][:, 256:], "b2": a["L1_ffn_b2"],
    }
    nc = bacc.Bacc("TRN2", target_bir_lowering=False, num_devices=1)
    feed, dram = {}, {}
    for name, x in arrays.items():
        x = np.ascontiguousarray(x)
        feed[f"in_{name}"] = x
        dram[name] = nc.dram_tensor(f"in_{name}", x.shape, mybir.dt.from_np(x.dtype), kind="ExternalInput").ap()
    out = nc.dram_tensor("out", (T, D), F32, kind="ExternalOutput").ap()
    program(nc, dram, out)
    r = run_bass_kernel_spmd(nc, [feed], core_ids=[0])
    return r.results[0]["out"].reshape(B, L, D)
```

```python
from contextlib import ExitStack

import numpy as np

import concourse.bass as bass
from concourse import mybir

F32 = mybir.dt.float32
BF16 = mybir.dt.bfloat16
I32 = mybir.dt.int32
U32 = mybir.dt.uint32
ALU = mybir.AluOpType
ACT = mybir.ActivationFunctionType
X = mybir.AxisListType.X

B, L, D = 64, 36, 256
T = B * L
PD = 768
KP = PD // 128
IB = 8
NB = B // IB
TB = IB * L
TT = 96
NT = TB // TT
PAIRS = IB // 2
PT = 2 * L
SLOT = 64
SP2 = SLOT + L
DC = D // 128
H = 16
DH = 64
INNER = H * DH
QC = INNER // 128
IG = 8
NG = (L + IG - 1) // IG
LAST = L - (NG - 1) * IG
TREES, NODES = 8, 256
FC = TREES * 2
E_, INTER = 16, 352
SH = 704
SC = (SH + 127) // 128
IC = (INTER + 127) // 128
SLOTS = T * 2
TILES = (SLOTS + E_ * 127) // 128
GT = T // TT
SETUP = 27
LOOKED_UP = 2 * NT + 7
RT_STEPS = LOOKED_UP + 7


def layout(parts):
    at, out = 0, {}
    for name, width in parts:
        out[name] = (at, width)
        at += width
    return out, at


COLS, CW = layout([("ident", 128), ("ones", 128), ("pair", PT), ("own", 2), ("query", IG),
                   ("head4", 4), ("right", 2), ("below", TT), ("below16", E_), ("iota", E_),
                   ("half", 4), ("pos", NT * D), ("minushalf", L), ("starts", TILES)])


def constants():
    c = np.zeros((128, CW), np.float32)

    def put(name, a):
        at, w = COLS[name]
        c[:a.shape[0], at:at + w] = a

    r = np.arange(128)
    put("ident", np.eye(128))
    put("ones", np.ones((128, 128)))
    pair = np.zeros((128, PT))
    for m in range(2):
        pair[m * SLOT + np.arange(L), m * L + np.arange(L)] = 1
    put("pair", pair)
    put("own", np.stack([r < L, (r >= L) & (r < PT)], 1))
    put("query", r[:, None] // H == np.arange(IG))
    put("head4", (r[:, None] % 64) // 16 == np.arange(4))
    put("below", r[:, None] < np.arange(TT))
    put("below16", r[:, None] < np.arange(E_))
    put("iota", np.tile(np.arange(E_), (128, 1)))
    put("minushalf", np.full((128, L), -0.5))
    put("starts", np.tile(128 * np.arange(TILES), (128, 1)))
    toward = np.zeros((128, NODES), np.float32)
    rights = np.full((128, 2), 99.0)
    for node in range(NODES - 1):
        n, k = node, 0
        while n:
            up = (n - 1) // 2
            toward[up, node] = 1 if n == 2 * up + 2 else -1
            k += n == 2 * up + 2
            n = up
        rights[node % 128, node // 128] = k
    put("right", rights)
    w = np.float32(1) / np.float32(10000.0) ** (np.arange(D // 4, dtype=np.float32) / np.float32(D // 4 - 1))
    y, x = np.meshgrid(np.arange(6, dtype=np.float32), np.arange(6, dtype=np.float32), indexing="ij")
    y, x = y.reshape(-1)[:, None] * w, x.reshape(-1)[:, None] * w
    pos = np.concatenate([np.sin(x), np.cos(x), np.sin(y), np.cos(y)], 1)
    put("pos", np.tile(pos, (IB, 1)).reshape(NT, TT, D).transpose(1, 0, 2).reshape(TT, NT * D))
    return c, toward


def program(nc, dram, out_dram):
    ctx = ExitStack()
    with ctx:
        def sb(name, shape, dt=F32):
            return ctx.enter_context(nc.sbuf_tensor(name, shape, dt))

        def semaphore(name):
            return ctx.enter_context(nc.semaphore(name))

        spill_h = nc.dram_tensor("spill_h", [T, D], F32, kind="Internal").ap()
        spill_x = nc.dram_tensor("spill_x", [T, D], F32, kind="Internal").ap()
        slot_x = nc.dram_tensor("slot_x", [TILES * 128, D], F32, kind="Internal").ap()
        slot_y = nc.dram_tensor("slot_y", [TILES * 128, D], F32, kind="Internal").ap()

        bank = [ctx.enter_context(nc.psum_tensor(f"bank{i}", [128, 512], F32)) for i in range(8)]
        oh = sb("oh", [TT, 2, GT, E_])
        gate = sb("gate", [TT, 2, GT])
        rank = sb("rank", [TT, 2, GT])
        load = sb("load", [TT, E_])
        const = sb("const", [128, CW])

        def C(name, parts=128):
            at, w = COLS[name]
            return const[0:parts, at:at + w]

        phase1(nc, dram, bank, oh, gate, rank, load, const, C, spill_h, spill_x, slot_x, semaphore)
        phase2(nc, dram, out_dram, bank, oh, gate, rank, load, const, C, spill_h, spill_x, slot_x, slot_y, semaphore)


def wait_apart(eng, sem, value, passed):
    eng.wait_ge(sem, value)
    eng.sem_inc(passed, 1)


class Signal:

    def __init__(self, sem, per, start=0):
        self.sem, self.per, self.start = sem, per, start

    def at(self, rnd, k):
        return rnd * self.per + (self.start + k)


def phase1(nc, dram, bank, oh, gate, rank, load, const, C, spill_h, spill_x, slot_x, semaphore):
    ctx = ExitStack()
    with ctx:
        def sb(name, shape, dt=F32):
            return ctx.enter_context(nc.sbuf_tensor(name, shape, dt))

        def sig(name, per=1, start=0):
            return Signal(semaphore(name), per, start)

        w_tok = sb("w_tok", [128, KP, D])
        w_qkv = sb("w_qkv", [128, DC, 3 * INNER])
        w_out0 = sb("w_out0", [128, QC, D])
        w_tree = sb("w_tree", [128, DC, TREES * NODES])
        w_leaf = sb("w_leaf", [128, FC, D])
        w_in1 = sb("w_in1", [128, DC, 3 * D])
        w_out1 = sb("w_out1", [128, DC, D])
        w_sh1 = sb("w_sh1", [128, DC, SH])
        w_sh3 = sb("w_sh3", [128, DC, SH])
        w_sh2 = sb("w_sh2", [128, SC, D])
        w_gate = sb("w_gate", [128, DC, E_])
        b_gate = sb("b_gate", [TT, E_])
        g_ln1 = sb("g_ln1", [128, KP])
        g_ln2 = sb("g_ln2", [TT, D])
        g_head = sb("g_head", [PT, H])
        b_head = sb("b_head", [128, QC])
        b_out0 = sb("b_out0", [128, DC])
        b_tree = sb("b_tree", [128, FC])
        b_tree2 = sb("b_tree2", [128, FC])
        b_in1 = sb("b_in1", [128, 6])
        b_k1 = sb("b_k1", [128, DC, 4])
        b_q1 = sb("b_q1", [128, DC])
        b_out1 = sb("b_out1", [128, DC])
        b_sh1 = sb("b_sh1", [128, SC])
        b_sh12 = sb("b_sh12", [128, SC])
        b_sh3 = sb("b_sh3", [128, SC])
        b_sh2 = sb("b_sh2", [128, DC])
        toward = sb("toward", [128, NODES], BF16)
        wx = sb("wx", [128, H])
        wm = sb("wm", [128, 2])
        mix8 = sb("mix8", [128, IG, H])
        patch = sb("patch", [TT, NT, PD])
        stA = sb("stA", [TT, NT, 12])
        mvA = sb("mvA", [TT, NT, 2])
        rsA = sb("rsA", [TT, 2, NT])
        wide = sb("wide", [128, 8, TB])
        mix = patch[0:PT, :, :].rearrange("q j d -> q (j d)")[:, 0:2 * L * H].rearrange("q (b n) -> q b n", b=2)
        hA = sb("hA", [TT, NT, D])
        hM = sb("hM", [TT, NT, D])
        xA = sb("xA", [TT, NT, D])
        xTA = sb("xTA", [128, DC, TB])
        qk = sb("qk", [128, 2 * QC, TB])
        xsum = sb("xsum", [128, DC, IB])
        vbias = sb("vbias", [128, QC, IB])
        val = sb("val", [PT, INNER])
        sc = sb("sc", [SP2, L, H])
        prob = sb("prob", [128, NG, PT])
        pmax = sb("pmax", [128, 3, NG, 2])
        sq = xA[0:PT, :, :].rearrange("q j d -> q (j d)")[:, 0:L * H].rearrange("q (i h) -> q i h", i=L)
        var = sb("var", [PT, 3, L])
        own = sb("own", [PT, 2, L])
        mixed_in = sb("mixed_in", [128, H * PT])
        att = mixed_in[0:PT, :].rearrange("q (g m i) -> q g m i", g=H, m=2)
        yTA = mixed_in[:, 0:DC * TB].rearrange("p (c t) -> p c t", c=DC)
        stB = sb("stB", [TT, NT, 6])
        stH = sb("stH", [TT, NT, 6])
        mvH = sb("mvH", [TT, NT, 2])
        rsH = sb("rsH", [TT, 2, NT])
        mvB = sb("mvB", [TT, NT, 2])
        rsB = sb("rsB", [TT, 2, NT])
        hB = sb("hB", [TT, NT, D])
        xB = sb("xB", [TT, NT, D])
        xTB = sb("xTB", [128, DC, TB])
        th = sb("th", [128, 2, TB])
        zb = sb("zb", [128, 2, TB])
        toward32 = th[:, :, :].rearrange("p a t -> p (a t)")[:, 0:NODES]
        dec = sb("dec", [128, TB], BF16)
        big = sb("big", [128, 20, TB])
        k4 = big[:, 0:8, :].rearrange("p (c a) t -> p c a t", c=DC)
        q1 = big[:, 8:10, :]
        v1 = big[:, 10:12, :]
        o1 = big[:, 12:14, :]
        up = big[:, 14:20, :]
        hout = big[0:TT, 8:11, :].rearrange("p a t -> p (a t)")[:, 0:NT * D].rearrange("p (j d) -> p j d", j=NT)
        soft = sb("soft", [128, H * L])
        e1 = soft[0:SP2, :].rearrange("q (h l) -> q h l", h=H)
        yTB = soft[:, :].rearrange("p (c t) -> p c t", c=DC)
        m1 = sb("m1", [SP2, 3, H])
        r1 = sb("r1", [SP2, H, 16])
        lg = sb("lg", [TT, NT, E_])
        ex = sb("ex", [TT, NT, E_])
        top = sb("top", [TT, NT, 8])
        topi = sb("topi", [TT, NT, 8], U32)
        topf = sb("topf", [TT, NT, 2])
        gsum = sb("gsum", [TT, 4, NT])
        both = sb("both", [TT, NT, E_])
        pick = r1[0:TT, :, :].rearrange("q h d -> q (h d)")[:, 0:2 * NT * E_].rearrange("q (b j e) -> q b j e", b=2, j=NT)
        zero = up[:, SC - 1, 0:D]

        weights_in = semaphore("weights_in")
        pe_passed = semaphore("pe_passed")
        dve_passed = semaphore("dve_passed")
        pool_passed = semaphore("pool_passed")
        made = semaphore("made")
        patch_in = sig("patch_in", 16)
        patch_stats = sig("patch_stats", 3 * NT)
        patch_rstd = sig("patch_rstd", 2)
        patch_norm = sig("patch_norm", NT)
        patch_turned = sig("patch_turned", KP)
        patch_T = sig("patch_T", KP)
        emb = sig("emb", 2)
        emb_T = sig("emb_T", 2)
        emb_turned = sig("emb_turned", 1)
        emb_stats = sig("emb_stats", 2 * NT)
        emb_rstd = sig("emb_rstd", 2)
        emb_steps = sig("emb_steps", 2 * NT)
        statsA = sig("statsA", 2 * NT)
        rstdA = sig("rstdA", 2)
        xA_ready = sig("xA_ready", NT)
        xH_ready = sig("xH_ready", NT)
        xA_turned = sig("xA_turned", 1)
        xTA_ready = sig("xTA_ready", 2)
        qk_done = sig("qk_done", 2 * QC)
        qk_ready = sig("qk_ready", 2 * QC)
        xsum_ready = sig("xsum_ready", 1)
        vsum_done = sig("vsum_done", 1)
        vbias_ready = sig("vbias_ready", 1)
        v_done = sig("v_done", 2 * PAIRS)
        v_ready = sig("v_ready", 2 * PAIRS)
        sc_done = sig("sc_done", PAIRS)
        sc_ready = sig("sc_ready", 2 * PAIRS)
        sc_turned = sig("sc_turned", PAIRS)
        sm_steps = sig("sm_steps", 5 * PAIRS)
        exp_done = sig("exp_done", PAIRS)
        mixed = sig("mixed", PAIRS)
        mix_copied = sig("mix_copied", 2 * PAIRS)
        squared = sig("squared", PAIRS)
        mixvar = sig("mixvar", PAIRS)
        mix_rstd = sig("mix_rstd", 3 * PAIRS)
        att_ready = sig("att_ready", 2 * PAIRS)
        av_done = sig("av_done", 2 * PAIRS)
        av_ready = sig("av_ready", 2 * PAIRS)
        out0_done = sig("out0_done", 2)
        out0_T = sig("out0_T", 2)
        out0_turned = sig("out0_turned", 1)
        hM_ready = sig("hM_ready", NT)
        statsH = sig("statsH", 2 * NT)
        rstdH = sig("rstdH", 2)
        hB_ready = sig("hB_ready", 3 * NT, 1)
        statsB = sig("statsB", 2 * 2 * NT)
        rstdB = sig("rstdB", 2 * 2)
        xB_ready = sig("xB_ready", 2 * NT)
        xB_turned = sig("xB_turned", 3)
        xTB_ready = sig("xTB_ready", 2 * 3)
        projB = sig("projB", 2 * 3)
        projB_T = sig("projB_T", 2 * 3)
        projB_turned = sig("projB_turned", 3)
        z_done = sig("z_done", FC)
        z_tanh = sig("z_tanh", FC)
        z_half = sig("z_half", FC)
        z_silu = sig("z_silu", FC)
        decided = sig("decided", TREES)
        path_done = sig("path_done", FC)
        leaf_ready = sig("leaf_ready", FC)
        qkv1_done = sig("qkv1_done", 6)
        q1_ready = sig("q1_ready", 2)
        k1_ready = sig("k1_ready", 8)
        v1_ready = sig("v1_ready", 2)
        sc1_done = sig("sc1_done", PAIRS)
        sm1_steps = sig("sm1_steps", 8 * PAIRS)
        exp1_done = sig("exp1_done", PAIRS)
        r1_turned = sig("r1_turned", PAIRS)
        o1_ready = sig("o1_ready", PAIRS)
        sh_done = sig("sh_done", 2 * SC)
        sh_tanh = sig("sh_tanh", SC)
        sh_half = sig("sh_half", SC)
        sh_silu = sig("sh_silu", SC)
        sh_up = sig("sh_up", SC)
        lg_done = sig("lg_done", 1)
        rt_steps = sig("rt_steps", RT_STEPS)
        rt_exp = sig("rt_exp", 1)
        rank_done = sig("rank_done", 1)
        spilled_h = sig("spilled_h", 16, 16)
        spilled_x = sig("spilled_x", 16, 16)
        zeroed = semaphore("zeroed")
        ranked = sig("ranked", 4 + NT)

        loads = [
            (const[:, :], dram["const"]), (w_tok[:, :, :], dram["w_tok"]), (w_qkv[:, :, :], dram["w_qkv"]),
            (w_out0[:, :, :], dram["w_out0"]), (w_tree[:, :, :], dram["w_tree"]), (w_leaf[:, :, :], dram["w_leaf"]),
            (w_in1[:, :, :], dram["w_in1"]), (w_out1[:, :, :], dram["w_out1"]), (w_sh1[:, :, :], dram["w_sh1"]),
            (w_sh3[:, :, :], dram["w_sh3"]), (w_sh2[:, :, :], dram["w_sh2"]), (w_gate[:, :, :], dram["w_gate"]),
            (b_gate[:, :], dram["b_gate"].partition_broadcast(TT)), (g_ln1[:, :], dram["g_ln1"]),
            (g_ln2[:, :], dram["g_ln2"].partition_broadcast(TT)),
            (g_head[:, :], dram["g_head"].partition_broadcast(PT)), (b_out0[:, :], dram["b_out0"]),
            (b_tree[:, :], dram["b_tree"]), (b_in1[:, :], dram["b_in1"]), (b_out1[:, :], dram["b_out1"]),
            (b_sh1[:, :], dram["b_sh1"]), (b_sh3[:, :], dram["b_sh3"]), (b_sh2[:, :], dram["b_sh2"]),
            (toward32, dram["toward"]), (b_head[:, :], dram["b_head"]),
            (wx[:, :], dram["wx"]),
        ]
        WEIGHTS = 16 * len(loads)
        ident = C("ident")
        START = """load patch patchM turnp embed turne ln2 ln3 ln4 xA qk0 qk1 qk2 qk3 qk4 qk5 qk6 qk7 vsum""".split()
        ATTEND = """S0 T0 V0 U0 M0 R0 S1 T1 N0 U1 W0 M1 R1 V1 S2 T2 N1 U2 W1 M2 R2 V2 S3 T3 N2 U3 W2 M3 R3 V3 N3 W3
            outP outT outN""".split()
        HAND_OVER = ["outM", "outX"]
        FINISH = ([f"z{c}" for c in range(FC + 1)] + """leafP0 leafP1 leafT leafN leafM leafX q1a q1b q1c s1_0 r1_0 p1_0
            s1_1 r1_1 p1_1 s1_2 r1_2 p1_2 s1_3 r1_3 p1_3 o1P o1T o1N o1M o1X sh0 lg sh1 lh sh2 sh3 rk sh4 sh5
            shP shT shN""".split())
        MIXED = """S0 z0 T0 z1 V0 U0 z2 M0 z3 R0 S1 z4 T1 z5 N0 z6 U1 W0 M1 z7 R1 V1 z8 S2 z9 T2 z10 N1 U2 W1 M2 z11 R2
            V2 z12 S3 z13 T3 z14 N2 U3 W2 M3 z15 R3 V3 z16 leafP0 N3 load W3 leafP1 leafT outP leafN patch leafM patchM
            outT outN turnp leafX embed q1a turne q1b ln2 q1c ln3 s1_0 ln4 r1_0 p1_0 s1_1 xA r1_1 qk0 p1_1 s1_2 qk1 qk2
            r1_2 p1_2 s1_3 qk3 qk4 r1_3 p1_3 o1P qk5 o1T o1N qk6 o1M qk7 o1X outM sh0 vsum lg sh1 lh sh2 sh3
            rk sh4 sh5 outX shP shT shN""".split()
        for part in START, ATTEND + HAND_OVER, FINISH:
            assert [s for s in MIXED if s in part] == part

        def rounds(eng, steps):
            def full_round(r):
                for s in MIXED:
                    steps(s, r + 1 if s in START else r - 1 if s in FINISH else r)

            for s in START:
                steps(s, 0)
            for s in ATTEND:
                steps(s, 0)
            for s in START:
                steps(s, 1)
            for s in HAND_OVER:
                steps(s, 0)
            with eng.Fori(1, NB - 1) as i:
                full_round(i)
            for s in MIXED:
                if s not in START:
                    steps(s, NB - 2 if s in FINISH else NB - 1)
            for s in FINISH:
                steps(s, NB - 1)

        block = ctx.enter_context(nc.Block())

        @block.sync
        def _(sp):
            sp.sem_inc(hB_ready.sem, 1)
            sp.sem_inc(spilled_h.sem, 16)
            sp.sem_inc(spilled_x.sem, 16)
            for dst, src in loads:
                sp.dma_start(dst, src).then_inc(weights_in, 16)
            sp.wait_ge(made, 1)
            for t in range(TILES):
                sp.dma_start(slot_x[t * 128:(t + 1) * 128, :], zero).then_inc(zeroed, 16)

            def steps(s, r):
                if s == "load":
                    if not isinstance(r, int) or r:
                        sp.wait_ge(patch_turned.sem, patch_turned.at(r - 1, KP))
                        sp.wait_ge(att_ready.sem, att_ready.at(r - 1, 2 * PAIRS))
                    sp.dma_start(patch[:, :, :], dram["patches"][bass.ds(r * TT, TT), :, :]).then_inc(patch_in.sem, 16)
                if s == "o1X":
                    sp.wait_ge(xB_ready.sem, xB_ready.at(r, 2 * NT))
                    sp.dma_start(spill_x[bass.ds(r * TB, TB), :].rearrange("(j p) d -> p j d", p=TT),
                                 xB[:, :, :]).then_inc(spilled_x.sem, 16)
                if s == "shN":
                    sp.wait_ge(hB_ready.sem, hB_ready.at(r, 3 * NT))
                    sp.dma_start(spill_h[bass.ds(r * TB, TB), :].rearrange("(j p) d -> p j d", p=TT),
                                 hout).then_inc(spilled_h.sem, 16)

            rounds(sp, steps)
            sp.wait_ge(spilled_h.sem, spilled_h.at(NB, 0))
            sp.wait_ge(spilled_x.sem, spilled_x.at(NB, 0))
            sp.wait_ge(zeroed, 16 * TILES)

        @block.gpsimd
        def _(pool):
            minus = C("minushalf")

            def inverse_root(out, mid, var_ap, done, r, k, eps):
                nc.gpsimd.tensor_scalar(mid, var_ap, 1.0, eps, ALU.mult, ALU.add).then_inc(done.sem, 1)
                pool.wait_ge(done.sem, done.at(r, k + 1))
                n = mid.shape[-1]
                nc.gpsimd.tensor_tensor(out, mid, minus[0:mid.shape[0], 0:n], ALU.pow).then_inc(done.sem, 1)

            pool.wait_ge(weights_in, WEIGHTS)

            def steps(s, r):
                if s == "patch":
                    wait_apart(pool, patch_stats.sem, patch_stats.at(r, 3 * NT), pool_passed)
                    inverse_root(rsA[:, 1, :], rsA[:, 0, :], mvA[:, :, 1], patch_rstd, r, 0, 1e-5)
                if s == "ln2":
                    wait_apart(pool, emb_stats.sem, emb_stats.at(r, 2 * NT), pool_passed)
                    inverse_root(rsA[:, 1, :], rsA[:, 0, :], mvA[:, :, 1], emb_rstd, r, 0, 1e-5)
                if s == "ln3":
                    wait_apart(pool, statsA.sem, statsA.at(r, 2 * NT), pool_passed)
                    inverse_root(rsA[:, 1, :], rsA[:, 0, :], mvA[:, :, 1], rstdA, r, 0, 1e-5)
                if s[0] == "M":
                    p = int(s[1:])
                    wait_apart(pool, mixvar.sem, mixvar.at(r, p + 1), pool_passed)
                    nc.gpsimd.tensor_scalar(var[:, 1, :], var[:, 0, :], 1.0 / H, 1e-3,
                                            ALU.mult, ALU.add).then_inc(mix_rstd.sem, 1)
                    pool.wait_ge(mix_rstd.sem, mix_rstd.at(r, 3 * p + 1))
                    nc.gpsimd.tensor_tensor(var[:, 2, :], var[:, 1, :], minus[0:PT, 0:L], ALU.pow).then_inc(mix_rstd.sem, 1)
                    pool.wait_ge(mix_rstd.sem, mix_rstd.at(r, 3 * p + 2))
                    if p:
                        pool.wait_ge(att_ready.sem, att_ready.at(r, 2 * p))
                    nc.gpsimd.tensor_tensor(own[:, :, :], var[:, 2, :].unsqueeze(1).to_broadcast([PT, 2, L]),
                                            C("own", PT).unsqueeze(2).to_broadcast([PT, 2, L]),
                                            ALU.mult).then_inc(mix_rstd.sem, 1)
                for g, name in enumerate(["outN", "leafN", "o1N"]):
                    if s == name:
                        st, rs, mv, done, k = (statsH, rsH, mvH, rstdH, 0) if g == 0 else (statsB, rsB, mvB, rstdB, g - 1)
                        wait_apart(pool, st.sem, st.at(r, 2 * NT * (k + 1)), pool_passed)
                        inverse_root(rs[:, 1, :], rs[:, 0, :], mv[:, :, 1], done, r, 2 * k, 1e-5)

            rounds(pool, steps)

        @block.scalar
        def _(act):
            def copy(dst, src, sem, **kw):
                nc.scalar.activation(dst, src, ACT.Identity, **kw).then_inc(sem.sem, 1)

            act.wait_ge(weights_in, WEIGHTS)
            act.wait_ge(made, SETUP)

            def turn_in(xT, turned, ready, r, k, base=0):
                act.wait_ge(turned.sem, turned.at(r, k + 1))
                for m in range(DC):
                    copy(xT[:, m, :], bank[base + m][:, 0:TB], ready)

            def glueB(r, g, bias):
                for m in range(DC):
                    act.wait_ge(projB.sem, projB.at(r, 2 * g + m + 1))
                    if bias is None:
                        copy(yTB[:, m, :], bank[5 + m][:, 0:TB], projB_T)
                    else:
                        copy(yTB[:, m, :], bank[5 + m][:, 0:TB], projB_T, bias=bias[:, m:m + 1])

            def steps(s, r):
                if s == "turnp":
                    for k in range(KP):
                        act.wait_ge(patch_turned.sem, patch_turned.at(r, k + 1))
                        copy(wide[:, k, :], bank[k % 2][:, 0:TB], patch_T)
                if s == "embed":
                    for m in range(DC):
                        act.wait_ge(emb.sem, emb.at(r, m + 1))
                        copy(yTA[:, m, :], bank[m][:, 0:TB], emb_T)
                if s == "xA":
                    turn_in(xTA, xA_turned, xTA_ready, r, 0)
                if s[:2] == "qk":
                    for c in range(2 * int(s[2:]), 2 * int(s[2:]) + 2):
                        act.wait_ge(qk_done.sem, qk_done.at(r, c + 1))
                        copy(qk[:, c, :], bank[c % 2][:, 0:TB], qk_ready, scale=DH ** -0.5 if c < QC else 1.0)
                if s[0] == "S":
                    p = int(s[1:])
                    act.wait_ge(sc_done.sem, sc_done.at(r, p + 1))
                    sv = sc[:, :, :].rearrange("q l (a e) -> q e a l", e=2)
                    for e in range(2):
                        copy(sv[:, e], bank[e][0:SP2, 0:8 * L].rearrange("q (a l) -> q a l", l=L), sc_ready)
                if s[0] == "T":
                    p = int(s[1:])
                    act.wait_ge(sm_steps.sem, sm_steps.at(r, 5 * p + 2))
                    nc.scalar.activation(prob[:, :, :], prob[:, :, :], ACT.Exp).then_inc(exp_done.sem, 1)
                if s[0] == "M":
                    p = int(s[1:])
                    act.wait_ge(mixed.sem, mixed.at(r, p + 1))
                    if p >= 2:
                        act.wait_ge(att_ready.sem, att_ready.at(r, 2 * (p - 1)))
                    for part, (i0, i1) in enumerate(((0, 32), (32, L))):
                        copy(mix[:, p % 2, i0 * H:i1 * H], bank[3 + part][0:PT, 0:(i1 - i0) * H], mix_copied)
                    act.wait_ge(mix_copied.sem, mix_copied.at(r, 2 * p + 2))
                    if p:
                        act.wait_ge(mixvar.sem, mixvar.at(r, p))
                    nc.scalar.activation(sq[:, :, :].rearrange("q i g -> q (i g)"), mix[:, p % 2, :],
                                         ACT.Square).then_inc(squared.sem, 1)
                if s == "outP":
                    for m in range(DC):
                        act.wait_ge(out0_done.sem, out0_done.at(r, m + 1))
                        copy(yTA[:, m, :], bank[m][:, 0:TB], out0_T, bias=b_out0[:, m:m + 1])
                if s == "outX":
                    turn_in(xTB, xB_turned, xTB_ready, r, 0)
                if s[0] == "z" and s != f"z{FC}":
                    c = int(s[1:])
                    act.wait_ge(z_done.sem, z_done.at(r, c + 1))
                    if c >= 2:
                        act.wait_ge(leaf_ready.sem, leaf_ready.at(r, c - 1))
                    copy(zb[:, c % 2, :], bank[5 + c % 2][:, 0:TB], z_half, scale=0.5, bias=b_tree2[:, c:c + 1])
                    act.wait_ge(z_half.sem, z_half.at(r, c + 1))
                    nc.scalar.activation(th[:, c % 2, :], zb[:, c % 2, :], ACT.Tanh).then_inc(z_tanh.sem, 1)
                if s == "leafP1":
                    glueB(r, 0, None)
                if s == "leafX":
                    turn_in(xTB, xB_turned, xTB_ready, r, 1, 5)
                if s == "q1a":
                    for c in (0, 1):
                        act.wait_ge(qkv1_done.sem, qkv1_done.at(r, c + 1))
                        copy(q1[:, c, :], bank[5 + c % 2][:, 0:TB], q1_ready, scale=0.25, bias=b_q1[:, c:c + 1])
                if s == "q1b":
                    for c in (2, 3):
                        act.wait_ge(qkv1_done.sem, qkv1_done.at(r, c + 1))
                        for a in range(4):
                            copy(k4[:, c - 2, a, :], bank[5 + c % 2][:, 0:TB], k1_ready, scale=C("head4")[:, a:a + 1],
                                 bias=b_k1[:, c - 2, a:a + 1])
                if s == "q1c":
                    for c in (4, 5):
                        act.wait_ge(qkv1_done.sem, qkv1_done.at(r, c + 1))
                        copy(v1[:, c - 4, :], bank[5 + c % 2][:, 0:TB], v1_ready, bias=b_in1[:, c:c + 1])
                if s[:2] == "s1":
                    p = int(s[3:])
                    act.wait_ge(sm1_steps.sem, sm1_steps.at(r, 8 * p + 4))
                    nc.scalar.activation(e1, e1, ACT.Exp).then_inc(exp1_done.sem, 1)
                if s == "o1P":
                    glueB(r, 1, b_out1)
                if s == "o1X":
                    turn_in(xTB, xB_turned, xTB_ready, r, 2, 5)
                if s[:2] == "sh" and s[2:].isdigit():
                    c = int(s[2:])
                    n = min(128, SH - 128 * c)
                    act.wait_ge(sh_done.sem, sh_done.at(r, 2 * c + 1))
                    if c >= 2:
                        act.wait_ge(sh_up.sem, sh_up.at(r, c - 1))
                    else:
                        act.wait_ge(leaf_ready.sem, leaf_ready.at(r, FC))
                    copy(zb[0:n, c % 2, :], bank[5][0:n, 0:TB], sh_half, scale=0.5, bias=b_sh12[0:n, c:c + 1])
                    act.wait_ge(sh_half.sem, sh_half.at(r, c + 1))
                    nc.scalar.activation(th[0:n, c % 2, :], zb[0:n, c % 2, :], ACT.Tanh).then_inc(sh_tanh.sem, 1)
                if s == "lg":
                    act.wait_ge(rt_steps.sem, rt_steps.at(r, NT + 2))
                    nc.scalar.activation(ex[:, :, :], ex[:, :, :], ACT.Exp).then_inc(rt_exp.sem, 1)
                if s == "shP":
                    glueB(r, 2, b_sh2)

            rounds(act, steps)

        @block.tensor
        def _(pe):
            def project(dst, weight, x, cols, chunks, sig_, rows=None):
                for k in range(chunks):
                    n = 128 if rows is None else min(128, rows - 128 * k)
                    last = nc.tensor.matmul(dst, weight[0:n, k, cols], x[0:n, k, :], start=k == 0, stop=k == chunks - 1)
                last.then_inc(sig_.sem, 1)

            def turn_out(yT, b0, turned):
                for j in range(NT):
                    for m in range(DC):
                        last = nc.tensor.transpose(bank[b0 + j // 2][0:TT, (j % 2) * D + m * 128:(j % 2) * D + (m + 1) * 128],
                                                   yT[:, m, j * TT:(j + 1) * TT], ident)
                last.then_inc(turned.sem, 1)

            def turn_back(x, b0, turned):
                for j in range(NT):
                    for m in range(DC):
                        last = nc.tensor.transpose(bank[b0 + m][:, j * TT:(j + 1) * TT],
                                                   x[:, j, m * 128:(m + 1) * 128], ident[0:TT, 0:TT])
                last.then_inc(turned.sem, 1)

            pe.wait_ge(weights_in, WEIGHTS)
            pe.wait_ge(made, SETUP)

            def outB(r, g):
                pe.wait_ge(projB_T.sem, projB_T.at(r, 2 * g + 2))
                turn_out(yTB, 5, projB_turned)

            def backB(r, g):
                pe.wait_ge(xB_ready.sem, xB_ready.at(r, NT * (g + 1)))
                turn_back(xB, 5, xB_turned)

            def path(r, c):
                pe.wait_ge(decided.sem, decided.at(r, c // 2 + 1))
                if c:
                    pe.wait_ge(leaf_ready.sem, leaf_ready.at(r, c))
                nc.tensor.matmul(bank[7][:, 0:TB], toward[:, (c % 2) * 128:(c % 2 + 1) * 128], dec[:, :],
                                 start=True, stop=True).then_inc(path_done.sem, 1)

            def steps(s, r):
                if s == "turnp":
                    if not isinstance(r, int) or r:
                        pe.wait_ge(hM_ready.sem, hM_ready.at(r - 1, NT))
                    for j in range(NT):
                        pe.wait_ge(patch_norm.sem, patch_norm.at(r, j + 1))
                    for k in range(KP):
                        if k >= 2:
                            pe.wait_ge(patch_T.sem, patch_T.at(r, k - 1))
                        for j in range(NT):
                            last = nc.tensor.transpose(bank[k % 2][:, j * TT:(j + 1) * TT],
                                                       patch[:, j, k * 128:(k + 1) * 128], ident[0:TT, 0:TT])
                        last.then_inc(patch_turned.sem, 1)
                if s == "embed":
                    pe.wait_ge(patch_T.sem, patch_T.at(r, KP))
                    for m in range(DC):
                        project(bank[m][:, 0:TB], w_tok, wide, slice(m * 128, (m + 1) * 128), KP, emb)
                if s == "turne":
                    pe.wait_ge(emb_T.sem, emb_T.at(r, 2))
                    turn_out(yTA, 0, emb_turned)
                if s == "xA":
                    pe.wait_ge(xA_ready.sem, xA_ready.at(r, NT))
                    turn_back(xA, 0, xA_turned)
                if s[:2] == "qk":
                    if s == "qk0":
                        pe.wait_ge(xTA_ready.sem, xTA_ready.at(r, 2))
                    for c in range(2 * int(s[2:]), 2 * int(s[2:]) + 2):
                        if c >= 2:
                            pe.wait_ge(qk_ready.sem, qk_ready.at(r, c - 1))
                        project(bank[c % 2][:, 0:TB], w_qkv, xTA, slice(c * 128, (c + 1) * 128), DC, qk_done)
                if s == "vsum":
                    pe.wait_ge(xsum_ready.sem, xsum_ready.at(r, 1))
                    for c in range(QC):
                        for k in range(DC):
                            last = nc.tensor.matmul(bank[2][:, c * IB:(c + 1) * IB],
                                                    w_qkv[:, k, 2 * INNER + c * 128:2 * INNER + (c + 1) * 128],
                                                    xsum[:, k, :], start=k == 0, stop=k == DC - 1)
                    last.then_inc(vsum_done.sem, 1)
                p = int(s[1:]) if s[0] in "SVTUMRNW" else 0
                if s[0] == "V":
                    for n in range(2):
                        if p:
                            pe.wait_ge(av_ready.sem, av_ready.at(r, 2 * (p - 1) + n + 1))
                        else:
                            pe.wait_ge(sc_ready.sem, sc_ready.at(r, n + 1))
                        for k in range(DC):
                            last = nc.tensor.matmul(bank[n][0:PT, :], xTA[:, k, p * PT:(p + 1) * PT],
                                                    w_qkv[:, k, 2 * INNER + 512 * n:2 * INNER + 512 * (n + 1)],
                                                    start=k == 0, stop=k == DC - 1)
                        last.then_inc(v_done.sem, 1)
                if s[0] == "S":
                    if p:
                        wait_apart(pe, v_ready.sem, v_ready.at(r, 2 * p), pe_passed)
                    else:
                        if not isinstance(r, int) or r:
                            pe.wait_ge(xTB_ready.sem, xTB_ready.at(r - 1, 2))
                        pe.wait_ge(vbias_ready.sem, vbias_ready.at(r, 1))
                        wait_apart(pe, qk_ready.sem, qk_ready.at(r, 2 * QC), pe_passed)
                    for h in range(H):
                        row = slice(64 * (h % 2), 64 * (h % 2) + 64)
                        for m in range(2):
                            t = slice(p * PT + m * L, p * PT + (m + 1) * L)
                            last = nc.tensor.matmul(bank[h % 2][SLOT * m:SLOT * m + L, (h // 2) * L:(h // 2 + 1) * L],
                                                    qk[row, QC + h // 2, t], qk[row, h // 2, t], start=True, stop=True)
                    last.then_inc(sc_done.sem, 1)
                if s[0] == "T":
                    pe.wait_ge(sc_ready.sem, sc_ready.at(r, 2 * p + 2))
                    for c in range(NG):
                        w = IG if c < NG - 1 else LAST
                        last = nc.tensor.transpose(bank[2][0:H * w, c * SP2:(c + 1) * SP2],
                                                   sc[:, c * IG:c * IG + w, :].rearrange("q i h -> q (i h)"),
                                                   ident[0:SP2, 0:SP2])
                    last.then_inc(sc_turned.sem, 1)
                if s[0] == "M":
                    if p:
                        pe.wait_ge(mix_copied.sem, mix_copied.at(r, 2 * p))
                    pe.wait_ge(sm_steps.sem, sm_steps.at(r, 5 * p + 5))
                    for c in range(NG):
                        w = IG if c < NG - 1 else LAST
                        dst = bank[3][0:PT, c * 128:(c + 1) * 128] if c < NG - 1 else bank[4][0:PT, 0:H * w]
                        mat = mix8[0:H * w, 0:w, :].rearrange("p i g -> p (i g)")
                        last = nc.tensor.matmul(dst, prob[0:H * w, c, :], mat, start=True, stop=True)
                    last.then_inc(mixed.sem, 1)
                if s[0] == "W":
                    pe.wait_ge(att_ready.sem, att_ready.at(r, 2 * p + 2))
                    pe.wait_ge(v_ready.sem, v_ready.at(r, 2 * p + 2))
                    pe.wait_ge(sc_ready.sem, sc_ready.at(r, min(2 * p + 4, 2 * PAIRS)))
                    for half in range(2):
                        for g in range(8 * half, 8 * half + 8):
                            at = (g // 2 - 4 * half) * PT
                            last = nc.tensor.matmul(bank[half][64 * (g % 2):64 * (g % 2) + 64, at:at + PT],
                                                    val[:, g * DH:(g + 1) * DH],
                                                    att[:, g, :, :].rearrange("q m i -> q (m i)"), start=True, stop=True)
                        last.then_inc(av_done.sem, 1)
                if s == "outP":
                    pe.wait_ge(av_ready.sem, av_ready.at(r, 2 * PAIRS))
                    for m in range(DC):
                        project(bank[m][:, 0:TB], w_out0, wide, slice(m * 128, (m + 1) * 128), QC, out0_done)
                if s == "outT":
                    pe.wait_ge(out0_T.sem, out0_T.at(r, 2))
                    turn_out(yTA, 0, out0_turned)
                if s == "outX":
                    if not isinstance(r, int) or r < NB - 1:
                        pe.wait_ge(qk_ready.sem, qk_ready.at(r + 1, 2 * QC))
                    pe.wait_ge(xH_ready.sem, xH_ready.at(r, NT))
                    turn_back(xA, 0, xB_turned)
                if s[0] == "z" and s != f"z{FC}":
                    c = int(s[1:])
                    if c == 0:
                        pe.wait_ge(xTB_ready.sem, xTB_ready.at(r, 2))
                        pe.wait_ge(hB_ready.sem, hB_ready.at(r, 0))
                    if c >= 2:
                        pe.wait_ge(z_half.sem, z_half.at(r, c - 1))
                    project(bank[5 + c % 2][:, 0:TB], w_tree, xTB, slice(c * 128, (c + 1) * 128), DC, z_done)
                    if c:
                        path(r, c - 1)
                if s == f"z{FC}":
                    path(r, FC - 1)
                if s == "leafP0":
                    pe.wait_ge(leaf_ready.sem, leaf_ready.at(r, FC))
                    project(bank[5][:, 0:TB], w_leaf, big, slice(0, 128), FC, projB)
                if s == "leafP1":
                    project(bank[6][:, 0:TB], w_leaf, big, slice(128, 256), FC, projB)
                if s == "leafT":
                    outB(r, 0)
                if s == "leafX":
                    backB(r, 0)
                if s == "q1a":
                    pe.wait_ge(xTB_ready.sem, xTB_ready.at(r, 4))
                if s[:2] == "q1":
                    for c in {"a": (0, 1), "b": (2, 3), "c": (4, 5)}[s[2]]:
                        if c in (2, 3):
                            pe.wait_ge(q1_ready.sem, q1_ready.at(r, c - 1))
                        if c in (4, 5):
                            pe.wait_ge(k1_ready.sem, k1_ready.at(r, 4 * (c - 3)))
                        project(bank[5 + c % 2][:, 0:TB], w_in1, xTB, slice(c * 128, (c + 1) * 128), DC, qkv1_done)
                if s[:2] == "s1":
                    p = int(s[3:])
                    if p:
                        wait_apart(pe, sm1_steps.sem, sm1_steps.at(r, 8 * (p - 1) + 4), pe_passed)
                    else:
                        wait_apart(pe, v1_ready.sem, v1_ready.at(r, 2), pe_passed)
                    for h in range(H):
                        c, b, a = h // 8, (h // 4) % 2, h % 4
                        for m in range(2):
                            t = slice(p * PT + m * L, p * PT + (m + 1) * L)
                            last = nc.tensor.matmul(bank[5 + b][SLOT * m:SLOT * m + L, (4 * c + a) * L:(4 * c + a + 1) * L],
                                                    q1[64 * b:64 * b + 64, c, t], k4[64 * b:64 * b + 64, c, a, t],
                                                    start=True, stop=True)
                    last.then_inc(sc1_done.sem, 1)
                if s[:2] == "r1":
                    p = int(s[3:])
                    pe.wait_ge(sm1_steps.sem, sm1_steps.at(r, 8 * p + 8))
                    if p:
                        pe.wait_ge(o1_ready.sem, o1_ready.at(r, p))
                    for c in range(DC):
                        last = nc.tensor.matmul(bank[7][:, c * PT:(c + 1) * PT],
                                                r1[:, c * 8:(c + 1) * 8, :].rearrange("q h d -> q (h d)"),
                                                C("pair", SP2), start=True, stop=True)
                    last.then_inc(r1_turned.sem, 1)
                if s == "o1P":
                    pe.wait_ge(o1_ready.sem, o1_ready.at(r, PAIRS))
                    for m in range(DC):
                        project(bank[5 + m][:, 0:TB], w_out1, o1, slice(m * 128, (m + 1) * 128), DC, projB)
                if s == "o1T":
                    outB(r, 1)
                if s == "o1X":
                    backB(r, 1)
                if s[:2] == "sh" and s[2:].isdigit():
                    c = int(s[2:])
                    n = min(128, SH - 128 * c)
                    if c:
                        pe.wait_ge(sh_half.sem, sh_half.at(r, c))
                    else:
                        pe.wait_ge(xTB_ready.sem, xTB_ready.at(r, 6))
                    project(bank[5][0:n, 0:TB], w_sh1, xTB, slice(c * 128, c * 128 + n), DC, sh_done)
                    if c:
                        pe.wait_ge(sh_up.sem, sh_up.at(r, c))
                    project(bank[6][0:n, 0:TB], w_sh3, xTB, slice(c * 128, c * 128 + n), DC, sh_done)
                if s == "lg":
                    for j in range(NT):
                        for k in range(DC):
                            last = nc.tensor.matmul(bank[7][0:TT, j * E_:(j + 1) * E_], xTB[:, k, j * TT:(j + 1) * TT],
                                                    w_gate[:, k, :], start=k == 0, stop=k == DC - 1)
                    last.then_inc(lg_done.sem, 1)
                if s == "rk":
                    pe.wait_ge(rt_steps.sem, rt_steps.at(r, LOOKED_UP))
                    for j in range(NT):
                        dst = bank[7][0:TT, 64 + j * E_:64 + (j + 1) * E_]
                        nc.tensor.matmul(dst, C("below", TT), both[:, j, :], start=True, stop=False)
                        for e in range(j):
                            nc.tensor.matmul(dst, C("ones", TT)[:, 0:TT], both[:, e, :], start=False, stop=False)
                        last = nc.tensor.matmul(dst, C("ones", TT)[:, 0:TT], load[:, :], start=False, stop=True)
                    last.then_inc(rank_done.sem, 1)
                if s == "shP":
                    pe.wait_ge(sh_up.sem, sh_up.at(r, SC))
                    for m in range(DC):
                        project(bank[5 + m][:, 0:TB], w_sh2, up, slice(m * 128, (m + 1) * 128), SC, projB, rows=SH)
                if s == "shT":
                    outB(r, 2)

            rounds(pe, steps)

        @block.vector
        def _(dve):
            v = nc.vector

            n = [0]

            def step(ins):
                n[0] += 1
                ins.then_inc(made, 1)
                dve.wait_ge(made, n[0])

            step(v.memset(zero, 0.0))
            step(v.memset(load[:, :], 0.0))
            step(v.memset(sc[:, :, :], 0.0))
            for i in range(8):
                step(v.memset(bank[i][:, :], 0.0))
            dve.wait_ge(weights_in, WEIGHTS)
            for k in range(KP):
                step(v.tensor_scalar(w_tok[:, k, :], w_tok[:, k, :], g_ln1[:, k:k + 1], None, ALU.mult))
            step(v.tensor_reduce(wm[:, 0:1], wx[:, :], X, ALU.add, negate=True))
            step(v.tensor_scalar(wm[:, 1:2], wm[:, 0:1], 1.0 / H, None, ALU.mult))
            step(v.tensor_scalar(wx[:, :], wx[:, :], wm[:, 1:2], None, ALU.add))
            step(v.tensor_tensor(mix8[:, :, :], wx[:, :].unsqueeze(1).to_broadcast([128, IG, H]),
                                 C("query").unsqueeze(2).to_broadcast([128, IG, H]), ALU.mult))
            step(v.tensor_scalar(b_tree2[:, :], b_tree[:, :], 0.5, None, ALU.mult))
            step(v.tensor_scalar(b_sh12[:, :], b_sh1[:, :], 0.5, None, ALU.mult))
            for c in range(DC):
                step(v.tensor_scalar(b_k1[:, c, :], C("head4"), b_in1[:, 2 + c:3 + c], None, ALU.mult))
            step(v.tensor_scalar(b_q1[:, :], b_in1[:, 0:2], 0.25, None, ALU.mult))
            step(v.tensor_copy(toward[:, :], toward32))
            assert n[0] == SETUP, n[0]

            def stats(srcs, sts, mv, sig_, r, k):
                for src, st in zip(srcs, sts):
                    v.bn_stats(st, src).then_inc(sig_.sem, 1)
                wait_apart(dve, sig_.sem, sig_.at(r, k + len(srcs)), dve_passed)
                for j, st in enumerate(sts):
                    v.bn_aggr(mv[:, j, :], st).then_inc(sig_.sem, 1)

            def norm(dst, src, mv, rs, j, sig_):
                v.tensor_scalar(dst, src, mv[:, j, 0:1], rs[:, 1, j:j + 1], ALU.subtract, ALU.mult).then_inc(sig_.sem, 1)

            def add(r, dst, old, base, turned, tk, sem):
                dve.wait_ge(turned.sem, turned.at(r, tk))
                for j in range(NT):
                    v.tensor_tensor(dst[:, j, :], bank[base + j // 2][0:TT, (j % 2) * D:(j % 2 + 1) * D],
                                    old[:, j, :], ALU.add).then_inc(sem.sem, 1)

            def measured(r, k, src, ready, st, mv, stats_):
                dve.wait_ge(ready.sem, ready.at(r, NT * (k + 1)))
                stats([src[:, j, :] for j in range(NT)], [st[:, j, :] for j in range(NT)], mv, stats_, r, 2 * NT * k)

            def normed(r, k, x, x_ready, src, mv, rs, stats_, rstd):
                dve.wait_ge(stats_.sem, stats_.at(r, 2 * NT * (k + 1)))
                dve.wait_ge(rstd.sem, rstd.at(r, 2 * (k + 1)))
                for j in range(NT):
                    norm(x[:, j, :], src[:, j, :], mv, rs, j, x_ready)

            def steps(s, r):
                if s == "patch":
                    dve.wait_ge(patch_in.sem, patch_in.at(r, 16))
                    for j in range(NT):
                        for e in range(2):
                            v.bn_stats(stA[:, j, 6 * e:6 * e + 6], patch[:, j, 384 * e:384 * e + 384]).then_inc(patch_stats.sem, 1)
                    wait_apart(dve, patch_stats.sem, patch_stats.at(r, 2 * NT), dve_passed)
                    for j in range(NT):
                        v.bn_aggr(mvA[:, j, :], stA[:, j, :]).then_inc(patch_stats.sem, 1)
                if s == "patchM":
                    dve.wait_ge(patch_stats.sem, patch_stats.at(r, 3 * NT))
                    dve.wait_ge(patch_rstd.sem, patch_rstd.at(r, 2))
                    for j in range(NT):
                        norm(patch[:, j, :], patch[:, j, :], mvA, rsA, j, patch_norm)
                if s == "ln2":
                    dve.wait_ge(emb_turned.sem, emb_turned.at(r, 1))
                    dve.wait_ge(patch_norm.sem, patch_norm.at(r, NT))
                    stats([bank[j // 2][0:TT, (j % 2) * D:(j % 2 + 1) * D] for j in range(NT)],
                          [stA[:, j, 0:6] for j in range(NT)], mvA, emb_stats, r, 0)
                if s == "ln3":
                    dve.wait_ge(emb_stats.sem, emb_stats.at(r, 2 * NT))
                    dve.wait_ge(emb_rstd.sem, emb_rstd.at(r, 2))
                    pos = C("pos", TT).rearrange("p (j d) -> p j d", j=NT)
                    for j in range(NT):
                        v.scalar_tensor_tensor(hA[:, j, :], bank[j // 2][0:TT, (j % 2) * D:(j % 2 + 1) * D],
                                               mvA[:, j, 0:1], g_ln2[:, :], ALU.subtract, ALU.mult).then_inc(emb_steps.sem, 1)
                    for j in range(NT):
                        dve.wait_ge(emb_steps.sem, emb_steps.at(r, j + 1))
                        v.scalar_tensor_tensor(hA[:, j, :], hA[:, j, :], rsA[:, 1, j:j + 1], pos[:, j, :],
                                               ALU.mult, ALU.add).then_inc(emb_steps.sem, 1)
                    dve.wait_ge(emb_steps.sem, emb_steps.at(r, 2 * NT))
                    stats([hA[:, j, :] for j in range(NT)], [stA[:, j, 0:6] for j in range(NT)], mvA, statsA, r, 0)
                if s == "ln4":
                    dve.wait_ge(statsA.sem, statsA.at(r, 2 * NT))
                    dve.wait_ge(rstdA.sem, rstdA.at(r, 2))
                    for j in range(NT):
                        norm(xA[:, j, :], hA[:, j, :], mvA, rsA, j, xA_ready)
                if s == "qk0":
                    dve.wait_ge(xTA_ready.sem, xTA_ready.at(r, 2))
                    v.tensor_reduce(xsum[:, :, :], xTA[:, :, :].rearrange("p c (m l) -> p c m l", m=IB), X,
                                    ALU.add).then_inc(xsum_ready.sem, 1)
                if s == "vsum":
                    dve.wait_ge(vsum_done.sem, vsum_done.at(r, 1))
                    v.tensor_tensor(vbias[:, :, :], bank[2][:, 0:QC * IB].rearrange("p (c m) -> p c m", c=QC),
                                    b_head[:, :].unsqueeze(2).to_broadcast([128, QC, IB]), ALU.mult).then_inc(vbias_ready.sem, 1)
                p = int(s[1:]) if s[0] in "SVTUMRNW" else 0
                if s[0] == "V":
                    for e in range(2):
                        dve.wait_ge(v_done.sem, v_done.at(r, 2 * p + e + 1))
                        v.tensor_tensor(val[:, 512 * e:512 * (e + 1)].rearrange("q (h d) -> q h d", h=8),
                                        bank[e][0:PT, :].rearrange("q (h d) -> q h d", h=8),
                                        g_head[:, 8 * e:8 * e + 8].unsqueeze(2).to_broadcast([PT, 8, DH]),
                                        ALU.mult).then_inc(v_ready.sem, 1)
                if s[0] == "T":
                    dve.wait_ge(sc_turned.sem, sc_turned.at(r, p + 1))
                    full = bank[2][:, 0:NG * SP2].rearrange("q (c s) -> q c s", s=SP2)
                    pv = prob[:, :, :].rearrange("q c (m l) -> q c m l", m=2)
                    k = 5 * p
                    view = two_images(full)
                    v.tensor_reduce(pmax[:, 0], view, X, ALU.max).then_inc(sm_steps.sem, 1)
                    dve.wait_ge(sm_steps.sem, sm_steps.at(r, k + 1))
                    v.tensor_tensor(pv, view, pmax[:, 0].unsqueeze(3).to_broadcast([128, NG, 2, L]),
                                    ALU.subtract).then_inc(sm_steps.sem, 1)
                if s[0] == "U":
                    pv = prob[:, :, :].rearrange("q c (m l) -> q c m l", m=2)
                    k = 5 * p
                    dve.wait_ge(exp_done.sem, exp_done.at(r, p + 1))
                    v.tensor_reduce(pmax[:, 1], pv, X, ALU.add).then_inc(sm_steps.sem, 1)
                    dve.wait_ge(sm_steps.sem, sm_steps.at(r, k + 3))
                    v.reciprocal(pmax[:, 2], pmax[:, 1]).then_inc(sm_steps.sem, 1)
                    dve.wait_ge(sm_steps.sem, sm_steps.at(r, k + 4))
                    v.tensor_tensor(pv, pv, pmax[:, 2].unsqueeze(3).to_broadcast([128, NG, 2, L]),
                                    ALU.mult).then_inc(sm_steps.sem, 1)
                if s[0] == "R":
                    dve.wait_ge(squared.sem, squared.at(r, p + 1))
                    if p:
                        dve.wait_ge(mix_rstd.sem, mix_rstd.at(r, 3 * p))
                    v.tensor_reduce(var[:, 0, :], sq[:, :, :], X, ALU.add).then_inc(mixvar.sem, 1)
                if s[0] == "N":
                    dve.wait_ge(mix_rstd.sem, mix_rstd.at(r, 3 * p + 3))
                    for part, (i0, i1) in enumerate(((0, 32), (32, L))):
                        n = i1 - i0
                        src = mix[:, p % 2, i0 * H:i1 * H].rearrange("q (i g) -> q g i", g=H)
                        v.tensor_tensor(att[:, :, :, i0:i1], src.unsqueeze(2).to_broadcast([PT, H, 2, n]),
                                        own[:, :, i0:i1].unsqueeze(1).to_broadcast([PT, H, 2, n]),
                                        ALU.mult).then_inc(att_ready.sem, 1)
                if s[0] == "W":
                    for half in range(2):
                        dve.wait_ge(av_done.sem, av_done.at(r, 2 * p + half + 1))
                        bias = vbias[:, 4 * half:4 * half + 4, 2 * p:2 * p + 2].unsqueeze(3).to_broadcast([128, 4, 2, L])
                        v.tensor_tensor(wide[:, 4 * half:4 * half + 4, p * PT:(p + 1) * PT].rearrange("q c (m l) -> q c m l", m=2),
                                        bank[half][:, 0:4 * PT].rearrange("q (c m l) -> q c m l", c=4, m=2),
                                        bias, ALU.add).then_inc(av_ready.sem, 1)
                if s == "outN":
                    add(r, hM, hA, 0, out0_turned, 1, hM_ready)
                    measured(r, 0, hM, hM_ready, stH, mvH, statsH)
                if s == "outM":
                    normed(r, 0, xA, xH_ready, hM, mvH, rsH, statsH, rstdH)
                if s[0] == "z":
                    e = int(s[1:]) - 1
                    if e >= 0:
                        dve.wait_ge(z_half.sem, z_half.at(r, e + 1))
                        if e % 2 == 0:
                            v.tensor_scalar(dec[:, :], zb[:, e % 2, :], 0.0, None, ALU.is_gt).then_inc(decided.sem, 1)
                            dve.wait_ge(decided.sem, decided.at(r, e // 2 + 1))
                        dve.wait_ge(z_tanh.sem, z_tanh.at(r, e + 1))
                        v.scalar_tensor_tensor(zb[:, e % 2, :], th[:, e % 2, :], 1.0, zb[:, e % 2, :],
                                               ALU.add, ALU.mult).then_inc(z_silu.sem, 1)
                        dve.wait_ge(z_silu.sem, z_silu.at(r, e + 1))
                        dve.wait_ge(path_done.sem, path_done.at(r, e + 1))
                        if e == 8:
                            dve.wait_ge(spilled_h.sem, spilled_h.at(r, 0))
                        v.scalar_tensor_tensor(big[:, e, :], bank[7][:, 0:TB], C("right")[:, e % 2:e % 2 + 1],
                                               zb[:, e % 2, :], ALU.is_equal, ALU.mult).then_inc(leaf_ready.sem, 1)
                if s == "leafN":
                    add(r, hB, hM, 5, projB_turned, 1, hB_ready)
                    measured(r, 0, hB, hB_ready, stB, mvB, statsB)
                if s == "leafM":
                    dve.wait_ge(spilled_x.sem, spilled_x.at(r, 0))
                    normed(r, 0, xB, xB_ready, hB, mvB, rsB, statsB, rstdB)
                if s[:2] == "s1":
                    p = int(s[3:])
                    dve.wait_ge(sc1_done.sem, sc1_done.at(r, p + 1))
                    for b in range(2):
                        src = bank[5 + b][0:SP2, 0:8 * L].rearrange("q (h l) -> q h l", l=L)
                        v.tensor_reduce(m1[:, 0, 8 * b:8 * b + 8], src, X, ALU.max).then_inc(sm1_steps.sem, 1)
                    dve.wait_ge(sm1_steps.sem, sm1_steps.at(r, 8 * p + 2))
                    for b in range(2):
                        src = bank[5 + b][0:SP2, 0:8 * L].rearrange("q (h l) -> q h l", l=L)
                        v.tensor_tensor(e1[:, 8 * b:8 * b + 8, :], src,
                                        m1[:, 0, 8 * b:8 * b + 8].unsqueeze(2).to_broadcast([SP2, 8, L]),
                                        ALU.subtract).then_inc(sm1_steps.sem, 1)
                if s[:2] == "r1":
                    p = int(s[3:])
                    dve.wait_ge(exp1_done.sem, exp1_done.at(r, p + 1))
                    v.tensor_reduce(m1[:, 1, :], e1, X, ALU.add).then_inc(sm1_steps.sem, 1)
                    dve.wait_ge(sm1_steps.sem, sm1_steps.at(r, 8 * p + 5))
                    v.reciprocal(m1[:, 2, :], m1[:, 1, :]).then_inc(sm1_steps.sem, 1)
                    dve.wait_ge(sm1_steps.sem, sm1_steps.at(r, 8 * p + 6))
                    for b in range(2):
                        bb = slice(8 * b, 8 * b + 8)
                        dst = r1[:, :, :].rearrange("q (c b a) d -> q b c a d", c=2, b=2)[:, b]
                        v.tensor_tensor(dst, m1[:, 1, bb].rearrange("q (c a) -> q c a", c=2).unsqueeze(3).to_broadcast([SP2, 2, 4, 16]),
                                        m1[:, 2, bb].rearrange("q (c a) -> q c a", c=2).unsqueeze(3).to_broadcast([SP2, 2, 4, 16]),
                                        ALU.mult).then_inc(sm1_steps.sem, 1)
                if s[:2] == "p1":
                    p = int(s[3:])
                    dve.wait_ge(r1_turned.sem, r1_turned.at(r, p + 1))
                    dve.wait_ge(v1_ready.sem, v1_ready.at(r, 2))
                    tok = slice(p * PT, (p + 1) * PT)
                    v.tensor_tensor(o1[:, :, tok], v1[:, :, tok], bank[7][:, 0:2 * PT].rearrange("q (c t) -> q c t", c=DC),
                                    ALU.mult).then_inc(o1_ready.sem, 1)
                if s == "o1N":
                    add(r, hB, hB, 5, projB_turned, 2, hB_ready)
                    measured(r, 1, hB, hB_ready, stB, mvB, statsB)
                if s == "o1M":
                    normed(r, 1, xB, xB_ready, hB, mvB, rsB, statsB, rstdB)
                if s[:2] == "sh" and s[2:].isdigit():
                    c = int(s[2:])
                    nn = min(128, SH - 128 * c)
                    dve.wait_ge(sh_half.sem, sh_half.at(r, c + 1))
                    dve.wait_ge(sh_tanh.sem, sh_tanh.at(r, c + 1))
                    v.scalar_tensor_tensor(zb[0:nn, c % 2, :], th[0:nn, c % 2, :], 1.0, zb[0:nn, c % 2, :],
                                           ALU.add, ALU.mult).then_inc(sh_silu.sem, 1)
                    dve.wait_ge(sh_silu.sem, sh_silu.at(r, c + 1))
                    dve.wait_ge(sh_done.sem, sh_done.at(r, 2 * c + 2))
                    if c == SC - 1:
                        dve.wait_ge(zeroed, 16 * TILES)
                    v.scalar_tensor_tensor(up[0:nn, c, :], bank[6][0:nn, 0:TB], b_sh3[0:nn, c:c + 1], zb[0:nn, c % 2, :],
                                           ALU.add, ALU.mult).then_inc(sh_up.sem, 1)
                if s in ("lg", "lh"):
                    gates(r, ("lg", "lh").index(s))
                if s == "rk":
                    ranks(r)
                if s == "shN":
                    add(r, hout, hB, 5, projB_turned, 3, hB_ready)

            def two_images(full):
                return bass.AP(full.tensor, full.offset, [list(full.ap[0]), list(full.ap[1]), [SLOT, 2], [1, L]])

            def gates(r, part):
                at = [part * (NT + 2)]

                def do(ins):
                    at[0] += 1
                    ins.then_inc(rt_steps.sem, 1)

                def own_wait():
                    dve.wait_ge(rt_steps.sem, rt_steps.at(r, at[0]))

                g = bass.ds(r * NT, NT)
                tile_by_expert = [TT, NT, E_]
                if part == 0:
                    dve.wait_ge(lg_done.sem, lg_done.at(r, 1))
                    do(v.tensor_tensor(lg[:, :, :], bank[7][0:TT, 0:NT * E_].rearrange("q (j e) -> q j e", j=NT),
                                       b_gate[:, :].unsqueeze(1).to_broadcast(tile_by_expert), ALU.add))
                    wait_apart(dve, rt_steps.sem, rt_steps.at(r, at[0]), dve_passed)
                    for j in range(NT):
                        do(v.max(top[:, j, :], lg[:, j, :]))
                    own_wait()
                    do(v.tensor_tensor(ex[:, :, :], lg[:, :, :], top[:, :, 0:1].to_broadcast(tile_by_expert), ALU.subtract))
                    assert at[0] == NT + 2
                    return
                for j in range(NT):
                    do(v.max_index(topi[:, j, :], top[:, j, :], lg[:, j, :]))
                own_wait()
                do(v.tensor_copy(topf[:, :, :], topi[:, :, 0:2]))
                own_wait()
                for e in range(2):
                    do(v.tensor_tensor(oh[:, e, g, :], C("iota", TT).unsqueeze(1).to_broadcast(tile_by_expert),
                                       topf[:, :, e:e + 1].to_broadcast(tile_by_expert), ALU.is_equal))
                own_wait()
                do(v.tensor_tensor(both[:, :, :], oh[:, 0, g, :], oh[:, 1, g, :], ALU.add))
                dve.wait_ge(rt_exp.sem, rt_exp.at(r, 1))
                do(v.tensor_reduce(gsum[:, 0, :], ex[:, :, :], X, ALU.add))
                own_wait()
                assert at[0] == LOOKED_UP
                do(v.reciprocal(gsum[:, 1, :], gsum[:, 0, :]))
                for e in range(2):
                    do(v.tensor_tensor(pick[:, e, :, :], oh[:, e, g, :], ex[:, :, :], ALU.mult))
                own_wait()
                for e in range(2):
                    do(v.tensor_reduce(gsum[:, 2 + e, :], pick[:, e, :, :], X, ALU.add))
                own_wait()
                for e in range(2):
                    do(v.tensor_tensor(gate[:, e, g], gsum[:, 2 + e, :], gsum[:, 1, :], ALU.mult))
                assert at[0] == RT_STEPS

            def ranks(r):
                g = bass.ds(r * NT, NT)
                dve.wait_ge(rank_done.sem, rank_done.at(r, 1))
                dve.wait_ge(rt_steps.sem, rt_steps.at(r, RT_STEPS))
                for e in range(2):
                    v.tensor_tensor(pick[:, e, :, :], oh[:, e, g, :],
                                    bank[7][0:TT, 64:64 + NT * E_].rearrange("q (j e) -> q j e", j=NT),
                                    ALU.mult).then_inc(ranked.sem, 1)
                for j in range(NT):
                    dve.wait_ge(ranked.sem, ranked.at(r, 2 + j))
                    v.tensor_tensor(load[:, :], load[:, :], both[:, j, :], ALU.add).then_inc(ranked.sem, 1)
                dve.wait_ge(ranked.sem, ranked.at(r, 2 + NT))
                for e in range(2):
                    v.tensor_reduce(rank[:, e, g], pick[:, e, :, :], X, ALU.add).then_inc(ranked.sem, 1)

            rounds(dve, steps)


def phase2(nc, dram, out_dram, bank, oh, gate, rank, load, const, C, spill_h, spill_x, slot_x, slot_y, semaphore):
    ctx = ExitStack()
    with ctx:
        def sb(name, shape, dt=F32):
            return ctx.enter_context(nc.sbuf_tensor(name, shape, dt))

        RING = 3
        WE = 4 * INTER + 2 * D + 2 * IC
        h = sb("h", [TT, GT, D])
        x = sb("x", [TT, GT, D])
        back = sb("back", [TT, 2 * GT, D])
        count = sb("count", [E_, 128], I32)
        padded = sb("padded", [E_, 128])
        off = sb("off", [TT, E_])
        prod = sb("prod", [TT, 2 * GT, E_])
        posf = sb("posf", [TT, 2, 2 * GT])
        pos = sb("pos", [TT, 2 * GT], I32)
        reach = sb("reach", [1, TILES, E_ - 1])
        owner = sb("owner", [1, TILES])
        owneri = sb("owneri", [1, TILES], I32)
        we = sb("we", [128, RING, WE])
        w2b = sb("w2b", [INTER - 2 * 128, RING, D])
        b2 = sb("b2", [128, RING, D])
        xg = sb("xg", [128, RING, D])
        xgT = sb("xgT", [128, RING, DC, 128])
        thx = sb("thx", [128, RING, IC, 128])
        zx = sb("zx", [128, RING, IC, 128])
        ax = sb("ax", [128, RING, IC, 128])
        yx = sb("yx", [128, RING, D])
        ident = C("ident")

        h_in = semaphore("h_in")
        x_in = semaphore("x_in")
        counted = semaphore("counted")
        placed = semaphore("placed")
        offsets = semaphore("offsets")
        scattered = semaphore("scattered")
        w_in = [semaphore(f"w_in{i}") for i in range(RING)]
        xg_in = [semaphore(f"xg_in{i}") for i in range(RING)]
        xg_turned = semaphore("xg_turned")
        xgT_ready = semaphore("xgT_ready")
        up_done = semaphore("up_done")
        half_done = semaphore("half_done")
        tanh_done = semaphore("tanh_done")
        silu_done = semaphore("silu_done")
        a_ready = semaphore("a_ready")
        y_done = semaphore("y_done")
        y_ready = semaphore("y_ready")
        y_out = [semaphore(f"y_out{i}") for i in range(RING)]
        gathered = [semaphore(f"gathered{i}") for i in range(GT // 4)]
        added = semaphore("added")
        stored = semaphore("stored")
        PLACED = 13

        def tiles(tile):
            def run(eng):
                for k in range(RING):
                    tile(0, k)
                with eng.Fori(1, TILES // RING - 1) as i:
                    for k in range(RING):
                        tile(i, k)
                for k in range(RING):
                    tile(TILES // RING - 1, k)
            return run

        def before(rnd, k):
            if k:
                return rnd, k - 1
            return None if isinstance(rnd, int) and rnd == 0 else (rnd - 1, RING - 1)

        def after(rnd, k):
            if k < RING - 1:
                return rnd, k + 1
            return None if isinstance(rnd, int) and rnd == TILES // RING - 1 else (rnd + 1, 0)

        turned = bank[0][:, 0:D]
        y_bank = bank[1][:, 0:D]
        w1 = [we[:, k, 0:2 * INTER].rearrange("p (c n) -> p c n", c=DC) for k in range(RING)]
        w3 = [we[:, k, 2 * INTER:4 * INTER].rearrange("p (c n) -> p c n", c=DC) for k in range(RING)]
        w2 = [we[:, k, 4 * INTER:4 * INTER + 2 * D].rearrange("p (c n) -> p c n", c=2) for k in range(RING)]
        bias = [we[:, k, 4 * INTER + 2 * D:WE] for k in range(RING)]

        block = ctx.enter_context(nc.Block())

        @block.sync
        def _(sp):
            sp.dma_start(x[:, :, :], spill_x.rearrange("(g p) d -> p g d", p=TT)).then_inc(x_in, 16)
            sp.dma_start(h[:, :, :], spill_h.rearrange("(g p) d -> p g d", p=TT)).then_inc(h_in, 16)
            sp.wait_ge(placed, PLACED)
            sp.wait_ge(scattered, 16 * 2 * GT)

            def tile(rnd, k):
                t = rnd * RING + k
                if not isinstance(rnd, int) or rnd:
                    sp.wait_ge(y_ready, t - RING + 1)
                e = sp.value_load(owneri[0:1, bass.ds(t, 1)], min_val=0, max_val=E_ - 1)
                sp.dma_start(xg[:, k, :], slot_x[bass.ds(t * 128, 128), :]).then_inc(xg_in[k], 16)
                sp.dma_start(we[:, k, :], dram["we"][bass.ds(e, 1), :, :].rearrange("a p n -> (a p) n")).then_inc(w_in[k], 16)
                sp.dma_start(w2b[:, k, :], dram["w2b"][bass.ds(e, 1), :, :].rearrange("a p n -> (a p) n")).then_inc(w_in[k], 16)
                sp.dma_start(b2[:, k, :], dram["b2"][bass.ds(e, 1), :].to_broadcast([128, D])).then_inc(w_in[k], 16)

            tiles(tile)(sp)
            for g in range(GT):
                sp.wait_ge(added, 2 * g + 2)
                sp.dma_start(out_dram[g * TT:(g + 1) * TT, :], h[:, g, :]).then_inc(stored, 16)
            sp.wait_ge(stored, 16 * GT)

        @block.gpsimd
        def _(pool):
            pool.wait_ge(x_in, 16)
            pool.wait_ge(placed, PLACED)
            for e in range(2):
                for g in range(GT):
                    nc.gpsimd.indirect_dma_start(
                        out=slot_x, out_offset=bass.IndirectOffsetOnAxis(ap=pos[:, e * GT + g:e * GT + g + 1], axis=0),
                        in_=x[:, g, :], in_offset=None).then_inc(scattered, 16)
            for k in range(RING):
                pool.wait_ge(y_out[k], 16 * (TILES // RING))
            for g in range(GT):
                for e in range(2):
                    nc.gpsimd.indirect_dma_start(
                        out=back[:, e * GT + g, :], out_offset=None, in_=slot_y,
                        in_offset=bass.IndirectOffsetOnAxis(ap=pos[:, e * GT + g:e * GT + g + 1], axis=0),
                    ).then_inc(gathered[g // 4], 16)

        @block.tensor
        def _(pe):
            nc.tensor.matmul(bank[0][0:E_, 0:128], load[:, :], C("ones", TT), start=True, stop=True).then_inc(counted, 1)
            pe.wait_ge(placed, 3)
            nc.tensor.matmul(bank[1][0:TT, 0:E_], padded[:, 0:TT], C("below16", E_), start=True, stop=True).then_inc(offsets, 1)
            pe.wait_ge(placed, PLACED)

            def turn(rnd, k):
                pe.wait_ge(xg_in[k], (rnd + 1) * 16)
                for m in range(DC):
                    last = nc.tensor.transpose(turned[:, m * 128:(m + 1) * 128], xg[:, k, m * 128:(m + 1) * 128], ident)
                last.then_inc(xg_turned, 1)

            def down(rnd, k):
                t = rnd * RING + k
                pe.wait_ge(a_ready, t * IC + IC)
                if not isinstance(rnd, int) or t:
                    pe.wait_ge(y_ready, t)
                for c in range(IC):
                    n = min(128, INTER - 128 * c)
                    last = nc.tensor.matmul(y_bank, ax[0:n, k, c, :], w2[k][:, c, :] if c < 2 else w2b[:, k, :],
                                            start=c == 0, stop=c == IC - 1)
                last.then_inc(y_done, 1)

            def tile(rnd, k):
                t = rnd * RING + k
                pe.wait_ge(xgT_ready, t + 1)
                pe.wait_ge(w_in[k], (rnd + 1) * 48)
                for e, w in enumerate((w1[k], w3[k])):
                    for c in range(IC):
                        n = min(128, INTER - 128 * c)
                        for m in range(DC):
                            last = nc.tensor.matmul(bank[2 + 2 * k + e][0:n, c * 128:(c + 1) * 128],
                                                    w[:, m, c * 128:c * 128 + n], xgT[:, k, m, :],
                                                    start=m == 0, stop=m == DC - 1)
                    last.then_inc(up_done, 1)
                if before(rnd, k):
                    down(*before(rnd, k))
                if after(rnd, k):
                    turn(*after(rnd, k))

            turn(0, 0)
            tiles(tile)(pe)
            down(TILES // RING - 1, RING - 1)

        @block.scalar
        def _(act):
            def rows(rnd, k):
                t = rnd * RING + k
                act.wait_ge(xg_turned, t + 1)
                nc.scalar.activation(xgT[:, k, :, :].rearrange("p c t -> p (c t)"), turned, ACT.Identity).then_inc(xgT_ready, 1)

            def store(rnd, k):
                t = rnd * RING + k
                act.wait_ge(y_ready, t + 1)
                act.dma_start(slot_y[bass.ds(t * 128, 128), :], yx[:, k, :]).then_inc(y_out[k], 16)

            def tile(rnd, k):
                t = rnd * RING + k
                act.wait_ge(half_done, t * IC + IC)
                nc.scalar.activation(thx[:, k, :, :], zx[:, k, :, :], ACT.Tanh).then_inc(tanh_done, 1)
                if after(rnd, k):
                    rows(*after(rnd, k))
                if before(rnd, k):
                    store(*before(rnd, k))

            rows(0, 0)
            tiles(tile)(act)
            store(TILES // RING - 1, RING - 1)

        @block.vector
        def _(dve):
            v = nc.vector
            n = [0]

            def step(ins):
                n[0] += 1
                ins.then_inc(placed, 1)
                dve.wait_ge(placed, n[0])

            dve.wait_ge(counted, 1)
            step(v.tensor_scalar(count[:, :], bank[0][0:E_, 0:128], 127.0, None, ALU.add))
            step(v.tensor_scalar(count[:, :], count[:, :], 7, 7, ALU.arith_shift_right, ALU.logical_shift_left))
            step(v.tensor_copy(padded[:, :], count[:, :]))
            dve.wait_ge(offsets, 1)
            step(v.tensor_copy(off[:, :], bank[1][0:TT, 0:E_]))
            step(v.tensor_tensor(prod[:, :, :], oh[:, :, :, :].rearrange("p b g e -> p (b g) e"),
                                 off[:, :].unsqueeze(1).to_broadcast([TT, 2 * GT, E_]), ALU.mult))
            step(v.tensor_reduce(posf[:, 0, :], prod[:, :, :], X, ALU.add))
            step(v.tensor_tensor(posf[:, 1, :], posf[:, 0, :], rank[:, :, :].rearrange("p b g -> p (b g)"), ALU.add))
            step(v.tensor_copy(pos[:, :], posf[:, 1, :]))
            step(v.tensor_tensor(reach[:, :, :], C("starts", 1).unsqueeze(2).to_broadcast([1, TILES, E_ - 1]),
                                 off[0:1, 1:E_].unsqueeze(1).to_broadcast([1, TILES, E_ - 1]), ALU.is_ge))
            step(v.tensor_reduce(owner[:, :], reach[:, :, :], X, ALU.add))
            step(v.tensor_copy(owneri[:, :], owner[:, :]))
            step(v.memset(zx[:, :, :, :], 0.0))
            step(v.memset(thx[:, :, :, :], 0.0))
            assert n[0] == PLACED

            def result(rnd, k):
                t = rnd * RING + k
                dve.wait_ge(y_done, t + 1)
                if not isinstance(rnd, int) or rnd:
                    dve.wait_ge(y_out[k], rnd * 16)
                v.tensor_tensor(yx[:, k, :], y_bank, b2[:, k, :], ALU.add).then_inc(y_ready, 1)

            def tile(rnd, k):
                t = rnd * RING + k
                dve.wait_ge(up_done, t * 2 + 1)
                for c in range(IC):
                    m = min(128, INTER - 128 * c)
                    v.tensor_scalar(zx[0:m, k, c, :], bank[2 + 2 * k][0:m, c * 128:(c + 1) * 128], bias[k][0:m, c:c + 1], 0.5,
                                    ALU.add, ALU.mult).then_inc(half_done, 1)
                if before(rnd, k):
                    result(*before(rnd, k))
                dve.wait_ge(tanh_done, t + 1)
                v.scalar_tensor_tensor(zx[:, k, :, :], thx[:, k, :, :], 1.0, zx[:, k, :, :], ALU.add, ALU.mult).then_inc(silu_done, 1)
                dve.wait_ge(silu_done, t + 1)
                dve.wait_ge(up_done, t * 2 + 2)
                for c in range(IC):
                    m = min(128, INTER - 128 * c)
                    v.scalar_tensor_tensor(ax[0:m, k, c, :], bank[3 + 2 * k][0:m, c * 128:(c + 1) * 128],
                                           bias[k][0:m, IC + c:IC + c + 1], zx[0:m, k, c, :], ALU.add, ALU.mult).then_inc(a_ready, 1)

            tiles(tile)(dve)
            result(TILES // RING - 1, RING - 1)
            dve.wait_ge(h_in, 16)
            for g in range(GT):
                if g % 4 == 0:
                    dve.wait_ge(gathered[g // 4], 16 * 8)
                for e in range(2):
                    if e:
                        dve.wait_ge(added, 2 * g + 1)
                    v.scalar_tensor_tensor(h[:, g, :], back[:, e * GT + g, :], gate[:, e, g:g + 1], h[:, g, :],
                                           ALU.mult, ALU.add).then_inc(added, 1)


def kernel(**inputs):
    import concourse.bacc as bacc
    from concourse.bass_utils import run_bass_kernel_spmd

    a = {k: np.asarray(v) for k, v in inputs.items()}

    def rows(w):
        return w.reshape(-1, 128, w.shape[1]).transpose(1, 0, 2)

    def column(b, chunks):
        out = np.zeros(chunks * 128, b.dtype)
        out[:b.size] = b
        return out.reshape(chunks, 128).T

    const, toward = constants()
    f = np.float32
    tree = np.zeros((TREES, NODES, D), f)
    tree[:, :NODES - 1] = a["L0_ffn_W_in"].reshape(TREES, NODES - 1, D)
    tree_b = np.zeros((TREES, NODES), f)
    tree_b[:, :NODES - 1] = a["L0_ffn_b_in"].reshape(TREES, NODES - 1)
    leaf = np.zeros((D, TREES, NODES), f)
    leaf[:, :, :NODES - 1] = a["L0_ffn_W_out"].reshape(D, TREES, NODES - 1)
    in1 = a["L1_attn_w_in"].reshape(H, 3, 16, D).transpose(1, 0, 2, 3).reshape(3 * D, D)
    in1_b = a["L1_attn_b_in"].reshape(H, 3, 16).transpose(1, 0, 2).reshape(3 * D)
    sh2 = np.zeros((SC * 128, D), f)
    sh2[:SH] = a["L1_ffn_sw2"]
    we = np.zeros((E_, 128, 4 * INTER + 2 * D + 2 * IC), f)
    for e in range(E_):
        we[e, :, 0:2 * INTER] = rows(a["L1_ffn_w1"][e]).reshape(128, -1)
        we[e, :, 2 * INTER:4 * INTER] = rows(a["L1_ffn_w3"][e]).reshape(128, -1)
        we[e, :, 4 * INTER:4 * INTER + 2 * D] = rows(a["L1_ffn_w2"][e, :256]).reshape(128, -1)
        we[e, :, -2 * IC:-IC] = column(a["L1_ffn_b1"][e], IC)
        we[e, :, -IC:] = column(a["L1_ffn_b3"][e], IC)
    arrays = {
        "const": const, "toward": toward,
        "patches": a["x"].reshape(B, 3, 6, 16, 6, 16).transpose(0, 2, 4, 1, 3, 5).reshape(NB, NT, TT, PD).transpose(0, 2, 1, 3).reshape(NB * TT, NT, PD),
        "w_tok": rows(a["L0_tok_W"].T), "g_ln1": column(a["L0_tok_ln1_w"], KP), "g_ln2": a["L0_tok_ln2_w"],
        "w_qkv": rows(a["L0_attn_w_qkv"]), "w_out0": rows(a["L0_attn_w_out"]), "b_out0": column(a["L0_attn_b_out"], DC),
        "g_head": a["L0_attn_ln_gamma"], "b_head": column(np.repeat(a["L0_attn_ln_beta"], DH), QC),
        "wx": np.tile(a["L0_attn_reattn_w"], (IG, 1)),
        "w_tree": rows(tree.reshape(-1, D).T), "b_tree": column(tree_b.reshape(-1), FC),
        "w_leaf": rows(leaf.reshape(D, -1).T),
        "w_in1": rows(in1.T), "b_in1": column(in1_b, 6), "w_out1": rows(a["L1_attn_w_out"].T), "b_out1": column(a["L1_attn_b_out"], DC),
        "w_sh1": rows(a["L1_ffn_sw1"]), "w_sh3": rows(a["L1_ffn_sw3"]), "w_sh2": rows(sh2),
        "b_sh1": column(a["L1_ffn_sb1"], SC), "b_sh3": column(a["L1_ffn_sb3"], SC), "b_sh2": column(a["L1_ffn_sb2"], DC),
        "w_gate": rows(a["L1_ffn_gate_w"]), "b_gate": a["L1_ffn_gate_b"],
        "we": we, "w2b": a["L1_ffn_w2"][:, 256:], "b2": a["L1_ffn_b2"],
    }
    nc = bacc.Bacc("TRN2", target_bir_lowering=False, num_devices=1)
    feed, dram = {}, {}
    for name, x in arrays.items():
        x = np.ascontiguousarray(x)
        feed[f"in_{name}"] = x
        dram[name] = nc.dram_tensor(f"in_{name}", x.shape, mybir.dt.from_np(x.dtype), kind="ExternalInput").ap()
    out = nc.dram_tensor("out", (T, D), F32, kind="ExternalOutput").ap()
    program(nc, dram, out)
    r = run_bass_kernel_spmd(nc, [feed], core_ids=[0])
    return r.results[0]["out"].reshape(B, L, D)
```

```python
from contextlib import ExitStack

import numpy as np

import concourse.bass as bass
from concourse import mybir

F32 = mybir.dt.float32
BF16 = mybir.dt.bfloat16
I32 = mybir.dt.int32
U32 = mybir.dt.uint32
ALU = mybir.AluOpType
ACT = mybir.ActivationFunctionType
X = mybir.AxisListType.X

B, L, D = 64, 36, 256
T = B * L
PD = 768
KP = PD // 128
IB = 8
NB = B // IB
TB = IB * L
TT = 96
NT = TB // TT
PAIRS = IB // 2
PT = 2 * L
SLOT = 64
SP2 = SLOT + L
DC = D // 128
H = 16
DH = 64
INNER = H * DH
QC = INNER // 128
IG = 8
NG = (L + IG - 1) // IG
LAST = L - (NG - 1) * IG
TREES, NODES = 8, 256
FC = TREES * 2
E_, INTER = 16, 352
SH = 704
SC = (SH + 127) // 128
IC = (INTER + 127) // 128
SLOTS = T * 2
TILES = (SLOTS + E_ * 127) // 128
GT = T // TT
WE = 4 * INTER + IC * D
EARLY = 11
MIDDLE = 14
EB = 2 * INTER + D
REGION = T + 128
SETUP = 26
LOOKED_UP = 2 * NT + 7
RT_STEPS = LOOKED_UP + 7


def layout(parts):
    at, out = 0, {}
    for name, width in parts:
        out[name] = (at, width)
        at += width
    return out, at


COLS, CW = layout([("ident", 128), ("ones", 128), ("pair", PT), ("own", 2), ("query", IG),
                   ("head4", 4), ("right", 2), ("below", TT), ("below16", E_), ("iota", E_),
                   ("spare", 4), ("pos", NT * D), ("minushalf", L), ("starts", TILES)])


def constants():
    c = np.zeros((128, CW), np.float32)

    def put(name, a):
        at, w = COLS[name]
        c[:a.shape[0], at:at + w] = a

    r = np.arange(128)
    put("ident", np.eye(128))
    put("ones", np.ones((128, 128)))
    pair = np.zeros((128, PT))
    for m in range(2):
        pair[m * SLOT + np.arange(L), m * L + np.arange(L)] = 1
    put("pair", pair)
    put("own", np.stack([r < L, (r >= L) & (r < PT)], 1))
    put("query", r[:, None] // H == np.arange(IG))
    put("head4", (r[:, None] % 64) // 16 == np.arange(4))
    put("below", r[:, None] < np.arange(TT))
    put("below16", r[:, None] < np.arange(E_))
    put("iota", np.tile(np.arange(E_), (128, 1)))
    put("minushalf", np.full((128, L), -0.5))
    put("starts", np.tile(128 * np.arange(TILES), (128, 1)))
    toward = np.zeros((128, NODES), np.float32)
    rights = np.full((128, 2), 99.0)
    for node in range(NODES - 1):
        n, k = node, 0
        while n:
            up = (n - 1) // 2
            toward[up, node] = 1 if n == 2 * up + 2 else -1
            k += n == 2 * up + 2
            n = up
        rights[node % 128, node // 128] = k
    put("right", rights)
    w = np.float32(1) / np.float32(10000.0) ** (np.arange(D // 4, dtype=np.float32) / np.float32(D // 4 - 1))
    y, x = np.meshgrid(np.arange(6, dtype=np.float32), np.arange(6, dtype=np.float32), indexing="ij")
    y, x = y.reshape(-1)[:, None] * w, x.reshape(-1)[:, None] * w
    pos = np.concatenate([np.sin(x), np.cos(x), np.sin(y), np.cos(y)], 1)
    put("pos", np.tile(pos, (IB, 1)).reshape(NT, TT, D).transpose(1, 0, 2).reshape(TT, NT * D))
    return c, toward


def program(nc, dram, out_dram):
    ctx = ExitStack()
    with ctx:
        def sb(name, shape, dt=F32):
            return ctx.enter_context(nc.sbuf_tensor(name, shape, dt))

        def semaphore(name):
            return ctx.enter_context(nc.semaphore(name))

        spill_h = nc.dram_tensor("spill_h", [T, D], F32, kind="Internal").ap()
        slot_x = nc.dram_tensor("slot_x", [E_ * REGION, D], F32, kind="Internal").ap()
        bias_parts = nc.dram_tensor("bias_parts", [E_, 3 * EB], BF16, kind="Internal").ap()
        slot_y = nc.dram_tensor("slot_y", [TILES * 128, D], F32, kind="Internal").ap()

        bank = [ctx.enter_context(nc.psum_tensor(f"bank{i}", [128, 512], F32)) for i in range(8)]
        oh = sb("oh", [TT, 2, GT, E_])
        gate = sb("gate", [TT, 2, GT])
        rank = sb("rank", [TT, 2, GT])
        load = sb("load", [TT, E_])
        const = sb("const", [128, CW])

        def C(name, parts=128):
            at, w = COLS[name]
            return const[0:parts, at:at + w]

        we = sb("we", [128, E_, WE])
        we_in = semaphore("we_in")

        phase1(nc, dram, bank, we, we_in, oh, gate, rank, load, const, C, spill_h, slot_x, semaphore)
        phase2(nc, dram, out_dram, bank, we, we_in, oh, gate, rank, load, C, spill_h, slot_x, slot_y, bias_parts, semaphore)


def wait_apart(eng, sem, value, passed):
    eng.wait_ge(sem, value)
    eng.sem_inc(passed, 1)


class Signal:

    def __init__(self, sem, per, start=0):
        self.sem, self.per, self.start = sem, per, start

    def at(self, rnd, k):
        return rnd * self.per + (self.start + k)


def phase1(nc, dram, bank, we, we_in, oh, gate, rank, load, const, C, spill_h, slot_x, semaphore):
    ctx = ExitStack()
    with ctx:
        def sb(name, shape, dt=F32):
            return ctx.enter_context(nc.sbuf_tensor(name, shape, dt))

        def sig(name, per=1, start=0):
            return Signal(semaphore(name), per, start)

        at = [0]

        def carve(shape):
            n = int(np.prod(shape[1:]))
            view = we[0:shape[0], :, :].rearrange("p e n -> p (e n)")[:, at[0]:at[0] + n]
            at[0] += n
            assert at[0] <= E_ * WE
            return view.rearrange("p (a b) -> p a b", b=shape[2]) if len(shape) == 3 else view

        w_tok = carve([128, KP, D])
        w_qkv = carve([128, DC, 3 * INNER])
        w_out0 = carve([128, QC, D])
        patch = carve([TT, NT, PD])
        wide = carve([128, 8, TB])
        hA = carve([TT, NT, D])
        xA = carve([TT, NT, D])
        xTA = carve([128, DC, TB])
        qk = carve([128, 2 * QC, TB])
        val = carve([PT, INNER])
        sc = carve([SP2, L, H])
        prob = carve([128, NG, PT])
        mixed_in = carve([128, H * PT])
        assert at[0] >= EARLY * WE
        w_tree = carve([128, DC, TREES * NODES])
        w_leaf = carve([128, FC, D])
        assert at[0] >= MIDDLE * WE
        w_in1 = carve([128, DC, 3 * D])
        w_out1 = carve([128, DC, D])
        r1 = carve([SP2, H, 16])
        lg = carve([TT, NT, E_])
        ex = carve([TT, NT, E_])
        both = carve([TT, NT, E_])
        w_sh1 = sb("w_sh1", [128, DC, SH])
        w_sh3 = sb("w_sh3", [128, DC, SH])
        w_sh2 = sb("w_sh2", [128, SC, D])
        w_gate = sb("w_gate", [128, DC, E_])
        b_gate = sb("b_gate", [TT, E_])
        g_ln1 = sb("g_ln1", [128, KP])
        g_ln2 = sb("g_ln2", [TT, D])
        g_head = sb("g_head", [PT, H])
        b_head = sb("b_head", [128, QC])
        b_out0 = sb("b_out0", [128, DC])
        b_tree = sb("b_tree", [128, FC])
        b_tree2 = sb("b_tree2", [128, FC])
        b_in1 = sb("b_in1", [128, 6])
        b_k1 = sb("b_k1", [128, DC, 4])
        b_q1 = sb("b_q1", [128, DC])
        b_out1 = sb("b_out1", [128, DC])
        b_sh1 = sb("b_sh1", [128, SC])
        b_sh12 = sb("b_sh12", [128, SC])
        b_sh3 = sb("b_sh3", [128, SC])
        b_sh2 = sb("b_sh2", [128, DC])
        toward = sb("toward", [128, NODES], BF16)
        wx = sb("wx", [128, H])
        wm = sb("wm", [128, 2])
        mix8 = sb("mix8", [128, IG, H])
        stA = sb("stA", [TT, NT, 12])
        mvA = sb("mvA", [TT, NT, 2])
        rsA = sb("rsA", [TT, 2, NT])
        mix = patch[0:PT, :, :].rearrange("q j d -> q (j d)")[:, 0:2 * L * H].rearrange("q (b n) -> q b n", b=2)
        hM = sb("hM", [TT, NT, D])
        xsum = sb("xsum", [128, DC, IB])
        vbias = sb("vbias", [128, QC, IB])
        pmax = sb("pmax", [128, 3, NG, 2])
        sq = xA[0:PT, :, :].rearrange("q j d -> q (j d)")[:, 0:L * H].rearrange("q (i h) -> q i h", i=L)
        var = sb("var", [PT, 3, L])
        own = sb("own", [PT, 2, L])
        att = mixed_in[0:PT, :].rearrange("q (g m i) -> q g m i", g=H, m=2)
        yTA = mixed_in[:, 0:DC * TB].rearrange("p (c t) -> p c t", c=DC)
        stB = sb("stB", [TT, NT, 6])
        stH = sb("stH", [TT, NT, 6])
        mvH = sb("mvH", [TT, NT, 2])
        rsH = sb("rsH", [TT, 2, NT])
        mvB = sb("mvB", [TT, NT, 2])
        rsB = sb("rsB", [TT, 2, NT])
        hB = sb("hB", [TT, NT, D])
        xB = sb("xB", [TT, NT, D])
        xTB = sb("xTB", [128, DC, TB])
        th = sb("th", [128, 2, TB])
        zb = sb("zb", [128, 2, TB])
        toward32 = th[:, :, :].rearrange("p a t -> p (a t)")[:, 0:NODES]
        dec = sb("dec", [128, TB], BF16)
        big = sb("big", [128, 20, TB])
        k4 = big[:, 0:8, :].rearrange("p (c a) t -> p c a t", c=DC)
        q1 = big[:, 8:10, :]
        v1 = big[:, 10:12, :]
        o1 = big[:, 12:14, :]
        up = big[:, 14:20, :]
        hout = big[0:TT, 8:11, :].rearrange("p a t -> p (a t)")[:, 0:NT * D].rearrange("p (j d) -> p j d", j=NT)
        soft = sb("soft", [128, H * L])
        e1 = up[0:SP2, :, :].rearrange("q c t -> q (c t)")[:, 0:2 * H * L].rearrange("q (b h l) -> q b h l", b=2, h=H)
        yTB = soft[:, :].rearrange("p (c t) -> p c t", c=DC)
        m1 = sb("m1", [SP2, 3, H])
        top = sb("top", [TT, NT, 8])
        topi = sb("topi", [TT, NT, 8], U32)
        topf = sb("topf", [TT, NT, 2])
        gsum = sb("gsum", [TT, 4, NT])
        pick = r1[0:TT, :, :].rearrange("q h d -> q (h d)")[:, 0:2 * NT * E_].rearrange("q (b j e) -> q b j e", b=2, j=NT)
        spot = sb("spot", [TT, 2, NT], I32)

        first_in = semaphore("first_in")
        small_in = semaphore("small_in")
        qkv_in = semaphore("qkv_in")
        rest_in = semaphore("rest_in")
        pe_passed = semaphore("pe_passed")
        dve_passed = semaphore("dve_passed")
        pool_passed = semaphore("pool_passed")
        made = semaphore("made")
        patch_in = sig("patch_in", 16)
        patch_stats = sig("patch_stats", 3 * NT)
        patch_rstd = sig("patch_rstd", 2)
        patch_norm = sig("patch_norm", NT)
        patch_turned = sig("patch_turned", KP)
        patch_T = sig("patch_T", KP)
        emb = sig("emb", 2)
        emb_T = sig("emb_T", 2)
        emb_turned = sig("emb_turned", 1)
        emb_stats = sig("emb_stats", 2 * NT)
        emb_rstd = sig("emb_rstd", 2)
        emb_steps = sig("emb_steps", 2 * NT)
        statsA = sig("statsA", 2 * NT)
        rstdA = sig("rstdA", 2)
        xA_ready = sig("xA_ready", NT)
        xH_ready = sig("xH_ready", NT)
        xA_turned = sig("xA_turned", 1)
        xTA_ready = sig("xTA_ready", 2)
        qk_done = sig("qk_done", 2 * QC)
        qk_ready = sig("qk_ready", 2 * QC)
        xsum_ready = sig("xsum_ready", 1)
        vsum_done = sig("vsum_done", 1)
        vbias_ready = sig("vbias_ready", 1)
        v_done = sig("v_done", 2 * PAIRS)
        v_ready = sig("v_ready", 2 * PAIRS)
        sc_done = sig("sc_done", PAIRS)
        sc_ready = sig("sc_ready", 2 * PAIRS)
        sc_turned = sig("sc_turned", PAIRS)
        sm_steps = sig("sm_steps", 5 * PAIRS)
        exp_done = sig("exp_done", PAIRS)
        mixed = sig("mixed", PAIRS)
        mix_copied = sig("mix_copied", 2 * PAIRS)
        squared = sig("squared", PAIRS)
        mixvar = sig("mixvar", PAIRS)
        mix_rstd = sig("mix_rstd", 3 * PAIRS)
        att_ready = sig("att_ready", 2 * PAIRS)
        av_done = sig("av_done", 2 * PAIRS)
        av_ready = sig("av_ready", 2 * PAIRS)
        out0_done = sig("out0_done", 2)
        out0_T = sig("out0_T", 2)
        out0_turned = sig("out0_turned", 1)
        hM_ready = sig("hM_ready", NT)
        statsH = sig("statsH", 2 * NT)
        rstdH = sig("rstdH", 2)
        hB_ready = sig("hB_ready", 3 * NT, 1)
        statsB = sig("statsB", 2 * 2 * NT)
        rstdB = sig("rstdB", 2 * 2)
        xB_ready = sig("xB_ready", 2 * NT)
        xB_turned = sig("xB_turned", 3)
        xTB_ready = sig("xTB_ready", 2 * 3)
        projB = sig("projB", 2 * 3)
        projB_T = sig("projB_T", 2 * 3)
        projB_turned = sig("projB_turned", 3)
        z_done = sig("z_done", FC)
        z_tanh = sig("z_tanh", FC)
        z_half = sig("z_half", FC)
        z_silu = sig("z_silu", FC)
        decided = sig("decided", TREES)
        path_done = sig("path_done", FC)
        leaf_ready = sig("leaf_ready", FC)
        qkv1_done = sig("qkv1_done", 6)
        q1_ready = sig("q1_ready", 2)
        k1_ready = sig("k1_ready", 8)
        v1_ready = sig("v1_ready", 2)
        sc1_done = sig("sc1_done", PAIRS)
        sm1_steps = sig("sm1_steps", 4 * PAIRS)
        sum1_steps = sig("sum1_steps", 4 * PAIRS)
        exp1_done = sig("exp1_done", PAIRS)
        r1_turned = sig("r1_turned", PAIRS)
        o1_ready = sig("o1_ready", PAIRS)
        sh_done = sig("sh_done", 2 * SC)
        sh_tanh = sig("sh_tanh", SC)
        sh_half = sig("sh_half", SC)
        sh_silu = sig("sh_silu", SC)
        sh_up = sig("sh_up", SC)
        lg_done = sig("lg_done", 1)
        rt_steps = sig("rt_steps", RT_STEPS)
        rt_exp = sig("rt_exp", 1)
        rank_done = sig("rank_done", 1)
        spilled_h = sig("spilled_h", 16, 16)
        scattered = sig("scattered", 16 * 2 * NT)
        xB_free = sig("xB_free", 1, 1)
        ranked = sig("ranked", 6 + NT)

        first = [(w_tok[:, :, :], dram["w_tok"]), (const[:, :], dram["const"])]
        small = [
            (g_ln1[:, :], dram["g_ln1"]), (wx[:, :], dram["wx"]), (toward32, dram["toward"]),
            (b_tree[:, :], dram["b_tree"]), (b_sh1[:, :], dram["b_sh1"]), (b_in1[:, :], dram["b_in1"]),
            (g_ln2[:, :], dram["g_ln2"].partition_broadcast(TT)), (g_head[:, :], dram["g_head"].partition_broadcast(PT)),
            (b_head[:, :], dram["b_head"]), (b_out0[:, :], dram["b_out0"]), (b_out1[:, :], dram["b_out1"]),
            (b_sh3[:, :], dram["b_sh3"]), (b_sh2[:, :], dram["b_sh2"]), (b_gate[:, :], dram["b_gate"].partition_broadcast(TT)),
        ]
        rest = [
            (w_out0[:, :, :], dram["w_out0"]), (w_tree[:, :, :], dram["w_tree"]), (w_leaf[:, :, :], dram["w_leaf"]),
            (w_in1[:, :, :], dram["w_in1"]), (w_out1[:, :, :], dram["w_out1"]), (w_sh1[:, :, :], dram["w_sh1"]),
            (w_sh3[:, :, :], dram["w_sh3"]), (w_sh2[:, :, :], dram["w_sh2"]), (w_gate[:, :, :], dram["w_gate"]),
        ]
        ident = C("ident")
        START = """load patch patchM turnp embed turne ln2 ln3 ln4 xA qk0 qk1 qk2 qk3 qk4 qk5 qk6 qk7 vsum""".split()
        ATTEND = """S0 T0 V0 U0 M0 R0 S1 T1 N0 U1 W0 M1 R1 V1 S2 T2 N1 U2 W1 M2 R2 V2 S3 T3 N2 U3 W2 M3 R3 V3 N3 W3
            outP outT outN""".split()
        HAND_OVER = ["outM", "outX"]
        FINISH = ([f"z{c}" for c in range(FC + 1)] + """leafP0 leafP1 leafT leafN leafM leafX q1a q1b q1c s1_0 s1_1
            r1_0 p1_0 s1_2 r1_1 p1_1 s1_3 r1_2 p1_2 r1_3 p1_3 o1P o1T o1N o1M o1X sh0 lg sh1 lh sh2 sh3 rk sh4 sh5
            shP shT shN""".split())
        MIXED = """S0 z0 T0 z1 V0 U0 z2 M0 z3 R0 S1 z4 T1 z5 z6 N0 U1 W0 M1 z7 R1 V1 z8 S2 z9 T2 N1 z10 U2 W1 M2 z11 R2
            V2 z12 S3 z13 T3 N2 z14 U3 W2 M3 z15 R3 V3 z16 leafP0 N3 load W3 leafP1 leafT outP leafN patch leafM patchM
            outT turnp outN leafX embed q1a turne q1b ln2 q1c ln3 s1_0 s1_1 ln4 xA r1_0 p1_0 s1_2 qk0 r1_1 qk1 p1_1 s1_3 qk2
            r1_2 qk3 p1_2 r1_3 p1_3 o1P qk4 o1T o1N qk5 o1M qk6 outM o1X qk7 sh0 vsum lg sh1 lh sh2 sh3
            rk sh4 sh5 outX shP shT shN""".split()
        for part in START, ATTEND + HAND_OVER, FINISH:
            assert [s for s in MIXED if s in part] == part

        def rounds(eng, steps):
            def full_round(r):
                for s in MIXED:
                    steps(s, r + 1 if s in START else r - 1 if s in FINISH else r)

            for s in START:
                steps(s, 0)
            for s in ATTEND:
                steps(s, 0)
            for s in START:
                steps(s, 1)
            for s in HAND_OVER:
                steps(s, 0)
            with eng.Fori(1, NB - 1) as i:
                full_round(i)
            for s in MIXED:
                if s not in START:
                    steps(s, NB - 2 if s in FINISH else NB - 1)
            steps("prefetch", NB - 1)
            for s in FINISH:
                steps(s, NB - 1)
                if s == "leafT":
                    steps("prefetch_more", NB - 1)

        block = ctx.enter_context(nc.Block())

        @block.sync
        def _(sp):
            sp.sem_inc(hB_ready.sem, 1)
            sp.sem_inc(spilled_h.sem, 16)
            sp.sem_inc(xB_free.sem, 1)
            def steps(s, r):
                if s == "prefetch":
                    sp.wait_ge(xTB_ready.sem, xTB_ready.at(r, 2))
                    sp.dma_start(we[:, 0:EARLY, :], dram["we"][0:EARLY, :, :].rearrange("e p n -> p e n")).then_inc(we_in, 16)
                if s == "prefetch_more":
                    sp.wait_ge(projB_T.sem, projB_T.at(r, 2))
                    sp.dma_start(we[:, EARLY:MIDDLE, :], dram["we"][EARLY:MIDDLE, :, :].rearrange("e p n -> p e n")).then_inc(we_in, 16)
                if s == "load":
                    if not isinstance(r, int) or r:
                        sp.wait_ge(patch_turned.sem, patch_turned.at(r - 1, KP))
                        sp.wait_ge(att_ready.sem, att_ready.at(r - 1, 2 * PAIRS))
                    sp.dma_start(patch[:, :, :], dram["patches"][bass.ds(r * TT, TT), :, :]).then_inc(patch_in.sem, 16)
                    if isinstance(r, int) and r == 0:
                        for dst, src in first:
                            sp.dma_start(dst, src).then_inc(first_in, 16)
                        sp.wait_ge(small_in, 16 * len(small))
                        sp.dma_start(w_qkv[:, :, :], dram["w_qkv"]).then_inc(qkv_in, 16)
                        for dst, src in rest:
                            sp.dma_start(dst, src).then_inc(rest_in, 16)
                if s == "shN":
                    sp.wait_ge(hB_ready.sem, hB_ready.at(r, 3 * NT))
                    sp.dma_start(spill_h[bass.ds(r * TB, TB), :].rearrange("(j p) d -> p j d", p=TT),
                                 hout).then_inc(spilled_h.sem, 16)

            rounds(sp, steps)
            sp.wait_ge(spilled_h.sem, spilled_h.at(NB, 0))
            sp.wait_ge(scattered.sem, scattered.at(NB, 0))

        @block.gpsimd
        def _(pool):
            minus = C("minushalf")

            def inverse_root(out, mid, var_ap, done, r, k, eps):
                nc.gpsimd.tensor_scalar(mid, var_ap, 1.0, eps, ALU.mult, ALU.add).then_inc(done.sem, 1)
                pool.wait_ge(done.sem, done.at(r, k + 1))
                n = mid.shape[-1]
                nc.gpsimd.tensor_tensor(out, mid, minus[0:mid.shape[0], 0:n], ALU.pow).then_inc(done.sem, 1)

            pool.wait_ge(first_in, 16 * len(first))

            def steps(s, r):
                if s == "patch":
                    wait_apart(pool, patch_stats.sem, patch_stats.at(r, 3 * NT), pool_passed)
                    inverse_root(rsA[:, 1, :], rsA[:, 0, :], mvA[:, :, 1], patch_rstd, r, 0, 1e-5)
                if s == "ln2":
                    wait_apart(pool, emb_stats.sem, emb_stats.at(r, 2 * NT), pool_passed)
                    inverse_root(rsA[:, 1, :], rsA[:, 0, :], mvA[:, :, 1], emb_rstd, r, 0, 1e-5)
                if s == "ln3":
                    wait_apart(pool, statsA.sem, statsA.at(r, 2 * NT), pool_passed)
                    inverse_root(rsA[:, 1, :], rsA[:, 0, :], mvA[:, :, 1], rstdA, r, 0, 1e-5)
                if s[0] == "M":
                    p = int(s[1:])
                    wait_apart(pool, mixvar.sem, mixvar.at(r, p + 1), pool_passed)
                    nc.gpsimd.tensor_scalar(var[:, 1, :], var[:, 0, :], 1.0 / H, 1e-3,
                                            ALU.mult, ALU.add).then_inc(mix_rstd.sem, 1)
                    pool.wait_ge(mix_rstd.sem, mix_rstd.at(r, 3 * p + 1))
                    nc.gpsimd.tensor_tensor(var[:, 2, :], var[:, 1, :], minus[0:PT, 0:L], ALU.pow).then_inc(mix_rstd.sem, 1)
                    pool.wait_ge(mix_rstd.sem, mix_rstd.at(r, 3 * p + 2))
                    if p:
                        pool.wait_ge(att_ready.sem, att_ready.at(r, 2 * p))
                    nc.gpsimd.tensor_tensor(own[:, :, :], var[:, 2, :].unsqueeze(1).to_broadcast([PT, 2, L]),
                                            C("own", PT).unsqueeze(2).to_broadcast([PT, 2, L]),
                                            ALU.mult).then_inc(mix_rstd.sem, 1)
                if s == "rk":
                    wait_apart(pool, ranked.sem, ranked.at(r, 6 + NT), pool_passed)
                    for e in range(2):
                        for j in range(NT):
                            nc.gpsimd.indirect_dma_start(
                                out=slot_x, out_offset=bass.IndirectOffsetOnAxis(ap=spot[:, e, j:j + 1], axis=0),
                                in_=xB[:, j, :], in_offset=None).then_inc(scattered.sem, 16)
                if s == "shN":
                    pool.wait_ge(scattered.sem, scattered.at(r, 16 * 2 * NT))
                    pool.sem_inc(xB_free.sem, 1)
                for g, name in enumerate(["outN", "leafN", "o1N"]):
                    if s == name:
                        st, rs, mv, done, k = (statsH, rsH, mvH, rstdH, 0) if g == 0 else (statsB, rsB, mvB, rstdB, g - 1)
                        wait_apart(pool, st.sem, st.at(r, 2 * NT * (k + 1)), pool_passed)
                        inverse_root(rs[:, 1, :], rs[:, 0, :], mv[:, :, 1], done, r, 2 * k, 1e-5)

            rounds(pool, steps)

        @block.scalar
        def _(act):
            def copy(dst, src, sem, **kw):
                nc.scalar.activation(dst, src, ACT.Identity, **kw).then_inc(sem.sem, 1)

            for dst, src in small:
                act.dma_start(dst, src).then_inc(small_in, 16)
            act.wait_ge(made, SETUP)

            def turn_in(xT, turned, ready, r, k, base=0):
                act.wait_ge(turned.sem, turned.at(r, k + 1))
                for m in range(DC):
                    copy(xT[:, m, :], bank[base + m][:, 0:TB], ready)

            def glueB(r, g, bias):
                for m in range(DC):
                    act.wait_ge(projB.sem, projB.at(r, 2 * g + m + 1))
                    if bias is None:
                        copy(yTB[:, m, :], bank[5 + m][:, 0:TB], projB_T)
                    else:
                        copy(yTB[:, m, :], bank[5 + m][:, 0:TB], projB_T, bias=bias[:, m:m + 1])

            def steps(s, r):
                if s == "turnp":
                    for k in range(KP):
                        act.wait_ge(patch_turned.sem, patch_turned.at(r, k + 1))
                        copy(wide[:, k, :], bank[3 + k % 2][:, 0:TB], patch_T)
                if s == "embed":
                    for m in range(DC):
                        act.wait_ge(emb.sem, emb.at(r, m + 1))
                        copy(yTA[:, m, :], bank[m][:, 0:TB], emb_T)
                if s == "xA":
                    turn_in(xTA, xA_turned, xTA_ready, r, 0)
                if s[:2] == "qk":
                    for c in range(2 * int(s[2:]), 2 * int(s[2:]) + 2):
                        act.wait_ge(qk_done.sem, qk_done.at(r, c + 1))
                        copy(qk[:, c, :], bank[c % 2][:, 0:TB], qk_ready, scale=DH ** -0.5 if c < QC else 1.0)
                if s[0] == "S":
                    p = int(s[1:])
                    act.wait_ge(sc_done.sem, sc_done.at(r, p + 1))
                    sv = sc[:, :, :].rearrange("q l (a e) -> q e a l", e=2)
                    for e in range(2):
                        copy(sv[:, e], bank[e][0:SP2, 0:8 * L].rearrange("q (a l) -> q a l", l=L), sc_ready)
                if s[0] == "T":
                    p = int(s[1:])
                    act.wait_ge(sm_steps.sem, sm_steps.at(r, 5 * p + 2))
                    nc.scalar.activation(prob[:, :, :], prob[:, :, :], ACT.Exp).then_inc(exp_done.sem, 1)
                if s[0] == "M":
                    p = int(s[1:])
                    act.wait_ge(mixed.sem, mixed.at(r, p + 1))
                    if p >= 2:
                        act.wait_ge(att_ready.sem, att_ready.at(r, 2 * (p - 1)))
                    for part, (i0, i1) in enumerate(((0, 32), (32, L))):
                        copy(mix[:, p % 2, i0 * H:i1 * H], bank[3 + part][0:PT, 0:(i1 - i0) * H], mix_copied)
                    act.wait_ge(mix_copied.sem, mix_copied.at(r, 2 * p + 2))
                    if p:
                        act.wait_ge(mixvar.sem, mixvar.at(r, p))
                    nc.scalar.activation(sq[:, :, :].rearrange("q i g -> q (i g)"), mix[:, p % 2, :],
                                         ACT.Square).then_inc(squared.sem, 1)
                if s == "outP":
                    for m in range(DC):
                        act.wait_ge(out0_done.sem, out0_done.at(r, m + 1))
                        copy(yTA[:, m, :], bank[m][:, 0:TB], out0_T, bias=b_out0[:, m:m + 1])
                if s == "outX":
                    turn_in(xTB, xB_turned, xTB_ready, r, 0)
                if s[0] == "z" and s != f"z{FC}":
                    c = int(s[1:])
                    act.wait_ge(z_done.sem, z_done.at(r, c + 1))
                    if c >= 2:
                        act.wait_ge(leaf_ready.sem, leaf_ready.at(r, c - 1))
                    copy(zb[:, c % 2, :], bank[5 + c % 2][:, 0:TB], z_half, scale=0.5, bias=b_tree2[:, c:c + 1])
                    act.wait_ge(z_half.sem, z_half.at(r, c + 1))
                    nc.scalar.activation(th[:, c % 2, :], zb[:, c % 2, :], ACT.Tanh).then_inc(z_tanh.sem, 1)
                if s == "leafP1":
                    glueB(r, 0, None)
                if s == "leafX":
                    turn_in(xTB, xB_turned, xTB_ready, r, 1, 5)
                if s == "q1a":
                    for c in (0, 1):
                        act.wait_ge(qkv1_done.sem, qkv1_done.at(r, c + 1))
                        copy(q1[:, c, :], bank[5 + c % 2][:, 0:TB], q1_ready, scale=0.25, bias=b_q1[:, c:c + 1])
                if s == "q1b":
                    for c in (2, 3):
                        act.wait_ge(qkv1_done.sem, qkv1_done.at(r, c + 1))
                        for a in range(4):
                            copy(k4[:, c - 2, a, :], bank[5 + c % 2][:, 0:TB], k1_ready, scale=C("head4")[:, a:a + 1],
                                 bias=b_k1[:, c - 2, a:a + 1])
                if s == "q1c":
                    for c in (4, 5):
                        act.wait_ge(qkv1_done.sem, qkv1_done.at(r, c + 1))
                        copy(v1[:, c - 4, :], bank[5 + c % 2][:, 0:TB], v1_ready, bias=b_in1[:, c:c + 1])
                if s[:2] == "s1":
                    p = int(s[3:])
                    act.wait_ge(sm1_steps.sem, sm1_steps.at(r, 4 * p + 4))
                    nc.scalar.activation(e1[:, p % 2, :, :], e1[:, p % 2, :, :], ACT.Exp).then_inc(exp1_done.sem, 1)
                if s == "o1P":
                    glueB(r, 1, b_out1)
                if s == "o1X":
                    turn_in(xTB, xB_turned, xTB_ready, r, 2, 5)
                if s[:2] == "sh" and s[2:].isdigit():
                    c = int(s[2:])
                    n = min(128, SH - 128 * c)
                    act.wait_ge(sh_done.sem, sh_done.at(r, 2 * c + 1))
                    if c >= 2:
                        act.wait_ge(sh_up.sem, sh_up.at(r, c - 1))
                    else:
                        act.wait_ge(leaf_ready.sem, leaf_ready.at(r, FC))
                    copy(zb[0:n, c % 2, :], bank[5][0:n, 0:TB], sh_half, scale=0.5, bias=b_sh12[0:n, c:c + 1])
                    act.wait_ge(sh_half.sem, sh_half.at(r, c + 1))
                    nc.scalar.activation(th[0:n, c % 2, :], zb[0:n, c % 2, :], ACT.Tanh).then_inc(sh_tanh.sem, 1)
                if s == "lg":
                    act.wait_ge(rt_steps.sem, rt_steps.at(r, NT + 2))
                    nc.scalar.activation(ex[:, :, :], ex[:, :, :], ACT.Exp).then_inc(rt_exp.sem, 1)
                if s == "shP":
                    glueB(r, 2, b_sh2)

            rounds(act, steps)

        @block.tensor
        def _(pe):
            def project(dst, weight, x, cols, chunks, sig_, rows=None, ready=None):
                for k in range(chunks):
                    if ready and k in (0, chunks - 2, chunks - 1):
                        pe.wait_ge(ready[0].sem, ready[0].at(ready[1], max(k + 1, chunks - 2)))
                    n = 128 if rows is None else min(128, rows - 128 * k)
                    last = nc.tensor.matmul(dst, weight[0:n, k, cols], x[0:n, k, :], start=k == 0, stop=k == chunks - 1)
                last.then_inc(sig_.sem, 1)

            def turn_out(yT, b0, turned):
                for j in range(NT):
                    for m in range(DC):
                        last = nc.tensor.transpose(bank[b0 + j // 2][0:TT, (j % 2) * D + m * 128:(j % 2) * D + (m + 1) * 128],
                                                   yT[:, m, j * TT:(j + 1) * TT], ident)
                last.then_inc(turned.sem, 1)

            def turn_back(x, b0, turned):
                for j in range(NT):
                    for m in range(DC):
                        last = nc.tensor.transpose(bank[b0 + m][:, j * TT:(j + 1) * TT],
                                                   x[:, j, m * 128:(m + 1) * 128], ident[0:TT, 0:TT])
                last.then_inc(turned.sem, 1)

            pe.wait_ge(first_in, 16 * len(first))
            pe.wait_ge(made, SETUP)

            def outB(r, g):
                pe.wait_ge(projB_T.sem, projB_T.at(r, 2 * g + 2))
                turn_out(yTB, 5, projB_turned)

            def backB(r, g):
                pe.wait_ge(xB_ready.sem, xB_ready.at(r, NT * (g + 1)))
                turn_back(xB, 5, xB_turned)

            def path(r, c):
                pe.wait_ge(decided.sem, decided.at(r, c // 2 + 1))
                if c:
                    pe.wait_ge(leaf_ready.sem, leaf_ready.at(r, c))
                nc.tensor.matmul(bank[7][:, 0:TB], toward[:, (c % 2) * 128:(c % 2 + 1) * 128], dec[:, :],
                                 start=True, stop=True).then_inc(path_done.sem, 1)

            def steps(s, r):
                if s == "turnp":
                    for j in range(NT):
                        pe.wait_ge(patch_norm.sem, patch_norm.at(r, j + 1))
                    for k in range(KP):
                        if k >= 2:
                            pe.wait_ge(patch_T.sem, patch_T.at(r, k - 1))
                        for j in range(NT):
                            last = nc.tensor.transpose(bank[3 + k % 2][:, j * TT:(j + 1) * TT],
                                                       patch[:, j, k * 128:(k + 1) * 128], ident[0:TT, 0:TT])
                        last.then_inc(patch_turned.sem, 1)
                if s == "embed":
                    if not isinstance(r, int) or r:
                        pe.wait_ge(hM_ready.sem, hM_ready.at(r - 1, NT))
                    for m in range(DC):
                        project(bank[m][:, 0:TB], w_tok, wide, slice(m * 128, (m + 1) * 128), KP, emb, ready=(patch_T, r))
                if s == "turne":
                    pe.wait_ge(emb_T.sem, emb_T.at(r, 2))
                    turn_out(yTA, 0, emb_turned)
                if s == "xA":
                    pe.wait_ge(xA_ready.sem, xA_ready.at(r, NT))
                    turn_back(xA, 0, xA_turned)
                if s[:2] == "qk":
                    if s == "qk0":
                        pe.wait_ge(xTA_ready.sem, xTA_ready.at(r, 2))
                        if isinstance(r, int) and r == 0:
                            pe.wait_ge(qkv_in, 16)
                    for c in range(2 * int(s[2:]), 2 * int(s[2:]) + 2):
                        if c >= 2:
                            pe.wait_ge(qk_ready.sem, qk_ready.at(r, c - 1))
                        project(bank[c % 2][:, 0:TB], w_qkv, xTA, slice(c * 128, (c + 1) * 128), DC, qk_done)
                if s == "vsum":
                    pe.wait_ge(xsum_ready.sem, xsum_ready.at(r, 1))
                    for c in range(QC):
                        for k in range(DC):
                            last = nc.tensor.matmul(bank[2][:, c * IB:(c + 1) * IB],
                                                    w_qkv[:, k, 2 * INNER + c * 128:2 * INNER + (c + 1) * 128],
                                                    xsum[:, k, :], start=k == 0, stop=k == DC - 1)
                    last.then_inc(vsum_done.sem, 1)
                p = int(s[1:]) if s[0] in "SVTUMRNW" else 0
                if s[0] == "V":
                    for n in range(2):
                        if p:
                            pe.wait_ge(av_ready.sem, av_ready.at(r, 2 * (p - 1) + n + 1))
                        else:
                            pe.wait_ge(sc_ready.sem, sc_ready.at(r, n + 1))
                        for k in range(DC):
                            last = nc.tensor.matmul(bank[n][0:PT, :], xTA[:, k, p * PT:(p + 1) * PT],
                                                    w_qkv[:, k, 2 * INNER + 512 * n:2 * INNER + 512 * (n + 1)],
                                                    start=k == 0, stop=k == DC - 1)
                        last.then_inc(v_done.sem, 1)
                if s[0] == "S":
                    if p:
                        wait_apart(pe, v_ready.sem, v_ready.at(r, 2 * p), pe_passed)
                    else:
                        if not isinstance(r, int) or r:
                            pe.wait_ge(xTB_ready.sem, xTB_ready.at(r - 1, 2))
                        pe.wait_ge(vbias_ready.sem, vbias_ready.at(r, 1))
                        wait_apart(pe, qk_ready.sem, qk_ready.at(r, 2 * QC), pe_passed)
                    for h in range(H):
                        row = slice(64 * (h % 2), 64 * (h % 2) + 64)
                        for m in range(2):
                            t = slice(p * PT + m * L, p * PT + (m + 1) * L)
                            last = nc.tensor.matmul(bank[h % 2][SLOT * m:SLOT * m + L, (h // 2) * L:(h // 2 + 1) * L],
                                                    qk[row, QC + h // 2, t], qk[row, h // 2, t], start=True, stop=True)
                    last.then_inc(sc_done.sem, 1)
                if s[0] == "T":
                    pe.wait_ge(sc_ready.sem, sc_ready.at(r, 2 * p + 2))
                    for c in range(NG):
                        w = IG if c < NG - 1 else LAST
                        last = nc.tensor.transpose(bank[2][0:H * w, c * SP2:(c + 1) * SP2],
                                                   sc[:, c * IG:c * IG + w, :].rearrange("q i h -> q (i h)"),
                                                   ident[0:SP2, 0:SP2])
                    last.then_inc(sc_turned.sem, 1)
                if s[0] == "M":
                    if p:
                        pe.wait_ge(mix_copied.sem, mix_copied.at(r, 2 * p))
                    pe.wait_ge(sm_steps.sem, sm_steps.at(r, 5 * p + 5))
                    for c in range(NG):
                        w = IG if c < NG - 1 else LAST
                        dst = bank[3][0:PT, c * 128:(c + 1) * 128] if c < NG - 1 else bank[4][0:PT, 0:H * w]
                        mat = mix8[0:H * w, 0:w, :].rearrange("p i g -> p (i g)")
                        last = nc.tensor.matmul(dst, prob[0:H * w, c, :], mat, start=True, stop=True)
                    last.then_inc(mixed.sem, 1)
                if s[0] == "W":
                    pe.wait_ge(att_ready.sem, att_ready.at(r, 2 * p + 2))
                    pe.wait_ge(v_ready.sem, v_ready.at(r, 2 * p + 2))
                    pe.wait_ge(sc_ready.sem, sc_ready.at(r, min(2 * p + 4, 2 * PAIRS)))
                    for half in range(2):
                        for g in range(8 * half, 8 * half + 8):
                            at = (g // 2 - 4 * half) * PT
                            last = nc.tensor.matmul(bank[half][64 * (g % 2):64 * (g % 2) + 64, at:at + PT],
                                                    val[:, g * DH:(g + 1) * DH],
                                                    att[:, g, :, :].rearrange("q m i -> q (m i)"), start=True, stop=True)
                        last.then_inc(av_done.sem, 1)
                if s == "outP":
                    if isinstance(r, int) and r == 0:
                        pe.wait_ge(rest_in, 16 * len(rest))
                    pe.wait_ge(av_ready.sem, av_ready.at(r, 2 * PAIRS))
                    for m in range(DC):
                        project(bank[m][:, 0:TB], w_out0, wide, slice(m * 128, (m + 1) * 128), QC, out0_done)
                if s == "outT":
                    pe.wait_ge(out0_T.sem, out0_T.at(r, 2))
                    turn_out(yTA, 0, out0_turned)
                if s == "outX":
                    if not isinstance(r, int) or r < NB - 1:
                        pe.wait_ge(qk_ready.sem, qk_ready.at(r + 1, 2 * QC))
                    pe.wait_ge(xH_ready.sem, xH_ready.at(r, NT))
                    turn_back(xA, 0, xB_turned)
                if s[0] == "z" and s != f"z{FC}":
                    c = int(s[1:])
                    if c == 0:
                        pe.wait_ge(xTB_ready.sem, xTB_ready.at(r, 2))
                        pe.wait_ge(hB_ready.sem, hB_ready.at(r, 0))
                    if c >= 2:
                        pe.wait_ge(z_half.sem, z_half.at(r, c - 1))
                    project(bank[5 + c % 2][:, 0:TB], w_tree, xTB, slice(c * 128, (c + 1) * 128), DC, z_done)
                    if c:
                        path(r, c - 1)
                if s == f"z{FC}":
                    path(r, FC - 1)
                if s == "leafP0":
                    project(bank[5][:, 0:TB], w_leaf, big, slice(0, 128), FC, projB, ready=(leaf_ready, r))
                if s == "leafP1":
                    project(bank[6][:, 0:TB], w_leaf, big, slice(128, 256), FC, projB)
                if s == "leafT":
                    outB(r, 0)
                if s == "leafX":
                    backB(r, 0)
                if s == "q1a":
                    pe.wait_ge(xTB_ready.sem, xTB_ready.at(r, 4))
                if s[:2] == "q1":
                    for c in {"a": (0, 1), "b": (2, 3), "c": (4, 5)}[s[2]]:
                        if c in (2, 3):
                            pe.wait_ge(q1_ready.sem, q1_ready.at(r, c - 1))
                        if c in (4, 5):
                            pe.wait_ge(k1_ready.sem, k1_ready.at(r, 4 * (c - 3)))
                        project(bank[5 + c % 2][:, 0:TB], w_in1, xTB, slice(c * 128, (c + 1) * 128), DC, qkv1_done)
                if s[:2] == "s1":
                    p = int(s[3:])
                    if p:
                        wait_apart(pe, sm1_steps.sem, sm1_steps.at(r, 4 * p), pe_passed)
                    else:
                        wait_apart(pe, v1_ready.sem, v1_ready.at(r, 2), pe_passed)
                    for h in range(H):
                        c, b, a = h // 8, (h // 4) % 2, h % 4
                        for m in range(2):
                            t = slice(p * PT + m * L, p * PT + (m + 1) * L)
                            last = nc.tensor.matmul(bank[5 + b][SLOT * m:SLOT * m + L, (4 * c + a) * L:(4 * c + a + 1) * L],
                                                    q1[64 * b:64 * b + 64, c, t], k4[64 * b:64 * b + 64, c, a, t],
                                                    start=True, stop=True)
                    last.then_inc(sc1_done.sem, 1)
                if s[:2] == "r1":
                    p = int(s[3:])
                    pe.wait_ge(sum1_steps.sem, sum1_steps.at(r, 4 * p + 4))
                    if p:
                        pe.wait_ge(o1_ready.sem, o1_ready.at(r, p))
                    for c in range(DC):
                        last = nc.tensor.matmul(bank[7][:, c * PT:(c + 1) * PT],
                                                r1[:, c * 8:(c + 1) * 8, :].rearrange("q h d -> q (h d)"),
                                                C("pair", SP2), start=True, stop=True)
                    last.then_inc(r1_turned.sem, 1)
                if s == "o1P":
                    pe.wait_ge(o1_ready.sem, o1_ready.at(r, PAIRS))
                    for m in range(DC):
                        project(bank[5 + m][:, 0:TB], w_out1, o1, slice(m * 128, (m + 1) * 128), DC, projB)
                if s == "o1T":
                    outB(r, 1)
                if s == "o1X":
                    backB(r, 1)
                if s[:2] == "sh" and s[2:].isdigit():
                    c = int(s[2:])
                    n = min(128, SH - 128 * c)
                    if c:
                        pe.wait_ge(sh_half.sem, sh_half.at(r, c))
                    else:
                        pe.wait_ge(xTB_ready.sem, xTB_ready.at(r, 6))
                    project(bank[5][0:n, 0:TB], w_sh1, xTB, slice(c * 128, c * 128 + n), DC, sh_done)
                    if c:
                        pe.wait_ge(sh_up.sem, sh_up.at(r, c))
                    project(bank[6][0:n, 0:TB], w_sh3, xTB, slice(c * 128, c * 128 + n), DC, sh_done)
                if s == "lg":
                    for j in range(NT):
                        for k in range(DC):
                            last = nc.tensor.matmul(bank[7][0:TT, j * E_:(j + 1) * E_], xTB[:, k, j * TT:(j + 1) * TT],
                                                    w_gate[:, k, :], start=k == 0, stop=k == DC - 1)
                    last.then_inc(lg_done.sem, 1)
                if s == "rk":
                    pe.wait_ge(rt_steps.sem, rt_steps.at(r, LOOKED_UP))
                    for j in range(NT):
                        dst = bank[7][0:TT, 64 + j * E_:64 + (j + 1) * E_]
                        nc.tensor.matmul(dst, C("below", TT), both[:, j, :], start=True, stop=False)
                        for e in range(j):
                            nc.tensor.matmul(dst, C("ones", TT)[:, 0:TT], both[:, e, :], start=False, stop=False)
                        last = nc.tensor.matmul(dst, C("ones", TT)[:, 0:TT], load[:, :], start=False, stop=True)
                    last.then_inc(rank_done.sem, 1)
                if s == "shP":
                    pe.wait_ge(sh_half.sem, sh_half.at(r, SC))
                    project(bank[5][:, 0:TB], w_sh2, up, slice(0, 128), SC, projB, rows=SH, ready=(sh_up, r))
                    project(bank[6][:, 0:TB], w_sh2, up, slice(128, 256), SC, projB, rows=SH)
                if s == "shT":
                    outB(r, 2)

            rounds(pe, steps)

        @block.vector
        def _(dve):
            v = nc.vector

            n = [0]

            def step(ins):
                n[0] += 1
                ins.then_inc(made, 1)
                dve.wait_ge(made, n[0])

            step(v.memset(load[:, :], 0.0))
            step(v.memset(sc[:, :, :], 0.0))
            for i in range(8):
                step(v.memset(bank[i][:, :], 0.0))
            dve.wait_ge(small_in, 16 * len(small))
            dve.wait_ge(first_in, 16 * len(first))
            for k in range(KP):
                step(v.tensor_scalar(w_tok[:, k, :], w_tok[:, k, :], g_ln1[:, k:k + 1], None, ALU.mult))
            step(v.tensor_reduce(wm[:, 0:1], wx[:, :], X, ALU.add, negate=True))
            step(v.tensor_scalar(wm[:, 1:2], wm[:, 0:1], 1.0 / H, None, ALU.mult))
            step(v.tensor_scalar(wx[:, :], wx[:, :], wm[:, 1:2], None, ALU.add))
            step(v.tensor_tensor(mix8[:, :, :], wx[:, :].unsqueeze(1).to_broadcast([128, IG, H]),
                                 C("query").unsqueeze(2).to_broadcast([128, IG, H]), ALU.mult))
            step(v.tensor_scalar(b_tree2[:, :], b_tree[:, :], 0.5, None, ALU.mult))
            step(v.tensor_scalar(b_sh12[:, :], b_sh1[:, :], 0.5, None, ALU.mult))
            for c in range(DC):
                step(v.tensor_scalar(b_k1[:, c, :], C("head4"), b_in1[:, 2 + c:3 + c], None, ALU.mult))
            step(v.tensor_scalar(b_q1[:, :], b_in1[:, 0:2], 0.25, None, ALU.mult))
            step(v.tensor_copy(toward[:, :], toward32))
            assert n[0] == SETUP, n[0]

            def stats(srcs, sts, mv, sig_, r, k):
                for src, st in zip(srcs, sts):
                    v.bn_stats(st, src).then_inc(sig_.sem, 1)
                wait_apart(dve, sig_.sem, sig_.at(r, k + len(srcs)), dve_passed)
                for j, st in enumerate(sts):
                    v.bn_aggr(mv[:, j, :], st).then_inc(sig_.sem, 1)

            def norm(dst, src, mv, rs, j, sig_):
                v.tensor_scalar(dst, src, mv[:, j, 0:1], rs[:, 1, j:j + 1], ALU.subtract, ALU.mult).then_inc(sig_.sem, 1)

            def add(r, dst, old, base, turned, tk, sem):
                dve.wait_ge(turned.sem, turned.at(r, tk))
                for j in range(NT):
                    v.tensor_tensor(dst[:, j, :], bank[base + j // 2][0:TT, (j % 2) * D:(j % 2 + 1) * D],
                                    old[:, j, :], ALU.add).then_inc(sem.sem, 1)

            def measured(r, k, src, ready, st, mv, stats_):
                dve.wait_ge(ready.sem, ready.at(r, NT * (k + 1)))
                stats([src[:, j, :] for j in range(NT)], [st[:, j, :] for j in range(NT)], mv, stats_, r, 2 * NT * k)

            def normed(r, k, x, x_ready, src, mv, rs, stats_, rstd):
                dve.wait_ge(stats_.sem, stats_.at(r, 2 * NT * (k + 1)))
                dve.wait_ge(rstd.sem, rstd.at(r, 2 * (k + 1)))
                for j in range(NT):
                    norm(x[:, j, :], src[:, j, :], mv, rs, j, x_ready)

            def steps(s, r):
                if s == "patch":
                    dve.wait_ge(patch_in.sem, patch_in.at(r, 16))
                    for j in range(NT):
                        for e in range(2):
                            v.bn_stats(stA[:, j, 6 * e:6 * e + 6], patch[:, j, 384 * e:384 * e + 384]).then_inc(patch_stats.sem, 1)
                    wait_apart(dve, patch_stats.sem, patch_stats.at(r, 2 * NT), dve_passed)
                    for j in range(NT):
                        v.bn_aggr(mvA[:, j, :], stA[:, j, :]).then_inc(patch_stats.sem, 1)
                if s == "patchM":
                    dve.wait_ge(patch_stats.sem, patch_stats.at(r, 3 * NT))
                    dve.wait_ge(patch_rstd.sem, patch_rstd.at(r, 2))
                    for j in range(NT):
                        norm(patch[:, j, :], patch[:, j, :], mvA, rsA, j, patch_norm)
                if s == "ln2":
                    dve.wait_ge(emb_turned.sem, emb_turned.at(r, 1))
                    dve.wait_ge(patch_norm.sem, patch_norm.at(r, NT))
                    stats([bank[j // 2][0:TT, (j % 2) * D:(j % 2 + 1) * D] for j in range(NT)],
                          [stA[:, j, 0:6] for j in range(NT)], mvA, emb_stats, r, 0)
                if s == "ln3":
                    dve.wait_ge(emb_stats.sem, emb_stats.at(r, 2 * NT))
                    dve.wait_ge(emb_rstd.sem, emb_rstd.at(r, 2))
                    pos = C("pos", TT).rearrange("p (j d) -> p j d", j=NT)
                    for j in range(NT):
                        v.scalar_tensor_tensor(hA[:, j, :], bank[j // 2][0:TT, (j % 2) * D:(j % 2 + 1) * D],
                                               mvA[:, j, 0:1], g_ln2[:, :], ALU.subtract, ALU.mult).then_inc(emb_steps.sem, 1)
                    for j in range(NT):
                        dve.wait_ge(emb_steps.sem, emb_steps.at(r, j + 1))
                        v.scalar_tensor_tensor(hA[:, j, :], hA[:, j, :], rsA[:, 1, j:j + 1], pos[:, j, :],
                                               ALU.mult, ALU.add).then_inc(emb_steps.sem, 1)
                    dve.wait_ge(emb_steps.sem, emb_steps.at(r, 2 * NT))
                    stats([hA[:, j, :] for j in range(NT)], [stA[:, j, 0:6] for j in range(NT)], mvA, statsA, r, 0)
                if s == "ln4":
                    dve.wait_ge(statsA.sem, statsA.at(r, 2 * NT))
                    dve.wait_ge(rstdA.sem, rstdA.at(r, 2))
                    for j in range(NT):
                        norm(xA[:, j, :], hA[:, j, :], mvA, rsA, j, xA_ready)
                if s == "qk0":
                    dve.wait_ge(xTA_ready.sem, xTA_ready.at(r, 2))
                    v.tensor_reduce(xsum[:, :, :], xTA[:, :, :].rearrange("p c (m l) -> p c m l", m=IB), X,
                                    ALU.add).then_inc(xsum_ready.sem, 1)
                if s == "vsum":
                    dve.wait_ge(vsum_done.sem, vsum_done.at(r, 1))
                    v.tensor_tensor(vbias[:, :, :], bank[2][:, 0:QC * IB].rearrange("p (c m) -> p c m", c=QC),
                                    b_head[:, :].unsqueeze(2).to_broadcast([128, QC, IB]), ALU.mult).then_inc(vbias_ready.sem, 1)
                p = int(s[1:]) if s[0] in "SVTUMRNW" else 0
                if s[0] == "V":
                    for e in range(2):
                        dve.wait_ge(v_done.sem, v_done.at(r, 2 * p + e + 1))
                        v.tensor_tensor(val[:, 512 * e:512 * (e + 1)].rearrange("q (h d) -> q h d", h=8),
                                        bank[e][0:PT, :].rearrange("q (h d) -> q h d", h=8),
                                        g_head[:, 8 * e:8 * e + 8].unsqueeze(2).to_broadcast([PT, 8, DH]),
                                        ALU.mult).then_inc(v_ready.sem, 1)
                if s[0] == "T":
                    dve.wait_ge(sc_turned.sem, sc_turned.at(r, p + 1))
                    full = bank[2][:, 0:NG * SP2].rearrange("q (c s) -> q c s", s=SP2)
                    pv = prob[:, :, :].rearrange("q c (m l) -> q c m l", m=2)
                    k = 5 * p
                    view = two_images(full)
                    v.tensor_reduce(pmax[:, 0], view, X, ALU.max).then_inc(sm_steps.sem, 1)
                    dve.wait_ge(sm_steps.sem, sm_steps.at(r, k + 1))
                    v.tensor_tensor(pv, view, pmax[:, 0].unsqueeze(3).to_broadcast([128, NG, 2, L]),
                                    ALU.subtract).then_inc(sm_steps.sem, 1)
                if s[0] == "U":
                    pv = prob[:, :, :].rearrange("q c (m l) -> q c m l", m=2)
                    k = 5 * p
                    dve.wait_ge(exp_done.sem, exp_done.at(r, p + 1))
                    v.tensor_reduce(pmax[:, 1], pv, X, ALU.add).then_inc(sm_steps.sem, 1)
                    dve.wait_ge(sm_steps.sem, sm_steps.at(r, k + 3))
                    v.reciprocal(pmax[:, 2], pmax[:, 1]).then_inc(sm_steps.sem, 1)
                    dve.wait_ge(sm_steps.sem, sm_steps.at(r, k + 4))
                    v.tensor_tensor(pv, pv, pmax[:, 2].unsqueeze(3).to_broadcast([128, NG, 2, L]),
                                    ALU.mult).then_inc(sm_steps.sem, 1)
                if s[0] == "R":
                    dve.wait_ge(squared.sem, squared.at(r, p + 1))
                    if p:
                        dve.wait_ge(mix_rstd.sem, mix_rstd.at(r, 3 * p))
                    v.tensor_reduce(var[:, 0, :], sq[:, :, :], X, ALU.add).then_inc(mixvar.sem, 1)
                if s[0] == "N":
                    dve.wait_ge(mix_rstd.sem, mix_rstd.at(r, 3 * p + 3))
                    for part, (i0, i1) in enumerate(((0, 32), (32, L))):
                        n = i1 - i0
                        src = mix[:, p % 2, i0 * H:i1 * H].rearrange("q (i g) -> q g i", g=H)
                        v.tensor_tensor(att[:, :, :, i0:i1], src.unsqueeze(2).to_broadcast([PT, H, 2, n]),
                                        own[:, :, i0:i1].unsqueeze(1).to_broadcast([PT, H, 2, n]),
                                        ALU.mult).then_inc(att_ready.sem, 1)
                if s[0] == "W":
                    for half in range(2):
                        dve.wait_ge(av_done.sem, av_done.at(r, 2 * p + half + 1))
                        bias = vbias[:, 4 * half:4 * half + 4, 2 * p:2 * p + 2].unsqueeze(3).to_broadcast([128, 4, 2, L])
                        v.tensor_tensor(wide[:, 4 * half:4 * half + 4, p * PT:(p + 1) * PT].rearrange("q c (m l) -> q c m l", m=2),
                                        bank[half][:, 0:4 * PT].rearrange("q (c m l) -> q c m l", c=4, m=2),
                                        bias, ALU.add).then_inc(av_ready.sem, 1)
                if s == "outN":
                    add(r, hM, hA, 0, out0_turned, 1, hM_ready)
                    measured(r, 0, hM, hM_ready, stH, mvH, statsH)
                if s == "outM":
                    normed(r, 0, xA, xH_ready, hM, mvH, rsH, statsH, rstdH)
                if s[0] == "z":
                    e = int(s[1:]) - 1
                    if e >= 0:
                        dve.wait_ge(z_half.sem, z_half.at(r, e + 1))
                        if e % 2 == 0:
                            v.tensor_scalar(dec[:, :], zb[:, e % 2, :], 0.0, None, ALU.is_gt).then_inc(decided.sem, 1)
                            dve.wait_ge(decided.sem, decided.at(r, e // 2 + 1))
                        dve.wait_ge(z_tanh.sem, z_tanh.at(r, e + 1))
                        v.scalar_tensor_tensor(zb[:, e % 2, :], th[:, e % 2, :], 1.0, zb[:, e % 2, :],
                                               ALU.add, ALU.mult).then_inc(z_silu.sem, 1)
                        dve.wait_ge(z_silu.sem, z_silu.at(r, e + 1))
                        dve.wait_ge(path_done.sem, path_done.at(r, e + 1))
                        if e == 8:
                            dve.wait_ge(spilled_h.sem, spilled_h.at(r, 0))
                        v.scalar_tensor_tensor(big[:, e, :], bank[7][:, 0:TB], C("right")[:, e % 2:e % 2 + 1],
                                               zb[:, e % 2, :], ALU.is_equal, ALU.mult).then_inc(leaf_ready.sem, 1)
                if s == "leafN":
                    add(r, hB, hM, 5, projB_turned, 1, hB_ready)
                    measured(r, 0, hB, hB_ready, stB, mvB, statsB)
                if s == "leafM":
                    dve.wait_ge(xB_free.sem, xB_free.at(r, 0))
                    normed(r, 0, xB, xB_ready, hB, mvB, rsB, statsB, rstdB)
                if s[:2] == "s1":
                    p = int(s[3:])
                    dve.wait_ge(sc1_done.sem, sc1_done.at(r, p + 1))
                    for b in range(2):
                        src = bank[5 + b][0:SP2, 0:8 * L].rearrange("q (h l) -> q h l", l=L)
                        v.tensor_reduce(m1[:, 0, 8 * b:8 * b + 8], src, X, ALU.max).then_inc(sm1_steps.sem, 1)
                    dve.wait_ge(sm1_steps.sem, sm1_steps.at(r, 4 * p + 2))
                    for b in range(2):
                        src = bank[5 + b][0:SP2, 0:8 * L].rearrange("q (h l) -> q h l", l=L)
                        v.tensor_tensor(e1[:, p % 2, 8 * b:8 * b + 8, :], src,
                                        m1[:, 0, 8 * b:8 * b + 8].unsqueeze(2).to_broadcast([SP2, 8, L]),
                                        ALU.subtract).then_inc(sm1_steps.sem, 1)
                if s[:2] == "r1":
                    p = int(s[3:])
                    dve.wait_ge(exp1_done.sem, exp1_done.at(r, p + 1))
                    v.tensor_reduce(m1[:, 1, :], e1[:, p % 2, :, :], X, ALU.add).then_inc(sum1_steps.sem, 1)
                    dve.wait_ge(sum1_steps.sem, sum1_steps.at(r, 4 * p + 1))
                    v.reciprocal(m1[:, 2, :], m1[:, 1, :]).then_inc(sum1_steps.sem, 1)
                    dve.wait_ge(sum1_steps.sem, sum1_steps.at(r, 4 * p + 2))
                    for b in range(2):
                        bb = slice(8 * b, 8 * b + 8)
                        dst = r1[:, :, :].rearrange("q (c b a) d -> q b c a d", c=2, b=2)[:, b]
                        v.tensor_tensor(dst, m1[:, 1, bb].rearrange("q (c a) -> q c a", c=2).unsqueeze(3).to_broadcast([SP2, 2, 4, 16]),
                                        m1[:, 2, bb].rearrange("q (c a) -> q c a", c=2).unsqueeze(3).to_broadcast([SP2, 2, 4, 16]),
                                        ALU.mult).then_inc(sum1_steps.sem, 1)
                if s[:2] == "p1":
                    p = int(s[3:])
                    dve.wait_ge(r1_turned.sem, r1_turned.at(r, p + 1))
                    dve.wait_ge(v1_ready.sem, v1_ready.at(r, 2))
                    tok = slice(p * PT, (p + 1) * PT)
                    v.tensor_tensor(o1[:, :, tok], v1[:, :, tok], bank[7][:, 0:2 * PT].rearrange("q (c t) -> q c t", c=DC),
                                    ALU.mult).then_inc(o1_ready.sem, 1)
                if s == "o1N":
                    add(r, hB, hB, 5, projB_turned, 2, hB_ready)
                    measured(r, 1, hB, hB_ready, stB, mvB, statsB)
                if s == "o1M":
                    normed(r, 1, xB, xB_ready, hB, mvB, rsB, statsB, rstdB)
                if s[:2] == "sh" and s[2:].isdigit():
                    c = int(s[2:])
                    nn = min(128, SH - 128 * c)
                    dve.wait_ge(sh_half.sem, sh_half.at(r, c + 1))
                    dve.wait_ge(sh_tanh.sem, sh_tanh.at(r, c + 1))
                    v.scalar_tensor_tensor(zb[0:nn, c % 2, :], th[0:nn, c % 2, :], 1.0, zb[0:nn, c % 2, :],
                                           ALU.add, ALU.mult).then_inc(sh_silu.sem, 1)
                    dve.wait_ge(sh_silu.sem, sh_silu.at(r, c + 1))
                    dve.wait_ge(sh_done.sem, sh_done.at(r, 2 * c + 2))
                    v.scalar_tensor_tensor(up[0:nn, c, :], bank[6][0:nn, 0:TB], b_sh3[0:nn, c:c + 1], zb[0:nn, c % 2, :],
                                           ALU.add, ALU.mult).then_inc(sh_up.sem, 1)
                if s in ("lg", "lh"):
                    gates(r, ("lg", "lh").index(s))
                if s == "rk":
                    ranks(r)
                if s == "shN":
                    add(r, hout, hB, 5, projB_turned, 3, hB_ready)

            def two_images(full):
                return bass.AP(full.tensor, full.offset, [list(full.ap[0]), list(full.ap[1]), [SLOT, 2], [1, L]])

            def gates(r, part):
                at = [part * (NT + 2)]

                def do(ins):
                    at[0] += 1
                    ins.then_inc(rt_steps.sem, 1)

                def own_wait():
                    dve.wait_ge(rt_steps.sem, rt_steps.at(r, at[0]))

                g = bass.ds(r * NT, NT)
                tile_by_expert = [TT, NT, E_]
                if part == 0:
                    dve.wait_ge(lg_done.sem, lg_done.at(r, 1))
                    do(v.tensor_tensor(lg[:, :, :], bank[7][0:TT, 0:NT * E_].rearrange("q (j e) -> q j e", j=NT),
                                       b_gate[:, :].unsqueeze(1).to_broadcast(tile_by_expert), ALU.add))
                    wait_apart(dve, rt_steps.sem, rt_steps.at(r, at[0]), dve_passed)
                    for j in range(NT):
                        do(v.max(top[:, j, :], lg[:, j, :]))
                    own_wait()
                    do(v.tensor_tensor(ex[:, :, :], lg[:, :, :], top[:, :, 0:1].to_broadcast(tile_by_expert), ALU.subtract))
                    assert at[0] == NT + 2
                    return
                for j in range(NT):
                    do(v.max_index(topi[:, j, :], top[:, j, :], lg[:, j, :]))
                own_wait()
                do(v.tensor_copy(topf[:, :, :], topi[:, :, 0:2]))
                own_wait()
                for e in range(2):
                    do(v.tensor_tensor(oh[:, e, g, :], C("iota", TT).unsqueeze(1).to_broadcast(tile_by_expert),
                                       topf[:, :, e:e + 1].to_broadcast(tile_by_expert), ALU.is_equal))
                own_wait()
                do(v.tensor_tensor(both[:, :, :], oh[:, 0, g, :], oh[:, 1, g, :], ALU.add))
                dve.wait_ge(rt_exp.sem, rt_exp.at(r, 1))
                do(v.tensor_reduce(gsum[:, 0, :], ex[:, :, :], X, ALU.add))
                own_wait()
                assert at[0] == LOOKED_UP
                do(v.reciprocal(gsum[:, 1, :], gsum[:, 0, :]))
                for e in range(2):
                    do(v.tensor_tensor(pick[:, e, :, :], oh[:, e, g, :], ex[:, :, :], ALU.mult))
                own_wait()
                for e in range(2):
                    do(v.tensor_reduce(gsum[:, 2 + e, :], pick[:, e, :, :], X, ALU.add))
                own_wait()
                for e in range(2):
                    do(v.tensor_tensor(gate[:, e, g], gsum[:, 2 + e, :], gsum[:, 1, :], ALU.mult))
                assert at[0] == RT_STEPS

            def ranks(r):
                g = bass.ds(r * NT, NT)
                dve.wait_ge(rank_done.sem, rank_done.at(r, 1))
                dve.wait_ge(rt_steps.sem, rt_steps.at(r, RT_STEPS))
                for e in range(2):
                    v.tensor_tensor(pick[:, e, :, :], oh[:, e, g, :],
                                    bank[7][0:TT, 64:64 + NT * E_].rearrange("q (j e) -> q j e", j=NT),
                                    ALU.mult).then_inc(ranked.sem, 1)
                for j in range(NT):
                    dve.wait_ge(ranked.sem, ranked.at(r, 2 + j))
                    v.tensor_tensor(load[:, :], load[:, :], both[:, j, :], ALU.add).then_inc(ranked.sem, 1)
                dve.wait_ge(ranked.sem, ranked.at(r, 2 + NT))
                for e in range(2):
                    v.tensor_reduce(rank[:, e, g], pick[:, e, :, :], X, ALU.add).then_inc(ranked.sem, 1)
                dve.wait_ge(ranked.sem, ranked.at(r, 4 + NT))
                for e in range(2):
                    v.scalar_tensor_tensor(spot[:, e, :], topf[:, :, e], float(REGION), rank[:, e, g],
                                           ALU.mult, ALU.add).then_inc(ranked.sem, 1)

            rounds(dve, steps)


def phase2(nc, dram, out_dram, bank, we, we_in, oh, gate, rank, load, C, spill_h, slot_x, slot_y, bias_parts, semaphore):
    ctx = ExitStack()
    with ctx:
        def sb(name, shape, dt=F32):
            return ctx.enter_context(nc.sbuf_tensor(name, shape, dt))

        RING = 3
        ROUNDS = (TILES - 3) // 6
        assert TILES == 3 + 6 * ROUNDS
        flat = we[0:TT, :, :].rearrange("p e n -> p (e n)")
        back = flat[:, 0:2 * GT * D].rearrange("p (g d) -> p g d", d=D)
        h = flat[:, 2 * GT * D:3 * GT * D].rearrange("p (g d) -> p g d", d=D)
        zero = sb("zero", [128, D])
        ones3 = sb("ones3", [3, 128], BF16)
        b32 = sb("b32", [E_, EB])
        parts = sb("parts", [E_, 3, EB], BF16)
        pad = sb("pad", [1, E_], I32)
        last1 = sb("last1", [1, 2], I32)
        last1f = sb("last1f", [1, 2])
        counti = sb("counti", [E_, 128], I32)
        padded = sb("padded", [E_, 128])
        off = sb("off", [TT, E_])
        prod = sb("prod", [TT, 2 * GT, E_])
        posf = sb("posf", [TT, 2, 2 * GT])
        pos = sb("pos", [TT, 2 * GT], I32)
        reach = sb("reach", [1, TILES, E_])
        where = sb("where", [1, 4, TILES])
        tilei = sb("tilei", [1, 2, TILES], I32)
        xg = sb("xg", [128, 6, D])
        bg = sb("bg", [3, 6, EB], BF16)
        xgT = sb("xgT", [128, RING, DC, 128])
        ax = sb("ax", [128, RING, INTER])
        axT = sb("axT", [128, RING, IC, 128])
        yx = sb("yx", [128, RING, D])
        ident = C("ident")

        h_in = semaphore("h_in")
        b_in = semaphore("b_in")
        split = semaphore("split")
        parts_out = semaphore("parts_out")
        counted = semaphore("counted")
        placed = semaphore("placed")
        found = semaphore("found")
        offsets = semaphore("offsets")
        padded_out = semaphore("padded_out")
        xg_in = [semaphore(f"xg_in{i}") for i in range(6)]
        xg_turned = semaphore("xg_turned")
        xgT_ready = semaphore("xgT_ready")
        z1_done = semaphore("z1_done")
        z3_done = semaphore("z3_done")
        tanh_done = semaphore("tanh_done")
        silu_done = semaphore("silu_done")
        a_ready = semaphore("a_ready")
        a_turned = semaphore("a_turned")
        aT_ready = semaphore("aT_ready")
        y_done = semaphore("y_done")
        y_ready = semaphore("y_ready")
        y_out = [semaphore(f"y_out{i}") for i in range(RING)]
        gathered = [semaphore(f"gathered{i}") for i in range(GT // 2)]
        added = semaphore("added")
        stored = semaphore("stored")
        SPLIT = 7
        PADDED = 5
        PLACED = 20
        FOUND = 4

        class Tile:

            def __init__(self, i, o):
                self.i, self.o = i, o
                self.t, self.lap = i * 6 + o, i * 2 + o // RING
                self.j, self.k, self.b = o % 6, o % RING, o % 2
                self.round = i + o // 6

            def has(self, n):
                return not isinstance(self.i, int) or self.t >= n

            def before(self):
                return Tile(self.i, self.o - 1) if self.has(1) else None

            def after(self):
                return None if isinstance(self.i, int) and self.t == TILES - 1 else Tile(self.i, self.o + 1)

        def tiles(eng, tile):
            for o in range(9):
                tile(Tile(0, o))
            with eng.Fori(1, ROUNDS - 1) as i:
                for o in range(3, 9):
                    tile(Tile(i, o))
            for o in range(3, 9):
                tile(Tile(ROUNDS - 1, o))

        FINAL = Tile(ROUNDS - 1, 8)
        x_bank = bank[0][:, 0:D]
        z1_bank = [bank[1][:, 0:INTER], bank[2][:, 0:INTER]]
        z3_bank = [bank[3][:, 0:INTER], bank[4][:, 0:INTER]]
        a_bank = bank[6]
        y_bank = bank[7][:, 0:D]
        W3, W2 = 2 * INTER, 4 * INTER

        def pad_rows(eng, experts):
            eng.wait_ge(placed, PADDED)
            for e in experts:
                row = eng.value_load(pad[0:1, e:e + 1], min_val=0, max_val=E_ * REGION - 128)
                eng.dma_start(slot_x[bass.ds(row, 128), :], zero[:, :]).then_inc(padded_out, 16)

        block = ctx.enter_context(nc.Block())

        @block.sync
        def _(sp):
            sp.dma_start(b32[:, :], dram["b_e"]).then_inc(b_in, 16)
            sp.dma_start(we[:, MIDDLE:, :], dram["we"][MIDDLE:, :, :].rearrange("e p n -> p e n")).then_inc(we_in, 16)
            pad_rows(sp, range(0, E_, 2))
            sp.wait_ge(split, SPLIT)
            sp.dma_start(bias_parts, parts[:, :, :].rearrange("e k n -> e (k n)")).then_inc(parts_out, 16)
            sp.wait_ge(parts_out, 16)
            sp.wait_ge(padded_out, 16 * E_)

            def tile(x):
                if x.has(6):
                    sp.wait_ge(y_done, x.t - 5)
                e = sp.value_load(tilei[0:1, 0, bass.ds(x.t, 1)], min_val=0, max_val=E_ - 1)
                row = sp.value_load(tilei[0:1, 1, bass.ds(x.t, 1)], min_val=0, max_val=E_ * REGION - 128)
                sp.dma_start(xg[:, x.j, :], slot_x[bass.ds(row, 128), :]).then_inc(xg_in[x.j], 16)
                sp.dma_start(bg[:, x.j, :], bias_parts[bass.ds(e, 1), :].rearrange("a (k n) -> (a k) n", k=3)).then_inc(xg_in[x.j], 16)

            tiles(sp, tile)
            sp.wait_ge(y_done, TILES)
            sp.dma_start(h[:, :, :], spill_h.rearrange("(g p) d -> p g d", p=TT)).then_inc(h_in, 16)
            for g in range(GT):
                sp.wait_ge(added, 2 * g + 2)
                sp.dma_start(out_dram[g * TT:(g + 1) * TT, :], h[:, g, :]).then_inc(stored, 16)
            sp.wait_ge(stored, 16 * GT)

        @block.gpsimd
        def _(pool):
            pool.wait_ge(found, FOUND)
            for k in range(RING):
                pool.wait_ge(y_out[k], 16 * (TILES // RING))
            for g in range(GT):
                for e in range(2):
                    nc.gpsimd.indirect_dma_start(
                        out=back[:, e * GT + g, :], out_offset=None, in_=slot_y,
                        in_offset=bass.IndirectOffsetOnAxis(ap=pos[:, e * GT + g:e * GT + g + 1], axis=0),
                    ).then_inc(gathered[g // 2], 16)

        @block.tensor
        def _(pe):
            nc.tensor.matmul(bank[0][0:E_, 0:128], load[:, :], C("ones", TT), start=True, stop=True).then_inc(counted, 1)
            nc.tensor.matmul(bank[2][0:TT, 0:E_], C("ones", TT)[:, 0:TT], load[:, :], start=True, stop=True).then_inc(counted, 1)
            pe.wait_ge(placed, 4)
            nc.tensor.matmul(bank[1][0:TT, 0:E_], padded[:, 0:TT], C("below16", E_), start=True, stop=True).then_inc(offsets, 1)
            pe.wait_ge(placed, PLACED)
            pe.wait_ge(we_in, 16 * 3)

            last_e = [None]

            def expert(t):
                return pe.value_load(tilei[0:1, 0, bass.ds(t, 1)], min_val=0, max_val=E_ - 1)

            def weight(e, n, a, width):
                return we[0:n, bass.ds(e, 1), a:a + width].rearrange("p a n -> p (a n)")

            def turn(x):
                pe.wait_ge(xg_in[x.j], (x.round + 1) * 32)
                if x.has(1):
                    pe.wait_ge(xgT_ready, x.t)
                for m in range(DC):
                    last = nc.tensor.transpose(x_bank[:, m * 128:(m + 1) * 128], xg[:, x.j, m * 128:(m + 1) * 128], ident)
                last.then_inc(xg_turned, 1)

            def up(x, e, part):
                if part == 0:
                    pe.wait_ge(xgT_ready, x.t + 1)
                dst, done = ((z1_bank[x.b], z1_done), (z3_bank[x.b], z3_done))[part]
                if x.has(2):
                    pe.wait_ge((silu_done, a_ready)[part], x.t - 1)
                for m in range(DC):
                    nc.tensor.matmul(dst, xgT[:, x.k, m, :], weight(e, 128, part * W3 + m * INTER, INTER), start=m == 0, stop=False)
                nc.tensor.matmul(dst, ones3[:, :], bg[:, x.j, part * INTER:(part + 1) * INTER], start=False, stop=True).then_inc(done, 1)

            def turn_a(x):
                pe.wait_ge(a_ready, x.t + 1)
                if x.has(1):
                    pe.wait_ge(aT_ready, x.t)
                for c in range(IC):
                    n = min(128, INTER - 128 * c)
                    last = nc.tensor.transpose(a_bank[0:n, c * 128:(c + 1) * 128], ax[:, x.k, c * 128:c * 128 + n], ident)
                last.then_inc(a_turned, 1)

            def down(x, e):
                pe.wait_ge(aT_ready, x.t + 1)
                if x.has(1):
                    pe.wait_ge(y_ready, x.t)
                for c in range(IC):
                    n = min(128, INTER - 128 * c)
                    nc.tensor.matmul(y_bank, axT[0:n, x.k, c, :], weight(e, n, W2 + c * D, D), start=c == 0, stop=False)
                nc.tensor.matmul(y_bank, ones3[:, :], bg[:, x.j, 2 * INTER:EB], start=False, stop=True).then_inc(y_done, 1)

            def tile(x):
                e = expert(x.t)
                up(x, e, 0)
                if x.before():
                    turn_a(x.before())
                up(x, e, 1)
                if x.after():
                    turn(x.after())
                if x.before():
                    down(x.before(), expert(x.before().t) if x.o == 3 else last_e[0])
                last_e[0] = e

            turn(Tile(0, 0))
            tiles(pe, tile)
            turn_a(FINAL)
            down(FINAL, last_e[0])

        @block.scalar
        def _(act):
            def copy(dst, src, sem):
                nc.scalar.activation(dst, src, ACT.Identity).then_inc(sem, 1)

            def rows(x):
                act.wait_ge(xg_turned, x.t + 1)
                copy(xgT[:, x.k, :, :].rearrange("p c t -> p (c t)"), x_bank, xgT_ready)

            def tile(x):
                act.wait_ge(z1_done, x.t + 1)
                if x.has(RING):
                    act.wait_ge(a_turned, x.t - RING + 1)
                nc.scalar.activation(ax[:, x.k, :], z1_bank[x.b], ACT.Tanh, scale=0.5).then_inc(tanh_done, 1)
                if x.before():
                    turned_a(x.before())
                if x.after():
                    rows(x.after())
                if x.before():
                    store(x.before())

            def turned_a(x):
                act.wait_ge(a_turned, x.t + 1)
                copy(axT[:, x.k, :, :].rearrange("p c t -> p (c t)"), a_bank[:, 0:IC * 128], aT_ready)

            def store(x):
                act.wait_ge(y_ready, x.t + 1)
                act.dma_start(slot_y[bass.ds(x.t * 128, 128), :], yx[:, x.k, :]).then_inc(y_out[x.k], 16)

            pad_rows(act, range(1, E_, 2))
            rows(Tile(0, 0))
            tiles(act, tile)
            turned_a(FINAL)
            store(FINAL)

        @block.vector
        def _(dve):
            v = nc.vector

            def stepper(sem):
                n = [0]

                def step(ins):
                    n[0] += 1
                    ins.then_inc(sem, 1)
                    dve.wait_ge(sem, n[0])
                return step, n

            step, n = stepper(placed)
            step(v.memset(zero[:, :], 0.0))
            dve.wait_ge(counted, 1)
            step(v.tensor_scalar(counti[:, :], bank[0][0:E_, 0:128], 127.0, None, ALU.add))
            step(v.tensor_scalar(counti[:, :], counti[:, :], 7, 7, ALU.arith_shift_right, ALU.logical_shift_left))
            step(v.tensor_copy(padded[:, :], counti[:, :]))
            dve.wait_ge(counted, 2)
            step(v.scalar_tensor_tensor(pad[:, :], C("iota", 1), float(REGION), bank[2][0:1, 0:E_], ALU.mult, ALU.add))
            assert n[0] == PADDED
            step(v.tensor_scalar(last1f[:, 0:1], bank[2][0:1, E_ - 1:E_], -1.0, 0.0, ALU.add, ALU.max))
            step(v.tensor_copy(last1[:, 0:1], last1f[:, 0:1]))
            step(v.tensor_scalar(last1[:, 1:2], last1[:, 0:1], 7, 7, ALU.arith_shift_right, ALU.logical_shift_left))
            step(v.tensor_copy(last1f[:, 1:2], last1[:, 1:2]))
            step(v.tensor_scalar(last1f[:, 0:1], last1f[:, 1:2], float((E_ - 1) * REGION), None, ALU.add))
            dve.wait_ge(offsets, 1)
            step(v.tensor_copy(off[:, :], bank[1][0:TT, 0:E_]))
            step(v.tensor_tensor(reach[:, :, :], C("starts", 1).unsqueeze(2).to_broadcast([1, TILES, E_]),
                                 off[0:1, :].unsqueeze(1).to_broadcast([1, TILES, E_]), ALU.is_ge))
            step(v.tensor_reduce(where[:, 0, :], reach[:, :, 1:E_], X, ALU.add))
            step(v.tensor_tensor(reach[:, :, :], reach[:, :, :], off[0:1, :].unsqueeze(1).to_broadcast([1, TILES, E_]), ALU.mult))
            step(v.tensor_reduce(where[:, 1, :], reach[:, :, :], X, ALU.max))
            step(v.tensor_tensor(where[:, 2, :], C("starts", 1), where[:, 1, :], ALU.subtract))
            step(v.scalar_tensor_tensor(where[:, 3, :], where[:, 0, :], float(REGION), where[:, 2, :], ALU.mult, ALU.add))
            step(v.tensor_scalar(tilei[:, 1, :], where[:, 3, :], last1f[:, 0:1], None, ALU.min))
            step(v.tensor_copy(tilei[:, 0, :], where[:, 0, :]))
            step(v.memset(ones3[:, :], 1.0))
            assert n[0] == PLACED

            step, n = stepper(split)
            dve.wait_ge(b_in, 16)
            for k in range(3):
                step(v.tensor_copy(parts[:, k, :], b32[:, :]))
                if k < 2:
                    step(v.tensor_tensor(b32[:, :], b32[:, :], parts[:, k, :], ALU.subtract))
            step(v.memset(axT[:, :, :, :], 0.0))
            step(v.memset(a_bank[:, :], 0.0))
            assert n[0] == SPLIT

            step, n = stepper(found)
            step(v.tensor_tensor(prod[:, :, :], oh[:, :, :, :].rearrange("p b g e -> p (b g) e"),
                                 off[:, :].unsqueeze(1).to_broadcast([TT, 2 * GT, E_]), ALU.mult))
            step(v.tensor_reduce(posf[:, 0, :], prod[:, :, :], X, ALU.add))
            step(v.tensor_tensor(posf[:, 1, :], posf[:, 0, :], rank[:, :, :].rearrange("p b g -> p (b g)"), ALU.add))
            step(v.tensor_copy(pos[:, :], posf[:, 1, :]))
            assert n[0] == FOUND

            def result(x):
                dve.wait_ge(y_done, x.t + 1)
                if x.has(RING):
                    dve.wait_ge(y_out[x.k], x.lap * 16)
                v.tensor_copy(yx[:, x.k, :], y_bank).then_inc(y_ready, 1)

            def tile(x):
                dve.wait_ge(tanh_done, x.t + 1)
                v.scalar_tensor_tensor(ax[:, x.k, :], ax[:, x.k, :], 1.0, z1_bank[x.b], ALU.add, ALU.mult).then_inc(silu_done, 1)
                dve.wait_ge(silu_done, x.t + 1)
                dve.wait_ge(z3_done, x.t + 1)
                v.scalar_tensor_tensor(ax[:, x.k, :], ax[:, x.k, :], 0.5, z3_bank[x.b], ALU.mult, ALU.mult).then_inc(a_ready, 1)
                if x.before():
                    result(x.before())

            tiles(dve, tile)
            result(FINAL)
            dve.wait_ge(h_in, 16)
            for g in range(GT):
                if g % 2 == 0:
                    dve.wait_ge(gathered[g // 2], 16 * 4)
                for e in range(2):
                    if e:
                        dve.wait_ge(added, 2 * g + 1)
                    v.scalar_tensor_tensor(h[:, g, :], back[:, e * GT + g, :], gate[:, e, g:g + 1], h[:, g, :],
                                           ALU.mult, ALU.add).then_inc(added, 1)


def kernel(**inputs):
    import concourse.bacc as bacc
    from concourse.bass_utils import run_bass_kernel_spmd

    a = {k: np.asarray(v) for k, v in inputs.items()}

    def rows(w):
        return w.reshape(-1, 128, w.shape[1]).transpose(1, 0, 2)

    def column(b, chunks):
        out = np.zeros(chunks * 128, b.dtype)
        out[:b.size] = b
        return out.reshape(chunks, 128).T

    const, toward = constants()
    f = np.float32
    tree = np.zeros((TREES, NODES, D), f)
    tree[:, :NODES - 1] = a["L0_ffn_W_in"].reshape(TREES, NODES - 1, D)
    tree_b = np.zeros((TREES, NODES), f)
    tree_b[:, :NODES - 1] = a["L0_ffn_b_in"].reshape(TREES, NODES - 1)
    leaf = np.zeros((D, TREES, NODES), f)
    leaf[:, :, :NODES - 1] = a["L0_ffn_W_out"].reshape(D, TREES, NODES - 1)
    in1 = a["L1_attn_w_in"].reshape(H, 3, 16, D).transpose(1, 0, 2, 3).reshape(3 * D, D)
    in1_b = a["L1_attn_b_in"].reshape(H, 3, 16).transpose(1, 0, 2).reshape(3 * D)
    sh2 = np.zeros((SC * 128, D), f)
    sh2[:SH] = a["L1_ffn_sw2"]
    we = np.zeros((E_, 128, WE), f)
    for e in range(E_):
        we[e, :, 0:2 * INTER] = rows(a["L1_ffn_w1"][e]).reshape(128, -1)
        we[e, :, 2 * INTER:4 * INTER] = rows(a["L1_ffn_w3"][e]).reshape(128, -1)
        we[e, :, 4 * INTER:4 * INTER + 2 * D] = rows(a["L1_ffn_w2"][e, :256]).reshape(128, -1)
        we[e, :INTER - 256, 4 * INTER + 2 * D:] = a["L1_ffn_w2"][e, 256:]
    arrays = {
        "const": const, "toward": toward,
        "patches": a["x"].reshape(B, 3, 6, 16, 6, 16).transpose(0, 2, 4, 1, 3, 5).reshape(NB, NT, TT, PD).transpose(0, 2, 1, 3).reshape(NB * TT, NT, PD),
        "w_tok": rows(a["L0_tok_W"].T), "g_ln1": column(a["L0_tok_ln1_w"], KP), "g_ln2": a["L0_tok_ln2_w"],
        "w_qkv": rows(a["L0_attn_w_qkv"]), "w_out0": rows(a["L0_attn_w_out"]), "b_out0": column(a["L0_attn_b_out"], DC),
        "g_head": a["L0_attn_ln_gamma"], "b_head": column(np.repeat(a["L0_attn_ln_beta"], DH), QC),
        "wx": np.tile(a["L0_attn_reattn_w"], (IG, 1)),
        "w_tree": rows(tree.reshape(-1, D).T), "b_tree": column(tree_b.reshape(-1), FC),
        "w_leaf": rows(leaf.reshape(D, -1).T),
        "w_in1": rows(in1.T), "b_in1": column(in1_b, 6), "w_out1": rows(a["L1_attn_w_out"].T), "b_out1": column(a["L1_attn_b_out"], DC),
        "w_sh1": rows(a["L1_ffn_sw1"]), "w_sh3": rows(a["L1_ffn_sw3"]), "w_sh2": rows(sh2),
        "b_sh1": column(a["L1_ffn_sb1"], SC), "b_sh3": column(a["L1_ffn_sb3"], SC), "b_sh2": column(a["L1_ffn_sb2"], DC),
        "w_gate": rows(a["L1_ffn_gate_w"]), "b_gate": a["L1_ffn_gate_b"],
        "we": we, "b_e": np.concatenate([a["L1_ffn_b1"], a["L1_ffn_b3"], a["L1_ffn_b2"]], 1),
    }
    nc = bacc.Bacc("TRN2", target_bir_lowering=False, num_devices=1)
    feed, dram = {}, {}
    for name, x in arrays.items():
        x = np.ascontiguousarray(x)
        feed[f"in_{name}"] = x
        dram[name] = nc.dram_tensor(f"in_{name}", x.shape, mybir.dt.from_np(x.dtype), kind="ExternalInput").ap()
    out = nc.dram_tensor("out", (T, D), F32, kind="ExternalOutput").ap()
    program(nc, dram, out)
    r = run_bass_kernel_spmd(nc, [feed], core_ids=[0])
    return r.results[0]["out"].reshape(B, L, D)
```
